# Optimizing a Trainium2 kernel written in Bass

```python
import numpy as np
import jax
import jax.numpy as jnp

def _softmax(x, axis=-1):
    return jax.nn.softmax(x, axis=axis)

def _gelu(x):
    return jax.nn.gelu(x, approximate=True)

def _silu(x):
    return jax.nn.silu(x)

def _sigmoid(x):
    return jax.nn.sigmoid(x)

def _layernorm(x, axis=-1, eps=1e-05):
    m = jnp.mean(x, axis=axis, keepdims=True)
    v = jnp.var(x, axis=axis, keepdims=True)
    return (x - m) / jnp.sqrt(v + eps)

def _scatter_add(tgt, idx, src, axis=0):
    return tgt.at[idx].add(src)

def _segment_sum(src, seg, n):
    return jax.ops.segment_sum(src, seg, n)
kernel_name = 'mk_gps_d1_gnn_r32_ade884'

def setup_inputs(seed: int=0):
    np.random.seed(seed)
    _w = jnp.asarray

    def _rec_inputs():
        import jax
        import jax.numpy as jnp
        _gk = jax.random.key(seed)
        x = -2.117e-06 + 0.01 * jax.random.normal(jax.random.fold_in(_gk, 1), (3125, 256), jnp.float32)
        src = jax.random.randint(jax.random.fold_in(_gk, 2), (50000,), 0, 3125, jnp.int32)
        dst = jax.random.randint(jax.random.fold_in(_gk, 3), (50000,), 0, 3125, jnp.int32)
        _o = jnp.argsort(dst, stable=True)
        src = src[_o]
        dst = dst[_o]
        edge_weight = jax.random.uniform(jax.random.fold_in(_gk, 12), (50000,), jnp.float32, 0.0, 0.03125)
        return (x, src, dst, edge_weight)
    x, src, dst, edge_weight = _rec_inputs()

    def _L0_gnn_setup():
        import jax, jax.numpy as jnp
        import numpy as np
        EPS = 1e-15
        PROJ_EPS = 1e-05
        MAX_TANH = 15.0
        N_NODES = 3125
        N_EDGES = 100000
        D_IN = 256
        D_OUT = 256

        def _norm(x):
            return jnp.sqrt(jnp.sum(x * x, axis=-1, keepdims=True))

        def hyperbolic_projection(x):
            n = jnp.maximum(_norm(x), EPS)
            maxnorm = 1.0 - PROJ_EPS
            return x * jnp.minimum(1.0, maxnorm / n)

        def log_map_zero(x):
            n = jnp.clip(_norm(x), EPS, 1.0 - PROJ_EPS)
            return jnp.arctanh(n) / n * x

        def exp_map_zero(v):
            n = jnp.maximum(_norm(v), EPS)
            return jnp.tanh(jnp.minimum(n, MAX_TANH)) / n * v

        def mobius_addition(u, v):
            dot = jnp.sum(u * v, axis=-1, keepdims=True)
            nu2 = jnp.sum(u * u, axis=-1, keepdims=True)
            nv2 = jnp.sum(v * v, axis=-1, keepdims=True)
            num = (1.0 + 2.0 * dot + nv2) * u + (1.0 - nu2) * v
            den = 1.0 + 2.0 * dot + nu2 * nv2
            return num / (den + EPS)
        key = jax.random.key(seed)
        k1, k2, k3, k4, k5, k6 = jax.random.split(key, 6)
        inputs = 0.01 * jax.random.normal(k1, (N_NODES, D_IN), dtype=jnp.float32)
        weight_mat = 0.05 * jax.random.normal(k2, (D_IN, D_OUT), dtype=jnp.float32)
        bias_vec = 0.01 * jax.random.normal(k3, (D_OUT,), dtype=jnp.float32)
        edge_row = jax.random.randint(k4, (N_EDGES,), 0, N_NODES)
        edge_col = jax.random.randint(k5, (N_EDGES,), 0, N_NODES)
        edge_val = jax.random.uniform(k6, (N_EDGES,), dtype=jnp.float32) / 32.0
        return {'inputs': inputs, 'weight_mat': weight_mat, 'bias_vec': bias_vec, 'edge_row': edge_row, 'edge_col': edge_col, 'edge_val': edge_val}
    _L0_gnn_all = _L0_gnn_setup()
    _L0_gnn_in = {k: v for k, v in _L0_gnn_all.items() if k in ('weight_mat', 'bias_vec')}
    del _L0_gnn_all

    def _L0_mix_setup():
        import jax, jax.numpy as jnp
        import numpy as np
        MIDC = 256
        HEADS = 8
        HEADC = MIDC // HEADS
        EPS = 1e-05

        def _ln(x, gamma, beta):
            mu = jnp.mean(x, axis=-1, keepdims=True)
            var = jnp.var(x, axis=-1, keepdims=True)
            return (x - mu) * jax.lax.rsqrt(var + EPS) * gamma + beta
        key = jax.random.key(seed)
        ks = jax.random.split(key, 8)
        B, HW, C = (8, 128, MIDC)
        s = 1.0 / np.sqrt(C)
        return {'x': jax.random.normal(ks[0], (B, HW, C), jnp.float32), 'w_qkv': jax.random.normal(ks[1], (C, 3 * C), jnp.float32) * s, 'b_qkv': jnp.zeros((3 * C,), jnp.float32), 'kln_g': jnp.ones((HEADC,), jnp.float32), 'kln_b': jnp.zeros((HEADC,), jnp.float32), 'vln_g': jnp.ones((HEADC,), jnp.float32), 'vln_b': jnp.zeros((HEADC,), jnp.float32), 'w1': jax.random.normal(ks[2], (C, C), jnp.float32) * s, 'b1': jnp.zeros((C,), jnp.float32), 'w2': jax.random.normal(ks[3], (C, C), jnp.float32) * s, 'b2': jnp.zeros((C,), jnp.float32)}
    _L0_mix_all = _L0_mix_setup()
    _L0_mix_in = {k: v for k, v in _L0_mix_all.items() if k in ('w_qkv', 'b_qkv', 'kln_g', 'kln_b', 'vln_g', 'vln_b', 'w1', 'b1', 'w2', 'b2')}
    del _L0_mix_all

    def _L0_ffn_setup():
        import jax, jax.numpy as jnp
        import numpy as np
        B, S, H, F, E, K = (8, 128, 256, 512, 16, 2)
        EPS = 1e-05
        key = jax.random.key(seed)
        ks = jax.random.split(key, 9)
        sc = 0.02
        return {'x': jax.random.normal(ks[0], (B, S, H), dtype=jnp.float32), 'gate_w': jax.random.normal(ks[1], (H, E), dtype=jnp.float32) * sc, 'gate_b': jnp.zeros((E,), dtype=jnp.float32), 'w1': jax.random.normal(ks[2], (E, H, F), dtype=jnp.float32) * sc, 'b1': jnp.zeros((E, F), dtype=jnp.float32), 'w2': jax.random.normal(ks[3], (E, F, H), dtype=jnp.float32) * sc, 'b2': jnp.zeros((E, H), dtype=jnp.float32), 'gamma': jnp.ones((H,), dtype=jnp.float32), 'beta': jnp.zeros((H,), dtype=jnp.float32)}
    _L0_ffn_all = _L0_ffn_setup()
    _L0_ffn_in = {k: v for k, v in _L0_ffn_all.items() if k in ('gate_w', 'gate_b', 'w1', 'b1', 'w2', 'b2', 'gamma', 'beta')}
    del _L0_ffn_all
    return {'x': x, 'src': src, 'dst': dst, 'edge_weight': edge_weight, 'L0_gnn_weight_mat': _L0_gnn_in['weight_mat'], 'L0_gnn_bias_vec': _L0_gnn_in['bias_vec'], 'L0_mix_w_qkv': _L0_mix_in['w_qkv'], 'L0_mix_b_qkv': _L0_mix_in['b_qkv'], 'L0_mix_kln_g': _L0_mix_in['kln_g'], 'L0_mix_kln_b': _L0_mix_in['kln_b'], 'L0_mix_vln_g': _L0_mix_in['vln_g'], 'L0_mix_vln_b': _L0_mix_in['vln_b'], 'L0_mix_w1': _L0_mix_in['w1'], 'L0_mix_b1': _L0_mix_in['b1'], 'L0_mix_w2': _L0_mix_in['w2'], 'L0_mix_b2': _L0_mix_in['b2'], 'L0_ffn_gate_w': _L0_ffn_in['gate_w'], 'L0_ffn_gate_b': _L0_ffn_in['gate_b'], 'L0_ffn_w1': _L0_ffn_in['w1'], 'L0_ffn_b1': _L0_ffn_in['b1'], 'L0_ffn_w2': _L0_ffn_in['w2'], 'L0_ffn_b2': _L0_ffn_in['b2'], 'L0_ffn_gamma': _L0_ffn_in['gamma'], 'L0_ffn_beta': _L0_ffn_in['beta']}

def reference(x, src, dst, edge_weight, L0_gnn_weight_mat, L0_gnn_bias_vec, L0_mix_w_qkv, L0_mix_b_qkv, L0_mix_kln_g, L0_mix_kln_b, L0_mix_vln_g, L0_mix_vln_b, L0_mix_w1, L0_mix_b1, L0_mix_w2, L0_mix_b2, L0_ffn_gate_w, L0_ffn_gate_b, L0_ffn_w1, L0_ffn_b1, L0_ffn_w2, L0_ffn_b2, L0_ffn_gamma, L0_ffn_beta):
    import jax
    import jax.numpy as jnp

    def _L0_gnn_ref(inputs, weight_mat, bias_vec, edge_row, edge_col, edge_val):
        import jax, jax.numpy as jnp
        import numpy as np
        EPS = 1e-15
        PROJ_EPS = 1e-05
        MAX_TANH = 15.0
        N_NODES = 3125
        N_EDGES = 100000
        D_IN = 256
        D_OUT = 256

        def _norm(x):
            return jnp.sqrt(jnp.sum(x * x, axis=-1, keepdims=True))

        def hyperbolic_projection(x):
            n = jnp.maximum(_norm(x), EPS)
            maxnorm = 1.0 - PROJ_EPS
            return x * jnp.minimum(1.0, maxnorm / n)

        def log_map_zero(x):
            n = jnp.clip(_norm(x), EPS, 1.0 - PROJ_EPS)
            return jnp.arctanh(n) / n * x

        def exp_map_zero(v):
            n = jnp.maximum(_norm(v), EPS)
            return jnp.tanh(jnp.minimum(n, MAX_TANH)) / n * v

        def mobius_addition(u, v):
            dot = jnp.sum(u * v, axis=-1, keepdims=True)
            nu2 = jnp.sum(u * u, axis=-1, keepdims=True)
            nv2 = jnp.sum(v * v, axis=-1, keepdims=True)
            num = (1.0 + 2.0 * dot + nv2) * u + (1.0 - nu2) * v
            den = 1.0 + 2.0 * dot + nu2 * nv2
            return num / (den + EPS)
        pre_sup = log_map_zero(inputs)
        out = pre_sup @ weight_mat
        gathered = out[edge_col] * edge_val[:, None]
        out = jax.ops.segment_sum(gathered, edge_row, num_segments=N_NODES)
        out = hyperbolic_projection(exp_map_zero(out))
        b = hyperbolic_projection(exp_map_zero(bias_vec))
        out = mobius_addition(out, b[None, :])
        out = hyperbolic_projection(out)
        return out

    def _L0_mix_ref(x, w_qkv, b_qkv, kln_g, kln_b, vln_g, vln_b, w1, b1, w2, b2):
        import jax, jax.numpy as jnp
        import numpy as np
        MIDC = 256
        HEADS = 8
        HEADC = MIDC // HEADS
        EPS = 1e-05

        def _ln(x, gamma, beta):
            mu = jnp.mean(x, axis=-1, keepdims=True)
            var = jnp.var(x, axis=-1, keepdims=True)
            return (x - mu) * jax.lax.rsqrt(var + EPS) * gamma + beta
        B, HW, C = x.shape
        bias = x
        qkv = (x @ w_qkv + b_qkv).reshape(B, HW, HEADS, 3 * HEADC)
        qkv = qkv.transpose(0, 2, 1, 3)
        q, k, v = jnp.split(qkv, 3, axis=-1)
        k = _ln(k, kln_g, kln_b)
        v = _ln(v, vln_g, vln_b)
        kv = jnp.einsum('bhnd,bhne->bhde', k, v) / HW
        out = jnp.einsum('bhnd,bhde->bhne', q, kv)
        out = out.transpose(0, 2, 1, 3).reshape(B, HW, C)
        ret = out + bias
        h = jax.nn.gelu(ret @ w1 + b1, approximate=False)
        return h @ w2 + b2 + bias

    def _L0_ffn_ref(x, gate_w, gate_b, w1, b1, w2, b2, gamma, beta):
        import jax, jax.numpy as jnp
        import numpy as np
        B, S, H, F, E, K = (8, 128, 256, 512, 16, 2)
        EPS = 1e-05
        gate_logits = x @ gate_w + gate_b
        topk_vals, topk_idx = jax.lax.top_k(gate_logits, K)
        topk_w = jax.nn.softmax(topk_vals, axis=-1)
        h = jax.nn.relu(jnp.einsum('bsh,ehf->bsef', x, w1) + b1)
        expert_out = jnp.einsum('bsef,efh->bseh', h, w2) + b2
        sel = jnp.take_along_axis(expert_out, topk_idx[:, :, :, None], axis=2)
        moe = jnp.sum(topk_w[..., None] * sel, axis=2)
        y = x + moe
        mu = jnp.mean(y, axis=-1, keepdims=True)
        var = jnp.var(y, axis=-1, keepdims=True)
        return (y - mu) / jnp.sqrt(var + EPS) * gamma + beta
    xn = _layernorm(x, axis=-1)
    x = x + _L0_gnn_ref(xn, L0_gnn_weight_mat, L0_gnn_bias_vec, src, dst, edge_weight) + _L0_mix_ref(xn[None], L0_mix_w_qkv, L0_mix_b_qkv, L0_mix_kln_g, L0_mix_kln_b, L0_mix_vln_g, L0_mix_vln_b, L0_mix_w1, L0_mix_b1, L0_mix_w2, L0_mix_b2)[0]
    x = x + _L0_ffn_ref(_layernorm(x, axis=-1)[None], L0_ffn_gate_w, L0_ffn_gate_b, L0_ffn_w1, L0_ffn_b1, L0_ffn_w2, L0_ffn_b2, L0_ffn_gamma, L0_ffn_beta)[0]
    return x

_drawn_inputs = setup_inputs


def setup_inputs(seed=0):
    import zlib

    import numpy as np

    out = dict(_drawn_inputs(seed))
    spreads = {'L0_mix_b_qkv': (0.0, 0.1),
     'L0_mix_kln_g': (1.0, 0.2),
     'L0_mix_kln_b': (0.0, 0.1),
     'L0_mix_vln_g': (1.0, 0.2),
     'L0_mix_vln_b': (0.0, 0.1),
     'L0_mix_b1': (0.0, 0.1),
     'L0_mix_b2': (0.0, 0.1),
     'L0_ffn_gate_b': (0.0, 0.1),
     'L0_ffn_b1': (0.0, 0.76),
     'L0_ffn_b2': (0.0, 0.1),
     'L0_ffn_gamma': (1.0, 0.2),
     'L0_ffn_beta': (0.0, 0.1)}
    factors = {'L0_gnn_bias_vec': 8.0}
    for name, (base, spread) in spreads.items():
        noise = np.random.default_rng([zlib.crc32(name.encode()), seed]).standard_normal(out[name].shape)
        drawn = base * np.exp(spread * noise) if base else spread * noise
        out[name] = jnp.asarray(drawn.astype(out[name].dtype))
    for name, factor in factors.items():
        out[name] = (out[name] * factor).astype(out[name].dtype)
    return out
```

```python
from contextlib import ExitStack, contextmanager


class Steps:

    def __init__(self, engine, semaphore):
        self.engine, self.semaphore, self.done, self.turn = engine, semaphore, 0, None

    def mark(self, instruction):
        instruction.then_inc(self.semaphore, 1)
        self.done += 1

    def wait(self):
        self.engine.wait_ge(self.semaphore, self.done if self.turn is None else self.turn + self.done)

    def __call__(self, instruction):
        self.mark(instruction)
        self.wait()

    @contextmanager
    def loop(self, turns, marks):
        start = self.done
        with self.engine.Fori(0, turns) as i:
            self.turn = i * marks
            yield i
            assert self.done - start == marks, self.done - start
        self.turn, self.done = None, start + turns * marks


def await_ge(engine, semaphore, value):
    if not isinstance(value, int) or value > 0:
        engine.wait_ge(semaphore, value)


def turns_of(engine, first, count, body, last=None):
    if first == 0:
        body(0)
        first = 1
    end = count - (last is not None)
    if end > first:
        with engine.Fori(first, end) as i:
            body(i)
    if last is not None:
        last(count - 1)


def shares(n, parts):
    return [(n * (k + 1)) // parts - (n * k) // parts for k in range(parts)]


def graph_transformer_layer(nc, x, src, dst, edge_weight, gnn_w, gnn_b, w_qkv, b_qkv, kln_g, kln_b, vln_g, vln_b,
                            mix_w1, mix_b1, mix_w2, mix_b2, gate_w, gate_b, w1, b1, w2, b2, gamma, beta, out):
    import concourse.bass as bass
    from concourse import mybir

    F32, I32, U32 = mybir.dt.float32, mybir.dt.int32, mybir.dt.uint32
    ALU, ACT, AX = mybir.AluOpType, mybir.ActivationFunctionType, mybir.AxisListType
    PE_, DVE_, ACT_ = mybir.EngineType.PE, mybir.EngineType.DVE, mybir.EngineType.Activation
    ds = bass.ds

    N, C = x.shape
    E = src.shape[0]
    NE, _, F = w1.shape
    B, NT = 125, N // 125
    KC, KF = C // 128, F // 128
    HEADS, HD = 8, 32
    assert N == B * NT and NT * 4195 < 2 ** 24
    COLS = -(-E // 128)
    FULL = E // 128
    EPS, LN_EPS, MAXNORM = 1e-15, 1e-5, 1.0 - 1e-5

    RING = 8
    T_OF = [59, 143, 189]
    assert sum(T_OF) == COLS
    AT = [0, 59, 202]
    H_OF = [-(-(t + NT - 1) // RING) * RING for t in T_OF]
    TURNS = [h // RING for h in H_OF]
    HMAX = max(H_OF)
    SORT = [T_OF[1] // TURNS[0], T_OF[2] // TURNS[1], 0]
    assert SORT[0] * TURNS[0] == T_OF[1] and SORT[1] * TURNS[1] == T_OF[2]
    SEGS = [(0, 1, 0, SORT[0], 1, 0),
            (0, NT - TURNS[1] - 1, 1, SORT[0], 1, 1),
            (0, TURNS[0] - (NT - TURNS[1]), NT - TURNS[1], SORT[0], 0, 0),
            (1, TURNS[1], 0, SORT[1], 1, NT - TURNS[1]),
            (2, 1, 0, 0, 2, 0),
            (2, NT - 1, 1, 0, 2, 1),
            (2, TURNS[2] - NT, NT, 0, 0, 0)]
    CHUNK0 = [0, H_OF[0], H_OF[0] + H_OF[1]]
    CHUNKS = sum(H_OF)
    GT = 5
    assert NT % GT == 0
    HALVES = 4
    SR = 4

    PAIRS = 2 * NT
    SLOTS = (2 * N + NE * 127) // 128
    assert SLOTS % RING == 0 and SLOTS == 64
    YROWS = 2 * N + 128 * SLOTS

    table = nc.dram_tensor("table", (N, C), F32).ap()
    tokens = nc.dram_tensor("tokens", (N, C), F32).ap()
    pair_out = nc.dram_tensor("pair_out", (YROWS, C), F32).ap()

    ctx = ExitStack()
    with ctx:
        def sb(name, shape, dt=F32):
            return ctx.enter_context(nc.sbuf_tensor(name, shape, dt))

        def sem(name):
            return ctx.enter_context(nc.semaphore(name))

        slab = sb("slab", [128, NE * 2048])
        used = [0]

        def part(of, shape, count=used, base=slab):
            n = 1
            for d in shape:
                n *= d
            a = base[:, count[0]:count[0] + n]
            count[0] += n
            assert count[0] <= base.shape[1]
            names = "abc"[:len(shape)]
            return a if len(shape) == 1 else a.rearrange(
                f"p ({' '.join(names)}) -> p {' '.join(names)}", **dict(zip(names[:-1], shape)))

        xnT = part("xnT", [KC, N])
        work = part("work", [2 * HMAX * NT])
        rt_one, rt_sum = work[:, 0:HMAX * NT], work[:, HMAX * NT:2 * HMAX * NT]
        xn = work[:, 0:NT * C].rearrange("p (t c) -> p t c", t=NT)
        wqkv = part("wqkv", [KC, 3 * C])
        wcen = part("wcen", [KC, 3 * C])
        wgnn = part("wgnn", [KC, C])
        mw1 = part("mw1", [KC, C])
        mw2 = part("mw2", [KC, C])
        weff = part("weff", [KC, C])
        kvw1 = part("kvw1", [KC, C])
        wqT = part("wqT", [KC, C])
        kvT = part("kvT", [KC, 128])
        kvc = part("kvc", [HEADS, 2, HD])
        kvs = part("kvs", [HEADS, 2, HD])
        xst = part("xst", [KC, B])
        kvn = part("kvn", [2, HEADS, HD])
        hot = part("hot", [RING, 128])
        s_lo = part("s_lo", [SR, 2, 128])
        s_hi = part("s_hi", [SR, HMAX])
        mhT = part("mhT", [KC, B])
        tout = part("tout", [2, C])
        bias_kv = part("bias_kv", [HEADS, 3 * HD])
        ln_g = part("ln_g", [2, HD])
        ln_b = part("ln_b", [2, HD])
        mb2 = part("mb2", [C])
        ew, pack, lo = part("ew", [COLS]), part("pack", [COLS]), part("lo", [COLS])
        key = hi = part("hi", [COLS])
        zeros = part("zeros", [256])
        brow = part("brow", [128])
        g_row = part("g_row", [HMAX]).bitcast(I32)
        g_lo, g_w = part("g_lo", [HMAX]), part("g_w", [HMAX])

        X = sb("X", [128, NT, C])
        acc = sb("acc", [128, NT, C])
        accf = acc[:, :, :].rearrange("p t c -> p (t c)")
        later = [0]
        b2b = part("b2b", [NE, C], later, accf)
        w1c = part("w1c", [KC, F], later, accf)
        hT = part("hT", [2, KF, 128], later, accf)
        p_lo = hT[:, :, :, :].rearrange("p a k n -> p (a k n)").rearrange("p (r a n) -> p r a n", r=SR, a=2)
        final = [0]
        yb = part("yb", [2, GT, C], final)
        zb = part("zb", [GT, C], final)
        ub = part("ub", [GT, C], final)
        ob = part("ob", [GT, C], final)
        gam, bet = part("gam", [C], final), part("bet", [C], final)

        rows = sb("rows", [128, RING, C])
        early = rows[:, :, :].rearrange("p k c -> p (k c)").bitcast(I32)
        esrc, edst, eq = (early[:, j * COLS:(j + 1) * COLS] for j in range(3))
        slot = sb("slot", [128, 192])
        slot_i = sb("slot_i", [128, HMAX], I32)
        slot_j = sb("slot_j", [128, HMAX], I32)
        small = sb("small", [128, 6, 32])
        cnt_i = sb("cnt_i", [128, 32], I32)
        bk_f = sb("bk_f", [1, HMAX])
        bk = [sb(f"bk{g}", [1, H_OF[g]], I32) for g in range(3)]
        idx = sb("idx", [128, RING], I32)
        iota = sb("iota", [128, HMAX])
        slot_id = sb("slot_id", [128, SLOTS])
        tT = sb("tT", [128, 2, KC, 128])
        yv = sb("yv", [128, 2, C])
        p_hi = yv[:, :, :].rearrange("p a c -> p (a c)")[:, 0:SR * SLOTS].rearrange("p (r n) -> p r n", r=SR)
        odx = sb("odx", [128, RING], I32)
        pair_key = sb("pair_key", [128, 2, NT])
        pair_lo = sb("pair_lo", [128, PAIRS])
        pair_hi = sb("pair_hi", [128, PAIRS])
        pair_row = sb("pair_row", [128, 2, NT])
        s_tok = sb("s_tok", [128, SLOTS], I32)
        s_row = sb("s_row", [128, SLOTS], I32)
        s_tmp = sb("s_tmp", [128, 2, SLOTS])
        ex_w = sb("ex_w", [1, SLOTS], I32)
        ex_b1 = sb("ex_b1", [1, SLOTS], I32)
        ex_b2 = sb("ex_b2", [1, SLOTS], I32)
        lg = sb("lg", [128, 2, NE])
        mx5 = sb("mx5", [128, GT, 8])
        ix5 = sb("ix5", [128, GT, 8], U32)
        topv = sb("topv", [128, 2, NT])
        pair_w = sb("pair_w", [128, 2, NT])
        mv5 = sb("mv5", [128, GT, 2])
        st5 = sb("st5", [128, 6, GT])
        mid_rs = sb("mid_rs", [128, NT])
        mid_nb = sb("mid_nb", [128, NT])
        tri = sb("tri", [128, 128])
        ident = sb("ident", [128, 128])
        ones = sb("ones", [128, 128])
        node = sb("node", [128, NT])
        gb = sb("gb", [128, C])
        gate = sb("gate", [128, KC, NE])
        gateb = sb("gateb", [128, NE])
        bcol = sb("bcol", [128, 68])
        beff = sb("beff", [128, KC])
        kvst = sb("kvst", [128, 4, 16])
        bn6 = sb("bn6", [128, 6])
        mv = sb("mv", [128, NT, 2])
        st = sb("st", [128, 16, NT + 1])
        wmean = sb("wmean", [128, KC, 3 * HEADS])

        bank = [ctx.enter_context(nc.psum_tensor(f"bank{i}", [128, 512], F32)) for i in range(8)]

        pads, ld_edge, ld_x, ld_w, ld_b = sem("pads"), sem("ld_edge"), sem("ld_x"), sem("ld_w"), sem("ld_b")
        consts = sem("consts")
        dve_step, act_step, pool_step = sem("dve_step"), sem("act_step"), sem("pool_step")
        rank_rows, rank_sums = sem("rank_rows"), sem("rank_sums")
        hots_made, hots_used, sorted_ = sem("hots_made"), sem("hots_used"), sem("sorted_")
        psum_zeroed = sem("psum_zeroed")
        var_ready, sqrt_done, squares = sem("var_ready"), sem("sqrt_done"), sem("squares")
        xn_ready, ln_arg, ln_done, row_scale = sem("xn_ready"), sem("ln_arg"), sem("ln_done"), sem("row_scale")
        xn_t, xn_t_out, tab_mm, tab_out, tab_stored = (sem("xn_t"), sem("xn_t_out"), sem("tab_mm"), sem("tab_out"),
                                                       [sem("tab_stored0"), sem("tab_stored1")])
        wcen_ready, setup_t, setup_t_out = sem("wcen_ready"), sem("setup_t"), sem("setup_t_out")
        x_plus = sem("x_plus")
        group_ready = sem("group_ready")
        may_go = sem("may_go")
        idx_ready = sem("idx_ready")
        gathered = [sem(f"gathered{k}") for k in range(RING)]
        hot_ready, chunk_done, chunk_added = sem("hot_ready"), sem("chunk_done"), sem("chunk_added")
        kv_mm, kv_sb, kv_sq, kv_norm, kv_used = sem("kv_mm"), sem("kv_sb"), sem("kv_sq"), sem("kv_norm"), sem("kv_used")
        xst_ready = sem("xst_ready")
        kv_var, kv_std = sem("kv_var"), sem("kv_std")
        kvT_ready, kvw1_mm, kvw1_out, weff_mm, weff_out = (sem("kvT_ready"), sem("kvw1_mm"), sem("kvw1_out"),
                                                           sem("weff_mm"), sem("weff_out"))
        mh_mm, mh_out, my_mm, my_out = sem("mh_mm"), sem("mh_out"), sem("my_mm"), sem("my_out")

        tail_ss, tail_sq, tail_tanh, tail_v = sem("tail_ss"), sem("tail_sq"), sem("tail_tanh"), sem("tail_v")
        mid_var, mid_root, mid_scale, mid_norm = sem("mid_var"), sem("mid_root"), sem("mid_scale"), sem("mid_norm")
        tok_stored, mt_mm, mt_out, mg_mm, mg_out = sem("tok_stored"), sem("mt_mm"), sem("mt_out"), sem("mg_mm"), sem("mg_out")
        acc_free, ld_gb, ld_moe, ld_b2 = sem("acc_free"), sem("ld_gb"), sem("ld_moe"), sem("ld_b2")
        exp_arg, exp_done = sem("exp_arg"), sem("exp_done")
        pairs_made, pairs_used, slots_ready = sem("pairs_made"), sem("pairs_used"), sem("slots_ready")
        tok_idx, out_idx = sem("tok_idx"), sem("out_idx")
        tok_got = [sem(f"tok_got{k}") for k in range(RING)]
        y_put = [sem(f"y_put{k}") for k in range(RING)]
        x_mm, x_out, w_copied, h_mm, h_out, y_mm, y_out = (sem("x_mm"), sem("x_out"), sem("w_copied"), sem("h_mm"),
                                                           sem("h_out"), sem("y_mm"), sem("y_out"))
        y_ld = [sem(f"y_ld{j}") for j in range(GT)]
        y_used, fz, fz_sum, fin_var, fin_root, fin_scale, fin_norm, fin_aff, fin_out = (
            sem("y_used"), sem("fz"), sem("fz_sum"), sem("fin_var"), sem("fin_root"), sem("fin_scale"), sem("fin_norm"),
            sem("fin_aff"), sem("fin_out"))
        out_put = [sem(f"out_put{j}") for j in range(GT)]

        block = ctx.enter_context(nc.Block())

        x_t = x.rearrange("(t p) c -> p t c", p=B)
        out_t = out.rearrange("(t p) c -> p t c", p=B)
        table_t = table.rearrange("(t p) c -> p t c", p=B)

        def edge_whole(a):
            return a[0:128 * FULL].rearrange("(p j) -> p j", j=FULL)

        def edge_rest(a):
            return a[128 * FULL:E].rearrange("(p j) -> p j", j=1)

        def row(v):
            return v.rearrange("(a n) -> a n", a=1)

        W_LOADS, B_LOADS = 5, 12
        @block.sync
        def _(sp):
            sp.wait_ge(pads, 3)
            for a, t in ((src, esrc), (dst, edst), (edge_weight, ew)):
                sp.dma_start(t[:, 0:FULL], edge_whole(a)).then_inc(ld_edge, 16)
                with nc.allow_non_contiguous_dma(reason="the last few edges, one a partition"):
                    sp.dma_start(t[0:E - 128 * FULL, FULL:FULL + 1], edge_rest(a)).then_inc(ld_edge, 16)
            sp.dma_start(X[0:112, :, :], x_t[0:112]).then_inc(ld_x, 16)
            sp.dma_start(X[112:B, :, :], x_t[112:B]).then_inc(ld_x, 16)
            for t, a in ((wgnn, gnn_w), (wqkv, w_qkv), (mw1, mix_w1), (mw2, mix_w2), (gate, gate_w)):
                sp.dma_start(t[:, :, :], a.rearrange("(k p) n -> p k n", p=128)).then_inc(ld_w, 16)
            for q in range(NT):
                sp.wait_ge(tab_out, q + 1)
                sp.dma_start(table_t[:, q, :], tout[0:B, q % 2, :]).then_inc(tab_stored[q % 2], 16)

            sp.wait_ge(chunk_done, RING + CHUNKS)
            sp.wait_ge(my_out, NT)
            for e in range(NE):
                half = slab[:, e * 2048:(e + 1) * 2048]
                sp.dma_start(half[:, 0:1024].rearrange("p (k n) -> p k n", k=KC),
                             w1[e].rearrange("(k p) n -> p k n", p=128)).then_inc(ld_moe, 16)
                sp.dma_start(half[:, 1024:2048].rearrange("p (k n) -> p k n", k=KF),
                             w2[e].rearrange("(k p) n -> p k n", p=128)).then_inc(ld_moe, 16)
            with sp.Fori(0, NT // GT) as i:
                sp.wait_ge(mid_norm, i * GT + GT)
                sp.dma_start(tokens.rearrange("(t p) c -> p t c", p=B)[:, ds(i * GT, GT), :], rows[0:B, 0:GT, :]).then_inc(tok_stored, 16)
            sp.wait_ge(acc_free, 1)
            sp.dma_start(b2b[:, :, :].rearrange("p e c -> p (e c)"), b2.rearrange("(a e) c -> a (e c)", a=1).to_broadcast([128, NE * C])).then_inc(ld_b2, 16)
            for k in range(RING):
                sp.wait_ge(y_put[k], 16 * SLOTS // RING)
            sp.wait_ge(y_out, SLOTS)
            for t, a in ((gam, gamma), (bet, beta)):
                sp.dma_start(t[:, :], row(a).to_broadcast([128, C])).then_inc(ld_gb, 16)
            y_t = pair_out[0:2 * N, :].rearrange("(k t p) c -> k p t c", k=2, p=B)

            def load_results(i, j):
                for k in range(2):
                    sp.wait_ge(y_used, i * GT + (j + 1))
                    sp.dma_start(yb[0:B, k, j, :], y_t[k, :, ds(i * GT + j, 1), :].rearrange("p a c -> p (a c)")).then_inc(y_ld[j], 16)

            def store_tile(i, j):
                sp.wait_ge(fin_out, i * GT + (j + 1))
                sp.dma_start(out_t[:, ds(i * GT + j, 1), :].rearrange("p a c -> p (a c)"), ob[0:B, j, :]).then_inc(out_put[j], 16)

            for j in range(GT):
                load_results(0, j)
            with sp.Fori(0, NT // GT - 1) as i:
                for j in range(GT):
                    load_results(i + 1, j)
                for j in range(GT):
                    store_tile(i, j)
            for j in range(GT):
                store_tile(NT // GT - 1, j)
            for j in range(GT):
                sp.wait_ge(out_put[j], 16 * (NT // GT))

        def attention_fold_act(act):
            act.wait_ge(kvw1_mm, 1)
            nc.scalar.activation(kvw1[:, :, :].rearrange("p k n -> p (k n)"), bank[4][:, :], ACT.Copy).then_inc(kvw1_out, 1)

        @block.scalar
        def _(act):
            step = Steps(act, act_step)
            act.dma_start(bias_kv[:, :, :].rearrange("p h c -> p (h c)"), row(b_qkv).to_broadcast([128, 3 * C])).then_inc(ld_b, 16)
            for t, k, a in ((ln_g, 0, kln_g), (ln_g, 1, vln_g), (ln_b, 0, kln_b), (ln_b, 1, vln_b)):
                act.dma_start(t[:, k, :], row(a).to_broadcast([128, HD])).then_inc(ld_b, 16)
            for t, a in ((mb2, mix_b2), (gb, gnn_b)):
                act.dma_start(t[:, :], row(a).to_broadcast([128, C])).then_inc(ld_b, 16)
            act.dma_start(gateb[:, :], row(gate_b).to_broadcast([128, NE])).then_inc(ld_b, 16)
            act.dma_start(brow[0:NE * KF, :], b1.rearrange("e (m p) -> (e m) p", p=128)).then_inc(ld_b, 16)
            for j in range(2):
                act.dma_start(brow[64 + j:65 + j, :].rearrange("a (h d) -> a h d", d=HD),
                              b_qkv.rearrange("(a h s d) -> a h s d", a=2, s=3, d=HD)[j:j + 1, :, 0, :]).then_inc(ld_b, 16)
            act.dma_start(brow[66:68, :], mix_b1.rearrange("(a d) -> a d", d=128)).then_inc(ld_b, 16)

            act.wait_ge(var_ready, 1)
            nc.scalar.activation(st[0:B, 0, 0:NT], st[0:B, 1, 0:NT], ACT.Sqrt).then_inc(sqrt_done, 1)
            act.wait_ge(xn_ready, 1)
            for t in range(NT):
                ins = nc.scalar.activation(tout[0:B, t % 2, :], xn[0:B, t, :], ACT.Square, accum_out=st[0:B, 2, t:t + 1])
                step(ins)
            nc.scalar.activation(st[0:1, 13, 0:1], st[0:1, 2, 0:1], ACT.Copy).then_inc(squares, 1)
            act.wait_ge(var_ready, 2)
            nc.scalar.activation(st[0:B, 0, 0:NT], st[0:B, 1, 0:NT], ACT.Sqrt).then_inc(sqrt_done, 1)
            act.wait_ge(ln_arg, 1)
            nc.scalar.activation(st[0:B, 0, 0:NT], st[0:B, 6, 0:NT], ACT.Ln).then_inc(ln_done, 1)
            for t in range(NT):
                act.wait_ge(xn_t, t + 1)
                nc.scalar.activation(xnT[:, :, t * B:(t + 1) * B], bank[4 + t % 2][:, 0:KC * B].rearrange("p (k n) -> p k n", k=KC),
                                     ACT.Copy).then_inc(xn_t_out, 1)
            act.wait_ge(row_scale, 1)
            act.wait_ge(squares, 1)
            for t in range(NT):
                act.wait_ge(tab_mm, t + 1)
                if t >= 2:
                    act.wait_ge(tab_stored[t % 2], 16 * (t // 2))
                nc.scalar.activation(tout[0:B, t % 2, :], bank[2 + t % 2][0:B, 0:C], ACT.Copy,
                                     scale=st[0:B, 7, t:t + 1]).then_inc(tab_out, 1)
            act.wait_ge(setup_t, 1)
            nc.scalar.activation(wqT[:, :, :].rearrange("p k n -> p (k n)"), bank[5][:, :], ACT.Copy)
            nc.scalar.activation(bcol[:, 0:68], bank[4][:, 0:68], ACT.Copy).then_inc(setup_t_out, 1)

            for g, turns, turn0, nsort, mix, tile0 in SEGS:
                c0 = CHUNK0[g] + RING * turn0
                if turn0 == 0:
                    act.wait_ge(group_ready, g + 1)
                if g == 2 and turn0 == 0:
                    attention_fold_act(act)
                def turn(i):
                    if mix == 1:
                        await_ge(act, kv_mm, i + tile0)
                        nc.scalar.activation(xst[:, :, :], xnT[:, :, ds((i + tile0) * B, B)], ACT.Copy).then_inc(xst_ready, 1)
                    for k in range(RING):
                        act.wait_ge(chunk_done, i * RING + (c0 + k + 1))
                        nc.scalar.activation(idx[:, k:k + 1], g_row[:, ds(i * RING + turn0 * RING + k, 1)], ACT.Copy).then_inc(idx_ready, 1)
                    if mix == 1:
                        act.wait_ge(kv_sb, i + tile0 + 1)
                        await_ge(act, kv_var, i + tile0)
                        nc.scalar.activation(kvs[0:B], kvc[0:B], ACT.Square).then_inc(kv_sq, 1)
                        act.wait_ge(kv_var, i + tile0 + 1)
                        nc.scalar.activation(kvst[0:B, 1, :], kvst[0:B, 0, :], ACT.Sqrt).then_inc(kv_std, 1)
                    if mix == 2:
                        act.wait_ge(mh_mm, i + (tile0 + 1))
                        await_ge(act, my_mm, i + tile0)
                        for m in range(KC):
                            ins = nc.scalar.activation(mhT[:, m, :], bank[4][:, m * B:(m + 1) * B], ACT.Gelu, bias=beff[:, m:m + 1])
                        ins.then_inc(mh_out, 1)

                if turns == 1:
                    turn(0)
                else:
                    with act.Fori(0, turns) as i:
                        turn(i)
            act.wait_ge(chunk_added, HALVES + CHUNKS)
            act.wait_ge(chunk_done, RING + CHUNKS)
            for t in range(NT + 1):
                step(nc.scalar.activation(rows[0:B, 0, :], acc[0:B, t, :] if t < NT else gb[0:B, :], ACT.Square,
                                          accum_out=st[0:B, 2, t:t + 1]))
            nc.scalar.activation(small[0:1, 5, 0:1], small[0:1, 4, 0:1], ACT.Copy).then_inc(tail_ss, 1)
            act.wait_ge(tail_v, 1)
            nc.scalar.activation(st[0:B, 0, :], st[0:B, 1, :], ACT.Sqrt).then_inc(tail_sq, 1)
            act.wait_ge(tail_v, 2)
            nc.scalar.activation(st[0:B, 7, :], st[0:B, 6, :], ACT.Tanh).then_inc(tail_tanh, 1)
            act.wait_ge(tail_v, 3)
            nc.scalar.activation(st[0:B, 0, 0:NT], st[0:B, 1, 0:NT], ACT.Sqrt).then_inc(tail_sq, 1)
            def middle_turn(i):
                act.wait_ge(mid_var, i + 1)
                nc.scalar.activation(st5[0:B, 1, :], st5[0:B, 0, :], ACT.Sqrt).then_inc(mid_root, 1)
                act.wait_ge(mid_scale, i + 1)
                await_ge(act, tok_stored, i * 16)
                await_ge(act, mt_mm, i * GT)
                for j in range(GT):
                    nc.scalar.activation(rows[0:B, j, :], X[0:B, ds(i * GT + j, 1), :].rearrange("p a c -> p (a c)"), ACT.Identity,
                                         bias=st5[0:B, 3, j:j + 1], scale=st5[0:B, 2, j:j + 1]).then_inc(mid_norm, 1)
                for j in range(GT):
                    act.wait_ge(mt_mm, i * GT + (j + 1))
                    await_ge(act, mg_mm, i * GT + max(j - 1, 0))
                    nc.scalar.activation(tT[:, j % 2, :, 0:B], bank[4 + j % 2][:, 0:KC * B].rearrange("p (k n) -> p k n", k=KC),
                                         ACT.Copy).then_inc(mt_out, 1)

            turns_of(act, 0, NT // GT, middle_turn)
            act.wait_ge(exp_arg, 1)
            nc.scalar.activation(st[0:B, 1, 0:NT], st[0:B, 0, 0:NT], ACT.Exp).then_inc(exp_done, 1)
            act.wait_ge(slots_ready, 1)

            def token_numbers(i, k):
                await_ge(act, tok_got[k], i * 16)
                nc.scalar.activation(idx[:, k:k + 1], s_tok[:, ds(i * RING + k, 1)], ACT.Copy).then_inc(tok_idx, 1)

            for k in range(RING):
                token_numbers(0, k)

            def expert_turn(i, last):
                _, offs = nc.values_load_multi_w_load_instructions(
                    ex_b1[0:1, ds(i * RING, RING)], engines=[ACT_], min_val=0, max_val=(NE - 1) * KF,
                    skip_runtime_bounds_check_because="the router clamps it")
                for k in range(RING):
                    await_ge(act, y_put[k], i * 16)
                    nc.scalar.activation(odx[:, k:k + 1], s_row[:, ds(i * RING + k, 1)], ACT.Copy).then_inc(out_idx, 1)
                    act.wait_ge(h_mm, i * RING + (k + 1))
                    await_ge(act, y_mm, i * RING + max(k - 1, 0))
                    for m in range(KF):
                        ins = nc.scalar.activation(hT[:, k % 2, m, :], bank[2 + k % 2][:, m * 128:(m + 1) * 128], ACT.Relu,
                                                   bias=bcol[:, ds(offs[k] + m, 1)])
                    ins.then_inc(h_out, 1)
                    if not last:
                        token_numbers(i + 1, k)

            turns_of(act, 0, SLOTS // RING, lambda i: expert_turn(i, False), lambda i: expert_turn(i, True))
            def last_turn(i):
                for j in range(GT):
                    await_ge(act, fin_norm, i * GT)
                    nc.scalar.activation(zb[0:B, j, :], X[0:B, ds(i * GT + j, 1), :].rearrange("p a c -> p (a c)"), ACT.Identity,
                                         bias=mid_nb[0:B, ds(i * GT + j, 1)], scale=mid_rs[0:B, ds(i * GT + j, 1)]).then_inc(fz, 1)
                act.wait_ge(fin_var, i + 1)
                nc.scalar.activation(st5[0:B, 1, :], st5[0:B, 0, :], ACT.Sqrt).then_inc(fin_root, 1)
                act.wait_ge(fin_scale, i + 1)
                for j in range(GT):
                    await_ge(act, fin_out, i * GT)
                    nc.scalar.activation(ub[0:B, j, :], zb[0:B, j, :], ACT.Identity,
                                         bias=st5[0:B, 3, j:j + 1], scale=st5[0:B, 2, j:j + 1]).then_inc(fin_norm, 1)

            turns_of(act, 0, NT // GT, last_turn)

        @block.gpsimd
        def _(pool):
            step = Steps(pool, pool_step)
            nc.gpsimd.memset(esrc[:, FULL:COLS], 0).then_inc(pads, 1)
            nc.gpsimd.memset(edst[:, FULL:COLS], 0).then_inc(pads, 1)
            nc.gpsimd.memset(ew[:, FULL:COLS], 0.0).then_inc(pads, 1)
            step.mark(nc.gpsimd.iota(iota[:, :], pattern=[[1, HMAX]], base=0, channel_multiplier=0, allow_small_or_imprecise_dtypes=True))
            step.mark(nc.gpsimd.iota(node[:, :], pattern=[[B, NT]], base=0, channel_multiplier=1, allow_small_or_imprecise_dtypes=True))
            step.mark(nc.gpsimd.iota(slot_id[:, :], pattern=[[128, SLOTS]], base=2 * N + 1, channel_multiplier=1,
                                     allow_small_or_imprecise_dtypes=True))
            step.mark(nc.gpsimd.memset(ones[:, :], 1.0))
            step.mark(nc.gpsimd.memset(ident[:, :], 0.0))
            step.mark(nc.gpsimd.memset(small[:, :, :], 0.0))
            step(nc.gpsimd.memset(zeros[:, :], 0.0))
            step(nc.gpsimd.affine_select(out=tri[:, :], in_=ones[:, :], compare_op=ALU.is_gt, fill=0.0, base=0,
                                         pattern=[[1, 128]], channel_multiplier=-1))
            nc.gpsimd.affine_select(out=ident[:, :], in_=ident[:, :], compare_op=ALU.not_equal, fill=1.0, base=0,
                                    pattern=[[-1, 128]], channel_multiplier=1).then_inc(consts, 1)
            step(nc.gpsimd.memset(accf[:, :], 0.0))
            pool.wait_ge(xn_ready, 1)
            pool.wait_ge(ld_b, 16 * B_LOADS)
            step(nc.gpsimd.tensor_tensor(X[0:B, :, :], X[0:B, :, :], xn[0:B, :, :], ALU.add))
            nc.gpsimd.tensor_tensor(X[0:B, :, :], X[0:B, :, :], mb2[0:B, :].unsqueeze(1).to_broadcast([B, NT, C]),
                                    ALU.add).then_inc(x_plus, 1)
            pool.wait_ge(tab_stored[0], 16 * (NT - NT // 2))
            pool.wait_ge(tab_stored[1], 16 * (NT // 2))
            for g in range(3):
                turn_base = CHUNK0[g] // RING
                with pool.Fori(0, TURNS[g]) as i:
                    for k in range(RING):
                        pool.wait_ge(idx_ready, i * RING + CHUNK0[g] + k + 1)
                        pool.wait_ge(chunk_done, i * RING + (CHUNK0[g] + k + 1))
                        pool.sem_inc(may_go, 1)
                        nc.gpsimd.indirect_dma_start(
                            out=rows[:, k, :], out_offset=None, in_=table[:, :],
                            in_offset=bass.IndirectOffsetOnAxis(ap=idx[:, k:k + 1], axis=0)).then_inc(gathered[k], 16)

            pool.wait_ge(tok_stored, 16 * (NT // GT))

            def get_tokens(i, k, turns_before, turned):
                pool.wait_ge(tok_idx, i * RING + (k + 1))
                await_ge(pool, x_mm, turns_before * RING + (k + 1 if turned else 0))
                pool.sem_inc(may_go, 1)
                nc.gpsimd.indirect_dma_start(
                    out=rows[:, k, :], out_offset=None, in_=tokens[:, :],
                    in_offset=bass.IndirectOffsetOnAxis(ap=idx[:, k:k + 1], axis=0)).then_inc(tok_got[k], 16)

            def put_results(i, k):
                pool.wait_ge(out_idx, i * RING + (k + 1))
                pool.wait_ge(y_out, i * RING + (k + 1))
                pool.sem_inc(may_go, 1)
                nc.gpsimd.indirect_dma_start(
                    out=pair_out[:, :], out_offset=bass.IndirectOffsetOnAxis(ap=odx[:, k:k + 1], axis=0),
                    in_=yv[:, k % 2, :], in_offset=None).then_inc(y_put[k], 16)

            for k in range(RING):
                get_tokens(0, k, 0, False)
            with pool.Fori(0, SLOTS // RING - 1) as i:
                for k in range(RING):
                    put_results(i, k)
                    get_tokens(i + 1, k, i, True)
            for k in range(RING):
                put_results(SLOTS // RING - 1, k)
            pool.wait_ge(ld_gb, 32)
            pstep = Steps(pool, pool_step)
            pstep.done = step.done
            with pstep.loop(NT // GT, GT) as i:
                for j in range(GT):
                    pool.wait_ge(fin_norm, i * GT + (j + 1))
                    pstep(nc.gpsimd.tensor_tensor(ub[0:B, j, :], ub[0:B, j, :], gam[0:B, :], ALU.mult))
                    nc.gpsimd.tensor_tensor(ub[0:B, j, :], ub[0:B, j, :], bet[0:B, :], ALU.add).then_inc(fin_aff, 1)

        def rsqrt_refined(step, out_, var, root, tmp):
            step(nc.vector.reciprocal(out_, root))
            step(nc.vector.tensor_tensor(tmp, out_, out_, ALU.mult))
            step(nc.vector.tensor_tensor(tmp, tmp, var, ALU.mult))
            step(nc.vector.tensor_scalar(tmp, tmp, -0.5, 1.5, ALU.mult, ALU.add))
            step(nc.vector.tensor_tensor(out_, out_, tmp, ALU.mult))

        def route(dve, step, rounds, P, T, nb, H, key_, lo_, hi_, buckets, rt_one=rt_one, rt_sum=rt_sum):
            one = rt_one[0:P, 0:nb * T]
            run = rt_sum[0:P, 0:nb * T]
            one3, run3 = one.rearrange("p (b t) -> p b t", b=nb), run.rearrange("p (b t) -> p b t", b=nb)
            ends, mine, first, off = small[0:P, 0, :], small[0:P, 1, :], small[0:P, 2, :], small[0:P, 3, :]
            step(nc.vector.tensor_tensor(one3, key_.unsqueeze(1).to_broadcast([P, nb, T]),
                                         iota[0:P, 0:nb].unsqueeze(2).to_broadcast([P, nb, T]), ALU.is_equal))
            step(nc.vector.tensor_tensor_scan(run, one, one, 0.0, ALU.add, ALU.max))
            step(nc.vector.tensor_copy(ends[:, 1:nb + 1], run3[:, :, T - 1]))
            nc.vector.tensor_tensor(mine[:, 0:nb], ends[:, 1:nb + 1], ends[:, 0:nb], ALU.subtract).then_inc(rank_rows, 1)
            dve.wait_ge(rank_sums, rounds)
            before, total = bank[6][0:P, 0:nb], bank[6][0:P, 32:32 + nb]
            step(nc.vector.tensor_scalar(slot_i[0:P, 0:nb], total, 127.0, None, ALU.add))
            step(nc.vector.tensor_scalar(cnt_i[0:P, 0:nb], slot_i[0:P, 0:nb], 7, None, ALU.logical_shift_right))
            step(nc.vector.tensor_copy(off[:, 0:nb], cnt_i[0:P, 0:nb]))
            step(nc.vector.tensor_tensor_scan(first[:, 1:nb + 1], off[:, 0:nb], off[:, 0:nb], 0.0, ALU.add, ALU.max))
            step(nc.vector.scalar_tensor_tensor(off[:, 0:nb], first[:, 0:nb], 128.0, before, ALU.mult, ALU.add))
            step(nc.vector.scalar_tensor_tensor(off[:, 0:nb], off[:, 0:nb], -1.0, ends[:, 0:nb], ALU.add, ALU.subtract))
            step(nc.vector.tensor_tensor(run3, run3, off[:, 0:nb].unsqueeze(2).to_broadcast([P, nb, T]), ALU.add))
            step(nc.vector.tensor_tensor(run, run, one, ALU.mult))
            step(nc.vector.tensor_reduce(slot[0:P, 0:T], run.rearrange("p (b t) -> p t b", b=nb), AX.X, ALU.add))
            cmp = rt_one[0:1, 0:H * nb].rearrange("p (h b) -> p h b", b=nb)
            step.mark(nc.vector.tensor_tensor(cmp, first[0:1, 1:nb + 1].unsqueeze(1).to_broadcast([1, H, nb]),
                                              iota[0:1, 0:H].unsqueeze(2).to_broadcast([1, H, nb]), ALU.is_le))
            step(nc.vector.tensor_copy(slot_i[0:P, 0:T], slot[0:P, 0:T]))
            step.mark(nc.vector.tensor_reduce(bk_f[0:1, 0:H], cmp, AX.X, ALU.add))
            step(nc.vector.tensor_scalar(slot_j[0:P, 0:T], slot_i[0:P, 0:T], 7, None, ALU.logical_shift_right))
            for bucket, scale in buckets:
                step.mark(nc.vector.tensor_scalar(bucket, bk_f[0:1, 0:H], float(nb - 1), float(scale), ALU.min, ALU.mult))
            step(nc.vector.tensor_copy(hi_, slot_j[0:P, 0:T]))
            step(nc.vector.tensor_scalar(slot_j[0:P, 0:T], slot_i[0:P, 0:T], 127, None, ALU.bitwise_and))
            step(nc.vector.tensor_copy(lo_, slot_j[0:P, 0:T]))

        def sort_column(dve, j, n, s, H):
            if n is not None:
                dve.wait_ge(hots_used, n)
            nc.vector.tensor_scalar(s_lo[:, s, 0, :], iota[:, 0:128], lo[:, ds(j, 1)], pack[:, ds(j, 1)], ALU.is_equal, ALU.mult)
            nc.vector.tensor_scalar(s_lo[:, s, 1, :], iota[:, 0:128], lo[:, ds(j, 1)], ew[:, ds(j, 1)], ALU.is_equal, ALU.mult)
            nc.vector.tensor_scalar(s_hi[:, s, 0:H], iota[:, 0:H], hi[:, ds(j, 1)], None, ALU.is_equal).then_inc(hots_made, 1)

        def take_group(dve, step, g):
            H = H_OF[g]
            dve.wait_ge(sorted_, g + 1)
            if g:
                dve.wait_ge(idx_ready, CHUNK0[g])
            step.mark(nc.vector.tensor_copy(g_w[:, 0:H], bank[1][:, 0:H]))
            step(nc.vector.tensor_copy(slot_i[:, 0:H], bank[0][:, 0:H]))
            step.mark(nc.vector.tensor_scalar(g_row[:, 0:H], slot_i[:, 0:H], 7, None, ALU.logical_shift_right))
            step(nc.vector.tensor_scalar(slot_j[:, 0:H], slot_i[:, 0:H], 127, None, ALU.bitwise_and))
            step(nc.vector.tensor_copy(g_lo[:, 0:H], slot_j[:, 0:H]))
            nc.vector.memset(slot[0:1, 191:192], 0.0).then_inc(group_ready, 1)

        def attention_fold_dve(dve, step):
            dve.wait_ge(kv_used, NT)
            step(nc.vector.memset(kvT[:, :, :], 0.0))
            for j in range(KC):
                for h in range(4):
                    s = slice(h * HD, (h + 1) * HD)
                    ins = nc.vector.tensor_scalar(kvT[s, j, s], bank[6 + j][s, s], 1.0 / N, None, ALU.mult)
            ins.then_inc(kvT_ready, 1)
            dve.wait_ge(weff_mm, 1)
            step.mark(nc.vector.tensor_tensor(weff[:, :, :].rearrange("p k n -> p (k n)"), bank[5][:, :],
                                              mw1[:, :, :].rearrange("p k n -> p (k n)"), ALU.add))
            for m in range(KC):
                step.mark(nc.vector.tensor_tensor(beff[:, m:m + 1], bank[6][:, m:m + 1], bcol[:, 66 + m:67 + m], ALU.add))
            step.wait()
            nc.vector.memset(slot[0:1, 191:192], 0.0).then_inc(weff_out, 1)

        def attention_keys_dve(dve, step, k, i, tile0):
            kv3 = kvc[0:B].rearrange("p h s d -> p (h s) d")
            if k == 1:
                dve.wait_ge(kv_mm, i + (tile0 + 1))
                nc.vector.tensor_tensor(kvc[0:B], bank[4][0:B, :].rearrange("p (h s d) -> p h s d", h=HEADS, s=2),
                                        bias_kv[0:B, :, HD:3 * HD].rearrange("p h (s d) -> p h s d", s=2), ALU.add).then_inc(kv_sb, 1)
            if k == 2:
                dve.wait_ge(kv_sq, i + (tile0 + 1))
                step(nc.vector.tensor_reduce(kvst[0:B, 2, :], kvs[0:B].rearrange("p h s d -> p (h s) d"), AX.X, ALU.add))
                nc.vector.tensor_scalar(kvst[0:B, 0, :], kvst[0:B, 2, :], 1.0 / HD, LN_EPS, ALU.mult, ALU.add).then_inc(kv_var, 1)
            if k == 4:
                dve.wait_ge(kv_std, i + (tile0 + 1))
                step(nc.vector.reciprocal(kvst[0:B, 3, :], kvst[0:B, 1, :]))
                step(nc.vector.tensor_tensor(kv3, kv3, kvst[0:B, 3, :].unsqueeze(2).to_broadcast([B, 2 * HEADS, HD]), ALU.mult))
            if k == 5:
                g3 = ln_g[0:B].rearrange("p s d -> p (s d)").unsqueeze(1).to_broadcast([B, HEADS, 2 * HD])
                kvr = kvc[0:B].rearrange("p h s d -> p h (s d)")
                step(nc.vector.tensor_tensor(kvr, kvr, g3, ALU.mult))
                step(nc.vector.memset(slot[0:1, 191:192], 0.0))
            if k == 6:
                await_ge(dve, kv_used, i + tile0)
                for s in range(2):
                    ins = nc.vector.tensor_tensor(kvn[0:B, s], kvc[0:B, :, s, :],
                                                  ln_b[0:B, s, :].unsqueeze(1).to_broadcast([B, HEADS, HD]), ALU.add)
                ins.then_inc(kv_norm, 1)

        @block.vector
        def _(dve):
            step = Steps(dve, dve_step)
            dve.wait_ge(ld_edge, 16 * 6)
            step(nc.vector.tensor_scalar(eq[:, :], esrc[:, :], 4195.0, None, ALU.mult))
            step(nc.vector.tensor_scalar(eq[:, :], eq[:, :], 19, None, ALU.logical_shift_right))
            step(nc.vector.tensor_copy(key[:, :], eq[:, :]))
            step(nc.vector.scalar_tensor_tensor(pack[:, :], key[:, :], -float(B), esrc[:, :], ALU.mult, ALU.add))
            step(nc.vector.scalar_tensor_tensor(pack[:, :], edst[:, :], 128.0, pack[:, :], ALU.mult, ALU.add))
            dve.wait_ge(consts, 1)
            nc.vector.memset(slot[0:1, 191:192], 0.0).then_inc(chunk_added, HALVES)
            T = T_OF[0]
            route(dve, step, 1, 128, T, NT, H_OF[0], key[:, 0:T], lo[:, 0:T], hi[:, 0:T], [(bk[0][0:1, :], C)])
            dve.wait_ge(ld_x, 32)
            for t in range(NT):
                step(nc.vector.bn_stats(bn6[0:B, :], X[0:B, t, :]))
                step(nc.vector.bn_aggr(mv[0:B, t, :], bn6[0:B, :]))
            nc.vector.tensor_scalar(st[0:B, 1, 0:NT], mv[0:B, :, 1], LN_EPS, None, ALU.add).then_inc(var_ready, 1)
            dve.wait_ge(sqrt_done, 1)
            rsqrt_refined(step, st[0:B, 3, 0:NT], st[0:B, 1, 0:NT], st[0:B, 0, 0:NT], st[0:B, 4, 0:NT])
            for t in range(NT):
                ins = nc.vector.tensor_scalar(xn[0:B, t, :], X[0:B, t, :], mv[0:B, t, 0:1], st[0:B, 3, t:t + 1], ALU.subtract, ALU.mult)
            ins.then_inc(xn_ready, 1)
            with dve.Fori(0, (T - 3) // SR) as i:
                for s in range(SR):
                    sort_column(dve, i * SR + s, i * SR + (s + 1), s, H_OF[0])
            for j in range((T - 3) // SR * SR, T):
                sort_column(dve, j, j + 1, j % SR, H_OF[0])
            def s_(k):
                return st[0:B, k, 0:NT]
            dve.wait_ge(squares, 1)
            nc.vector.tensor_scalar(s_(1), s_(2), EPS * EPS, None, ALU.max).then_inc(var_ready, 1)
            dve.wait_ge(sqrt_done, 2)
            rsqrt_refined(step, s_(3), s_(1), s_(0), s_(4))
            step(nc.vector.tensor_tensor(s_(3), s_(3), s_(1), ALU.mult))
            step(nc.vector.tensor_scalar(s_(3), s_(3), MAXNORM, None, ALU.min))
            step.mark(nc.vector.tensor_scalar(s_(4), s_(3), -1.0, 1.0, ALU.mult, ALU.add))
            step(nc.vector.tensor_scalar(s_(5), s_(3), 1.0, None, ALU.add))
            step(nc.vector.reciprocal(s_(4), s_(4)))
            nc.vector.tensor_tensor(s_(6), s_(5), s_(4), ALU.mult).then_inc(ln_arg, 1)
            step(nc.vector.tensor_tensor(s_(11), s_(3), s_(3), ALU.mult))
            step(nc.vector.tensor_scalar(s_(8), s_(11), 1 / 7, 1 / 5, ALU.mult, ALU.add))
            step(nc.vector.tensor_tensor(s_(8), s_(8), s_(11), ALU.mult))
            step(nc.vector.tensor_scalar(s_(8), s_(8), 1 / 3, None, ALU.add))
            step(nc.vector.tensor_tensor(s_(8), s_(8), s_(11), ALU.mult))
            step(nc.vector.tensor_scalar(s_(8), s_(8), 1.0, None, ALU.add))
            step(nc.vector.reciprocal(s_(9), s_(3)))
            dve.wait_ge(ln_done, 1)
            step(nc.vector.scalar_tensor_tensor(s_(9), s_(0), 0.5, s_(9), ALU.mult, ALU.mult))
            step(nc.vector.tensor_tensor(s_(8), s_(8), s_(9), ALU.subtract))
            step(nc.vector.tensor_scalar(s_(10), s_(3), 0.06, None, ALU.is_lt))
            step(nc.vector.tensor_tensor(s_(8), s_(8), s_(10), ALU.mult))
            nc.vector.tensor_tensor(s_(7), s_(8), s_(9), ALU.add).then_inc(row_scale, 1)
            take_group(dve, step, 0)
            dve.wait_ge(ld_w, 16 * W_LOADS)
            dve.wait_ge(ld_b, 16 * B_LOADS)
            for k in range(KC):
                step.mark(nc.vector.tensor_copy(weff[:, k, :].rearrange("p (h d) -> p h d", d=HD),
                                                wqkv[:, k, :].rearrange("p (h s d) -> p h s d", s=3, d=HD)[:, :, 0, :]))
                w3 = wqkv[:, k, :].rearrange("p (a d) -> p a d", d=HD)
                step(nc.vector.tensor_reduce(wmean[:, k, :], w3, AX.X, ALU.add))
                step.mark(nc.vector.scalar_tensor_tensor(
                    wcen[:, k, :].rearrange("p (a d) -> p a d", d=HD), wmean[:, k, :].unsqueeze(2).to_broadcast([128, 3 * HEADS, HD]),
                    -1.0 / HD, w3, ALU.mult, ALU.add))
            b3 = bias_kv[:, :, :].rearrange("p h (s d) -> p (h s) d", d=HD)
            step(nc.vector.tensor_reduce(wmean[:, 0, :], b3, AX.X, ALU.add))
            step(nc.vector.scalar_tensor_tensor(b3, wmean[:, 0, :].unsqueeze(2).to_broadcast([128, 3 * HEADS, HD]),
                                                -1.0 / HD, b3, ALU.mult, ALU.add))
            nc.vector.memset(slot[0:1, 191:192], 0.0).then_inc(wcen_ready, 1)
            dve.wait_ge(xn_t, NT)
            dve.wait_ge(squares, 1)
            dve.wait_ge(x_plus, 1)
            for g in (1, 2):
                a, T = AT[g], T_OF[g]
                route(dve, step, g + 1, 128, T, NT, H_OF[g], key[:, a:a + T], lo[:, a:a + T], hi[:, a:a + T], [(bk[g][0:1, :], C)])

            for g, turns, turn0, nsort, mix, tile0 in SEGS:
                c0 = CHUNK0[g] + RING * turn0
                if g and turn0 == 0:
                    take_group(dve, step, g)
                if g == 2 and turn0 == 0:
                    attention_fold_dve(dve, step)
                col0 = AT[g + 1] + nsort * turn0 if nsort else 0
                split = shares(nsort, RING)
                def turn(i):
                    _, offs = nc.values_load_multi_w_load_instructions(
                        bk[g][0:1, ds(i * RING + turn0 * RING, RING)], engines=[DVE_], min_val=0, max_val=(NT - 1) * C,
                        skip_runtime_bounds_check_because="the router clamps it")
                    for k in range(RING):
                        if k == 0:
                            dve.wait_ge(chunk_done, i * RING + (RING + c0))
                        nc.vector.tensor_scalar(hot[:, k, :], iota[:, 0:128], g_lo[:, ds(i * RING + turn0 * RING + k, 1)],
                                                g_w[:, ds(i * RING + turn0 * RING + k, 1)], ALU.is_equal, ALU.mult).then_inc(hot_ready, 1)
                    m = 0
                    for k in range(RING):
                        for _ in range(split[k]):
                            before = m - SR if m >= SR else m + SR * ((nsort - 1 - m) // SR) - nsort
                            sort_column(dve, i * nsort + (col0 + m), i * nsort + (SR + col0 + before + 1), m % SR, H_OF[g + 1])
                            m += 1
                        if mix == 1:
                            attention_keys_dve(dve, step, k, i, tile0)
                        if mix == 2 and k == 6:
                            dve.wait_ge(my_mm, i + (tile0 + 1))
                            nc.vector.tensor_tensor(X[0:B, ds(i + tile0, 1), :], X[0:B, ds(i + tile0, 1), :],
                                                    bank[5][0:B, 0:C].unsqueeze(1), ALU.add).then_inc(my_out, 1)
                        if k % 2:
                            dve.wait_ge(chunk_done, i * RING + (RING + c0 + k + 1))
                            for h in (k - 1, k):
                                dve.wait_ge(chunk_added, i * RING + (HALVES + c0 + h))
                                to = accf[:, ds(offs[h], C)]
                                nc.vector.tensor_tensor(to, to, bank[2 + h // 2 % 2][:, h % 2 * C:(h % 2 + 1) * C],
                                                        ALU.add).then_inc(chunk_added, 1)

                if turns == 1:
                    turn(0)
                else:
                    with step.loop(turns, 5 if mix == 1 else 0) as i:
                        turn(i)
            dve.wait_ge(chunk_added, HALVES + CHUNKS)
            for t in range(NT):
                step(nc.vector.tensor_tensor_reduce(out=rows[0:B, 1, :], in0=acc[0:B, t, :], in1=gb[0:B, :], scale=1.0, scalar=0.0,
                                                    op0=ALU.mult, op1=ALU.add, accum_out=st[0:B, 3, t:t + 1]))

            def a_(k):
                return st[0:B, k, :]

            def one(k):
                return st[0:B, k, NT:NT + 1]
            dve.wait_ge(tail_ss, 1)
            nc.vector.tensor_scalar(a_(1), a_(2), EPS * EPS, None, ALU.max).then_inc(tail_v, 1)
            dve.wait_ge(tail_sq, 1)
            rsqrt_refined(step, a_(4), a_(1), a_(0), a_(5))
            step(nc.vector.tensor_tensor(a_(5), a_(4), a_(1), ALU.mult))
            nc.vector.tensor_scalar(a_(6), a_(5), 15.0, None, ALU.min).then_inc(tail_v, 1)
            dve.wait_ge(tail_tanh, 1)
            step(nc.vector.tensor_scalar(a_(8), a_(7), EPS, None, ALU.max))
            step(nc.vector.reciprocal(a_(8), a_(8)))
            step(nc.vector.tensor_scalar(a_(8), a_(8), MAXNORM, 1.0, ALU.mult, ALU.min))
            step(nc.vector.tensor_tensor(a_(4), a_(4), a_(7), ALU.mult))
            step(nc.vector.tensor_tensor(a_(8), a_(8), a_(4), ALU.mult))
            step(nc.vector.tensor_tensor(a_(9), a_(8), a_(8), ALU.mult))
            step(nc.vector.tensor_tensor(a_(9), a_(9), a_(2), ALU.mult))
            step(nc.vector.tensor_tensor(s_(10), s_(8), s_(3), ALU.mult))
            step(nc.vector.tensor_scalar(s_(10), s_(10), one(8), 2.0, ALU.mult, ALU.mult))
            step(nc.vector.tensor_scalar(s_(11), s_(10), 1.0, None, ALU.add))
            step(nc.vector.scalar_tensor_tensor(s_(12), s_(11), one(9), s_(8), ALU.add, ALU.mult))
            step(nc.vector.scalar_tensor_tensor(s_(13), s_(9), one(9), s_(11), ALU.mult, ALU.add))
            step(nc.vector.tensor_scalar(s_(13), s_(13), EPS, None, ALU.add))
            step(nc.vector.reciprocal(s_(13), s_(13)))
            step(nc.vector.tensor_scalar(s_(10), s_(9), -1.0, 1.0, ALU.mult, ALU.add))
            step(nc.vector.tensor_scalar(s_(10), s_(10), one(8), None, ALU.mult))
            step(nc.vector.tensor_tensor(s_(12), s_(12), s_(13), ALU.mult))
            step(nc.vector.tensor_tensor(s_(13), s_(10), s_(13), ALU.mult))
            step(nc.vector.tensor_tensor(s_(5), s_(13), s_(3), ALU.mult))
            step(nc.vector.tensor_tensor(s_(6), s_(12), s_(2), ALU.mult))
            step(nc.vector.scalar_tensor_tensor(s_(5), s_(5), 2.0, s_(6), ALU.mult, ALU.add))
            step(nc.vector.tensor_tensor(s_(5), s_(5), s_(12), ALU.mult))
            step(nc.vector.tensor_tensor(s_(6), s_(13), s_(13), ALU.mult))
            step(nc.vector.scalar_tensor_tensor(s_(5), s_(6), one(2), s_(5), ALU.mult, ALU.add))
            nc.vector.tensor_scalar(s_(1), s_(5), EPS * EPS, None, ALU.max).then_inc(tail_v, 1)
            dve.wait_ge(tail_sq, 2)
            rsqrt_refined(step, s_(4), s_(1), s_(0), s_(5))
            step(nc.vector.tensor_scalar(s_(4), s_(4), MAXNORM, 1.0, ALU.mult, ALU.min))
            step.mark(nc.vector.tensor_tensor(s_(14), s_(12), s_(4), ALU.mult))
            step(nc.vector.tensor_tensor(s_(15), s_(13), s_(4), ALU.mult))

            def norm_scale(step, signal):
                rsqrt_refined(step, st5[0:B, 2, :], st5[0:B, 0, :], st5[0:B, 1, :], st5[0:B, 4, :])
                nc.vector.scalar_tensor_tensor(st5[0:B, 3, :], mv5[0:B, :, 0], -1.0, st5[0:B, 2, :], ALU.mult, ALU.mult).then_inc(signal, 1)

            for i in range(NT // GT):
                for j in range(GT):
                    xt = X[0:B, ds(i * GT + j, 1), :].rearrange("p a c -> p (a c)")
                    step(nc.vector.scalar_tensor_tensor(xt, acc[0:B, ds(i * GT + j, 1), :].rearrange("p a c -> p (a c)"),
                                                        st[0:B, 14, ds(i * GT + j, 1)], xt, ALU.mult, ALU.add))
                    step(nc.vector.scalar_tensor_tensor(xt, gb[0:B, :], st[0:B, 15, ds(i * GT + j, 1)], xt, ALU.mult, ALU.add))
                    step(nc.vector.bn_stats(bn6[0:B, :], xt))
                    step(nc.vector.bn_aggr(mv5[0:B, j, :], bn6[0:B, :]))
                nc.vector.tensor_scalar(st5[0:B, 0, :], mv5[0:B, :, 1], LN_EPS, None, ALU.add).then_inc(mid_var, 1)
                dve.wait_ge(mid_root, i + 1)
                norm_scale(step, mid_scale)
                step.mark(nc.vector.tensor_copy(mid_rs[0:B, ds(i * GT, GT)], st5[0:B, 2, :]))
                dve.wait_ge(mid_scale, i + 1)
                step.mark(nc.vector.tensor_copy(mid_nb[0:B, ds(i * GT, GT)], st5[0:B, 3, :]))
                for j in range(GT):
                    dve.wait_ge(mg_mm, i * GT + (j + 1))
                    nc.vector.tensor_tensor(lg[0:B, j % 2, :], bank[6 + j % 2][0:B, 0:NE], gateb[0:B, :], ALU.add).then_inc(mg_out, 1)
                    dve.wait_ge(mg_out, i * GT + (j + 1))
                    step(nc.vector.max(mx5[0:B, j, :], lg[0:B, j % 2, :]))
                    step(nc.vector.max_index(ix5[0:B, j, :], mx5[0:B, j, :], lg[0:B, j % 2, :]))
                step.mark(nc.vector.tensor_copy(topv[0:B, :, ds(i * GT, GT)], mx5[0:B, :, 0:2].rearrange("p t k -> p k t")))
                step(nc.vector.tensor_copy(pair_key[0:B, :, ds(i * GT, GT)], ix5[0:B, :, 0:2].rearrange("p t k -> p k t")))
            nc.vector.tensor_tensor(s_(0), topv[0:B, 1, :], topv[0:B, 0, :], ALU.subtract).then_inc(exp_arg, 1)
            nc.vector.memset(slot[0:1, 191:192], 0.0).then_inc(acc_free, 1)
            dve.wait_ge(tok_stored, 16 * (NT // GT))
            dve.wait_ge(mt_mm, NT)
            flat = rows[:, :, :].rearrange("p k c -> p (k c)")
            route(dve, step, 4, B, PAIRS, NE, SLOTS, pair_key[0:B, :, :].rearrange("p k t -> p (k t)"), pair_lo[0:B, :], pair_hi[0:B, :],
                  [(ex_w[0:1, :], 2048), (ex_b1[0:1, :], KF), (ex_b2[0:1, :], C)], flat[:, 0:NE * SLOTS], flat[:, 1024:2048])
            dve.wait_ge(exp_done, 1)
            step(nc.vector.tensor_scalar(s_(2), s_(1), 1.0, None, ALU.add))
            step(nc.vector.reciprocal(pair_w[0:B, 0, :], s_(2)))
            step(nc.vector.tensor_tensor(pair_w[0:B, 1, :], s_(1), pair_w[0:B, 0, :], ALU.mult))
            step.mark(nc.vector.tensor_scalar(pair_row[0:B, 0, :], node[0:B, :], 1.0, None, ALU.add))
            step(nc.vector.tensor_scalar(pair_row[0:B, 1, :], node[0:B, :], float(N + 1), None, ALU.add))

            def pair_column(j, node_, row_, s):
                nc.vector.tensor_scalar(p_lo[0:B, s, 0, :], iota[0:B, 0:128], pair_lo[0:B, ds(j, 1)], node_, ALU.is_equal, ALU.mult)
                nc.vector.tensor_scalar(p_lo[0:B, s, 1, :], iota[0:B, 0:128], pair_lo[0:B, ds(j, 1)], row_, ALU.is_equal, ALU.mult)
                nc.vector.tensor_scalar(p_hi[0:B, s, :], iota[0:B, 0:SLOTS], pair_hi[0:B, ds(j, 1)], None,
                                        ALU.is_equal).then_inc(pairs_made, 1)

            for k in range(2):
                rowk = pair_row[0:B, k, :]
                if k:
                    dve.wait_ge(pairs_used, NT)
                pair_column(k * NT, node[0:B, 0:1], rowk[:, 0:1], 0)
                with dve.Fori(0, (NT - 1) // SR) as i:
                    dve.wait_ge(pairs_used, i * SR + (k * NT + 1))
                    for s in range(SR):
                        pair_column(i * SR + (k * NT + 1 + s), node[0:B, ds(i * SR + (1 + s), 1)], rowk[:, ds(i * SR + (1 + s), 1)], s)
            dve.wait_ge(pairs_used, PAIRS)
            step.mark(nc.vector.tensor_copy(s_tok[:, :], bank[0][:, 0:SLOTS]))
            step(nc.vector.tensor_copy(s_tmp[:, 0, :], bank[1][:, 0:SLOTS]))
            step(nc.vector.tensor_scalar(s_tmp[:, 1, :], s_tmp[:, 0, :], 0.0, None, ALU.is_equal))
            step(nc.vector.tensor_tensor(s_tmp[:, 1, :], s_tmp[:, 1, :], slot_id[:, :], ALU.mult))
            step(nc.vector.scalar_tensor_tensor(s_row[:, :], s_tmp[:, 0, :], -1.0, s_tmp[:, 1, :], ALU.add, ALU.add))
            nc.vector.memset(slot[0:1, 191:192], 0.0).then_inc(slots_ready, 1)
            dve.wait_ge(ld_moe, 32 * NE)
            dve.wait_ge(ld_b2, 16)

            def expert_weights(off):
                nc.vector.tensor_copy(w1c[:, :, :].rearrange("p k n -> p (k n)"), slab[:, ds(off, 1024)]).then_inc(w_copied, 1)

            def expert_turn(i):
                _, woff = nc.values_load_multi_w_load_instructions(
                    ex_w[0:1, ds(i * RING, RING)], engines=[DVE_], min_val=0, max_val=(NE - 1) * 2048,
                    skip_runtime_bounds_check_because="the router clamps it")
                _, boff = nc.values_load_multi_w_load_instructions(
                    ex_b2[0:1, ds(i * RING, RING)], engines=[DVE_], min_val=0, max_val=(NE - 1) * C,
                    skip_runtime_bounds_check_because="the router clamps it")
                for k in range(RING):
                    await_ge(dve, h_mm, i * RING + k)
                    expert_weights(woff[k])
                    dve.wait_ge(x_mm, i * RING + (k + 1))
                    nc.vector.tensor_copy(tT[:, k % 2, :, :].rearrange("p k n -> p (k n)"), bank[k % 2][:, 0:C]).then_inc(x_out, 1)
                    dve.wait_ge(y_mm, i * RING + (k + 1))
                    if k >= 2:
                        dve.wait_ge(y_put[k - 2], i * 16 + 16)
                    else:
                        await_ge(dve, y_put[k + RING - 2], i * 16)
                    nc.vector.tensor_tensor(yv[:, k % 2, :], bank[4 + k % 2][:, 0:C],
                                            b2b[:, :, :].rearrange("p e c -> p (e c)")[:, ds(boff[k], C)], ALU.add).then_inc(y_out, 1)

            turns_of(dve, 0, SLOTS // RING, expert_turn)
            nc.vector.memset(slot[0:1, 191:192], 0.0).then_inc(y_used, GT)
            for i in range(NT // GT):
                for j in range(GT):
                    dve.wait_ge(y_ld[j], i * 32 + 32)
                    dve.wait_ge(fz, i * GT + (j + 1))
                    step(nc.vector.scalar_tensor_tensor(zb[0:B, j, :], yb[0:B, 0, j, :], pair_w[0:B, 0, ds(i * GT + j, 1)], zb[0:B, j, :],
                                                        ALU.mult, ALU.add))
                    nc.vector.scalar_tensor_tensor(zb[0:B, j, :], yb[0:B, 1, j, :], pair_w[0:B, 1, ds(i * GT + j, 1)], zb[0:B, j, :],
                                                   ALU.mult, ALU.add).then_inc(y_used, 1)
                    dve.wait_ge(y_used, i * GT + (GT + j + 1))
                    step(nc.vector.bn_stats(bn6[0:B, :], zb[0:B, j, :]))
                    step(nc.vector.bn_aggr(mv5[0:B, j, :], bn6[0:B, :]))
                nc.vector.tensor_scalar(st5[0:B, 0, :], mv5[0:B, :, 1], LN_EPS, None, ALU.add).then_inc(fin_var, 1)
                dve.wait_ge(fin_root, i + 1)
                norm_scale(step, fin_scale)
                for j in range(GT):
                    dve.wait_ge(fin_aff, i * GT + (j + 1))
                    await_ge(dve, out_put[j], i * 16)
                    nc.vector.tensor_tensor(ob[0:B, j, :], ub[0:B, j, :], X[0:B, ds(i * GT + j, 1), :].rearrange("p a c -> p (a c)"),
                                            ALU.add).then_inc(fin_out, 1)

        def rank_products(pe, rounds, P, nb):
            pe.wait_ge(rank_rows, rounds)
            mine = small[0:P, 1, 0:nb]
            nc.tensor.matmul(bank[6][0:P, 0:nb], tri[0:P, 0:P], mine, start=True, stop=True)
            nc.tensor.matmul(bank[6][0:P, 32:32 + nb], ones[0:P, 0:P], mine, start=True, stop=True).then_inc(rank_sums, 1)

        def clear_banks(which, cols):
            for b in which:
                ins = nc.tensor.matmul(bank[b][:, 0:cols], zeros[:, 0:128], zeros[:, 0:cols], start=True, stop=True)
            return ins

        def sort_product(pe, n, s, H):
            pe.wait_ge(hots_made, n)
            for b in range(2):
                ins = nc.tensor.matmul(bank[b][:, 0:H], s_lo[:, s, b, :], s_hi[:, s, 0:H], start=False, stop=True,
                                       skip_group_check=True)
            ins.then_inc(hots_used, 1)

        def attention_fold_pe(pe):
            pe.wait_ge(kvT_ready, 1)
            for j in range(KC):
                ins = nc.tensor.matmul(bank[4][:, j * C:(j + 1) * C], kvT[:, j, :], mw1[:, j, :], start=True, stop=True)
            ins.then_inc(kvw1_mm, 1)
            pe.wait_ge(kvw1_out, 1)
            for m in range(KC):
                for j in range(KC):
                    nc.tensor.matmul(bank[5][:, m * C:(m + 1) * C], wqT[:, j, m * 128:(m + 1) * 128], kvw1[:, j, :],
                                     start=(j == 0), stop=(j == KC - 1))
            for m in range(KC):
                for j in range(KC):
                    ins = nc.tensor.matmul(bank[6][:, m:m + 1], kvw1[:, j, m * 128:(m + 1) * 128], bcol[:, 64 + j:65 + j],
                                           start=(j == 0), stop=(j == KC - 1))
            ins.then_inc(weff_mm, 1)
            pe.wait_ge(weff_out, 1)

        @block.tensor
        def _(pe):
            pe.wait_ge(consts, 1)
            clear_banks((0, 1), HMAX).then_inc(hots_used, SR)
            nc.tensor.matmul(bank[7][0:1, 1:2], zeros[:, 0:1], zeros[:, 0:1], start=True, stop=True).then_inc(chunk_done, RING)
            rank_products(pe, 1, 128, NT)
            T = T_OF[0]
            with pe.Fori(0, (T - 3) // SR) as i:
                for s in range(SR):
                    sort_product(pe, i * SR + s + 1, s, H_OF[0])
            for j in range((T - 3) // SR * SR, T):
                sort_product(pe, j + 1, j % SR, H_OF[0])
            nc.tensor.matmul(bank[7][0:1, 0:1], zeros[:, 0:1], zeros[:, 0:1], start=True, stop=True).then_inc(sorted_, 1)
            pe.wait_ge(xn_ready, 1)
            for t in range(NT):
                if t >= 2:
                    pe.wait_ge(xn_t_out, t - 1)
                for k in range(KC):
                    ins = nc.tensor.transpose(bank[4 + t % 2][:, k * B:(k + 1) * B], xn[0:B, t, k * 128:(k + 1) * 128],
                                              ident[0:B, 0:B])
                ins.then_inc(xn_t, 1)
            pe.wait_ge(ld_w, 16 * W_LOADS)
            pe.wait_ge(xn_t_out, NT)
            for t in range(NT):
                if t >= 2:
                    pe.wait_ge(tab_out, t - 1)
                for k in range(KC):
                    ins = nc.tensor.matmul(bank[2 + t % 2][0:B, 0:C], xnT[:, k, t * B:(t + 1) * B], wgnn[:, k, :],
                                           start=(k == 0), stop=(k == KC - 1))
                ins.then_inc(tab_mm, 1)
            pe.wait_ge(ld_b, 16 * B_LOADS)
            pe.wait_ge(wcen_ready, 1)
            for j in range(KC):
                for k in range(KC):
                    nc.tensor.transpose(bank[5][:, j * C + k * 128:j * C + (k + 1) * 128], weff[:, k, j * 128:(j + 1) * 128],
                                        ident[:, :])
            nc.tensor.transpose(bank[4][:, 0:68], brow[0:68, :], ident[0:68, 0:68]).then_inc(setup_t, 1)
            rank_products(pe, 2, 128, NT)
            rank_products(pe, 3, 128, NT)
            pe.wait_ge(group_ready, 1)
            clear_banks((0, 1), HMAX)
            pe.wait_ge(hots_made, T_OF[0])
            pe.wait_ge(setup_t_out, 1)
            pe.wait_ge(hots_made, T_OF[0] + 1)
            clear_banks((6, 7), 128)
            for g, turns, turn0, nsort, mix, tile0 in SEGS:
                c0 = CHUNK0[g] + RING * turn0
                if g and turn0 == 0:
                    pe.wait_ge(group_ready, g + 1)
                    if g == 1:
                        clear_banks((0, 1), HMAX)
                if g == 2 and turn0 == 0:
                    attention_fold_pe(pe)
                col0 = AT[g + 1] + nsort * turn0 if nsort else 0
                split = shares(nsort, RING)
                def turn(i):
                    m = 0
                    for k in range(RING):
                        pe.wait_ge(hot_ready, i * RING + (c0 + k + 1))
                        pe.wait_ge(gathered[k], i * 16 + (c0 // RING + 1) * 16)
                        if k % 2 == 0:
                            pe.wait_ge(chunk_added, i * RING + (c0 + k + 2))
                        nc.tensor.matmul(bank[2 + k // 2 % 2][:, k % 2 * C:(k % 2 + 1) * C], hot[:, k, :], rows[:, k, :],
                                         start=True, stop=True).then_inc(chunk_done, 1)
                        for _ in range(split[k]):
                            sort_product(pe, i * nsort + (col0 + m + 1), m % SR, H_OF[g + 1])
                            m += 1
                        if mix == 1 and k == 0:
                            await_ge(pe, kv_sb, i + tile0)
                            pe.wait_ge(xst_ready, i + (tile0 + 1))
                            for kc in range(KC):
                                wkv = wcen[:, kc, :].rearrange("p (h c) -> p h c", h=HEADS)[:, :, HD:3 * HD]
                                ins = nc.tensor.matmul(bank[4][0:B, :], xst[:, kc, :],
                                                       wkv, start=(kc == 0), stop=(kc == KC - 1))
                            ins.then_inc(kv_mm, 1)
                        if mix == 1 and k == 7:
                            pe.wait_ge(kv_norm, i + (tile0 + 1))
                            for j in range(KC):
                                ins = nc.tensor.matmul(bank[6 + j][:, 0:128], kvn[0:B, 1, 4 * j:4 * j + 4, :].rearrange("p h d -> p (h d)"),
                                                       kvn[0:B, 0, 4 * j:4 * j + 4, :].rearrange("p h d -> p (h d)"),
                                                       start=False, stop=True, skip_group_check=True)
                            ins.then_inc(kv_used, 1)
                        if mix == 2 and k == 0:
                            await_ge(pe, mh_out, i + tile0)
                            for m2 in range(KC):
                                for kc in range(KC):
                                    ins = nc.tensor.matmul(bank[4][:, m2 * B:(m2 + 1) * B], weff[:, kc, m2 * 128:(m2 + 1) * 128],
                                                           xnT[:, kc, ds((i + tile0) * B, B)], start=(kc == 0), stop=(kc == KC - 1))
                            ins.then_inc(mh_mm, 1)
                        if mix == 2 and k == 4:
                            pe.wait_ge(mh_out, i + (tile0 + 1))
                            await_ge(pe, my_out, i + tile0)
                            for kc in range(KC):
                                ins = nc.tensor.matmul(bank[5][0:B, 0:C], mhT[:, kc, :], mw2[:, kc, :],
                                                       start=(kc == 0), stop=(kc == KC - 1))
                            ins.then_inc(my_mm, 1)
                if turns == 1:
                    turn(0)
                else:
                    with pe.Fori(0, turns) as i:
                        turn(i)
                if nsort and turn0 + turns == TURNS[g]:
                    nc.tensor.matmul(bank[7][0:1, 128:129], zeros[:, 0:1], zeros[:, 0:1], start=False, stop=True,
                                     skip_group_check=True).then_inc(sorted_, 1)
            def mid_transpose(i, j):
                pe.wait_ge(mid_norm, i * GT + (j + 1))
                await_ge(pe, mt_out, i * GT + max(j - 1, 0))
                for k in range(KC):
                    ins = nc.tensor.transpose(bank[4 + j % 2][:, k * B:(k + 1) * B], rows[0:B, j, k * 128:(k + 1) * 128], ident[0:B, 0:B])
                ins.then_inc(mt_mm, 1)

            def middle_turn(i):
                mid_transpose(i, 0)
                for j in range(GT):
                    if j + 1 < GT:
                        mid_transpose(i, j + 1)
                    pe.wait_ge(mt_out, i * GT + (j + 1))
                    await_ge(pe, mg_out, i * GT + max(j - 1, 0))
                    for k in range(KC):
                        ins = nc.tensor.matmul(bank[6 + j % 2][0:B, 0:NE], tT[:, j % 2, k, 0:B], gate[:, k, :],
                                               start=(k == 0), stop=(k == KC - 1))
                    ins.then_inc(mg_mm, 1)

            turns_of(pe, 0, NT // GT, middle_turn)
            pe.wait_ge(mg_out, NT)
            rank_products(pe, 4, B, NE)

            def pair_product(n, s, first):
                pe.wait_ge(pairs_made, n)
                for b in range(2):
                    ins = nc.tensor.matmul(bank[b][:, 0:SLOTS], p_lo[0:B, s, b, :], p_hi[0:B, s, :], start=first, stop=True,
                                           skip_group_check=True)
                ins.then_inc(pairs_used, 1)

            for k in range(2):
                pair_product(k * NT + 1, 0, k == 0)
                with pe.Fori(0, (NT - 1) // SR) as i:
                    for s in range(SR):
                        pair_product(i * SR + (k * NT + 2 + s), s, False)
            pe.wait_ge(slots_ready, 1)

            def tokens_transposed(i, k):
                pe.wait_ge(tok_got[k], i * 16 + 16)
                await_ge(pe, x_out, i * RING + max(k - 1, 0))
                for c in range(KC):
                    ins = nc.tensor.transpose(bank[k % 2][:, c * 128:(c + 1) * 128], rows[:, k, c * 128:(c + 1) * 128], ident[:, :])
                ins.then_inc(x_mm, 1)

            def expert_turn(i, last):
                _, woff = nc.values_load_multi_w_load_instructions(
                    ex_w[0:1, ds(i * RING, RING)], engines=[PE_], min_val=0, max_val=(NE - 1) * 2048,
                    skip_runtime_bounds_check_because="the router clamps it")
                for k in range(RING):
                    pe.wait_ge(w_copied, i * RING + (k + 1))
                    pe.wait_ge(x_out, i * RING + (k + 1))
                    await_ge(pe, h_out, i * RING + max(k - 1, 0))
                    for m in range(KF):
                        for c in range(KC):
                            ins = nc.tensor.matmul(bank[2 + k % 2][:, m * 128:(m + 1) * 128], w1c[:, c, m * 128:(m + 1) * 128],
                                                   tT[:, k % 2, c, :], start=(c == 0), stop=(c == KC - 1))
                    ins.then_inc(h_mm, 1)
                    if k + 1 < RING:
                        tokens_transposed(i, k + 1)
                    elif not last:
                        tokens_transposed(i + 1, 0)
                    pe.wait_ge(h_out, i * RING + (k + 1))
                    await_ge(pe, y_out, i * RING + max(k - 1, 0))
                    for m in range(KF):
                        ins = nc.tensor.matmul(bank[4 + k % 2][:, 0:C], hT[:, k % 2, m, :], slab[:, ds(woff[k] + (1024 + m * C), C)],
                                               start=(m == 0), stop=(m == KF - 1))
                    ins.then_inc(y_mm, 1)

            tokens_transposed(0, 0)
            turns_of(pe, 0, SLOTS // RING, lambda i: expert_turn(i, False), lambda i: expert_turn(i, True))


_INS = ["x", "src", "dst", "edge_weight", "L0_gnn_weight_mat", "L0_gnn_bias_vec", "L0_mix_w_qkv", "L0_mix_b_qkv",
        "L0_mix_kln_g", "L0_mix_kln_b", "L0_mix_vln_g", "L0_mix_vln_b", "L0_mix_w1", "L0_mix_b1", "L0_mix_w2",
        "L0_mix_b2", "L0_ffn_gate_w", "L0_ffn_gate_b", "L0_ffn_w1", "L0_ffn_b1", "L0_ffn_w2", "L0_ffn_b2",
        "L0_ffn_gamma", "L0_ffn_beta"]


def kernel(**inputs):
    import numpy as np
    import concourse.bacc as bacc
    from concourse import mybir
    from concourse.bass_utils import run_bass_kernel_spmd

    nc = bacc.Bacc("TRN2", target_bir_lowering=False, num_devices=1)
    arrays, args = {}, []
    for name in _INS:
        a = np.ascontiguousarray(inputs[name])
        arrays[f"in_{name}"] = a
        args.append(nc.dram_tensor(f"in_{name}", a.shape, mybir.dt.from_np(a.dtype), kind="ExternalInput").ap())
    out = nc.dram_tensor("out", arrays["in_x"].shape, mybir.dt.float32, kind="ExternalOutput").ap()
    graph_transformer_layer(nc, *args, out)
    r = run_bass_kernel_spmd(nc, [arrays], core_ids=[0])
    return r.results[0]["out"]
```

```python
from contextlib import ExitStack, contextmanager


class Steps:

    def __init__(self, engine, semaphore):
        self.engine, self.semaphore, self.done, self.turn = engine, semaphore, 0, None

    def mark(self, instruction):
        instruction.then_inc(self.semaphore, 1)
        self.done += 1

    def wait(self):
        self.engine.wait_ge(self.semaphore, self.done if self.turn is None else self.turn + self.done)

    def __call__(self, instruction):
        self.mark(instruction)
        self.wait()

    @contextmanager
    def loop(self, turns, marks):
        start = self.done
        with self.engine.Fori(0, turns) as i:
            self.turn = i * marks
            yield i
            assert self.done - start == marks, self.done - start
        self.turn, self.done = None, start + turns * marks


def await_ge(engine, semaphore, value):
    if not isinstance(value, int) or value > 0:
        engine.wait_ge(semaphore, value)


def turns_of(engine, first, count, body, last=None):
    if first == 0:
        body(0)
        first = 1
    end = count - (last is not None)
    if end > first:
        with engine.Fori(first, end) as i:
            body(i)
    if last is not None:
        last(count - 1)


def shares(n, parts):
    return [(n * (k + 1)) // parts - (n * k) // parts for k in range(parts)]


def graph_transformer_layer(nc, x, src, dst, edge_weight, gnn_w, gnn_b, w_qkv, b_qkv, kln_g, kln_b, vln_g, vln_b,
                            mix_w1, mix_b1, mix_w2, mix_b2, gate_w, gate_b, w1, b1, w2, b2, gamma, beta, out):
    import concourse.bass as bass
    from concourse import mybir

    F32, I32, U32 = mybir.dt.float32, mybir.dt.int32, mybir.dt.uint32
    ALU, ACT, AX = mybir.AluOpType, mybir.ActivationFunctionType, mybir.AxisListType
    PE_, DVE_, ACT_ = mybir.EngineType.PE, mybir.EngineType.DVE, mybir.EngineType.Activation
    ds = bass.ds

    N, C = x.shape
    E = src.shape[0]
    NE, _, F = w1.shape
    B, NT = 125, N // 125
    KC, KF = C // 128, F // 128
    HEADS, HD = 8, 32
    assert N == B * NT and NT * 4195 < 2 ** 24
    COLS = -(-E // 128)
    FULL = E // 128
    EPS, LN_EPS, MAXNORM = 1e-15, 1e-5, 1.0 - 1e-5

    RING = 8
    T_OF = [63, 160, 168]
    assert sum(T_OF) == COLS
    AT = [0, T_OF[0], T_OF[0] + T_OF[1]]
    H_OF = [-(-(t + NT - 1) // RING) * RING for t in T_OF]
    TURNS = [h // RING for h in H_OF]
    HMAX = max(H_OF)
    CHUNK0 = [0, H_OF[0], H_OF[0] + H_OF[1]]
    CHUNKS = sum(H_OF)
    SORT_TURNS = [10, 21]
    SORT = [T_OF[1] // SORT_TURNS[0], T_OF[2] // SORT_TURNS[1]]
    assert SORT[0] * SORT_TURNS[0] == T_OF[1] and SORT[1] * SORT_TURNS[1] == T_OF[2]
    P1 = NT - TURNS[0]
    P2 = TURNS[1] - SORT_TURNS[1]
    SEGS = [(0, 1, 0, SORT[0], 1, 0),
            (0, SORT_TURNS[0] - 1, 1, SORT[0], 1, 1),
            (0, TURNS[0] - SORT_TURNS[0], SORT_TURNS[0], 0, 1, SORT_TURNS[0]),
            (1, 1, 0, SORT[1], 1, TURNS[0]),
            (1, P1 - 1, 1, SORT[1], 1, TURNS[0] + 1),
            (1, SORT_TURNS[1] - P1, P1, SORT[1], 0, 0),
            (1, 1, SORT_TURNS[1], 0, 2, 0),
            (1, P2 - 1, SORT_TURNS[1] + 1, 0, 2, 1),
            (2, NT - P2, 0, 0, 2, P2),
            (2, TURNS[2] - (NT - P2), NT - P2, 0, 0, 0)]
    assert TURNS[2] - (NT - P2) == 1
    CHUNK_BANKS = [2, 3, 5, 7]
    GT = 5
    assert NT % GT == 0
    SR = 8
    LAG = 4
    assert all(n % SR == 0 for n in SORT)

    PAIRS = 2 * NT
    SLOTS = (2 * N + NE * 127) // 128
    assert SLOTS % RING == 0 and SLOTS == 64
    PR = 4
    YROWS = 2 * N + 128 * SLOTS

    table = nc.dram_tensor("table", (N, C), F32).ap()
    tokens = nc.dram_tensor("tokens", (N, C), F32).ap()
    pair_out = nc.dram_tensor("pair_out", (YROWS, C), F32).ap()

    ctx = ExitStack()
    with ctx:
        def sb(name, shape, dt=F32):
            return ctx.enter_context(nc.sbuf_tensor(name, shape, dt))

        def sem(name):
            return ctx.enter_context(nc.semaphore(name))

        slab = sb("slab", [128, NE * 2048])
        used = [0]

        def part(of, shape, count=used, base=slab):
            n = 1
            for d in shape:
                n *= d
            a = base[:, count[0]:count[0] + n]
            count[0] += n
            assert count[0] <= base.shape[1]
            names = "abc"[:len(shape)]
            return a if len(shape) == 1 else a.rearrange(
                f"p ({' '.join(names)}) -> p {' '.join(names)}", **dict(zip(names[:-1], shape)))

        xnT = part("xnT", [KC, N])
        work = part("work", [2 * HMAX * NT])
        rt_one, rt_sum = work[:, 0:HMAX * NT], work[:, HMAX * NT:2 * HMAX * NT]
        xn = work[:, 0:NT * C].rearrange("p (t c) -> p t c", t=NT)
        wqkv = part("wqkv", [KC, 3 * C])
        wcen = part("wcen", [KC, 3 * C])
        wgnn = part("wgnn", [KC, C])
        mw1 = part("mw1", [KC, C])
        mw2 = part("mw2", [KC, C])
        weff = part("weff", [KC, C])
        wqT = part("wqT", [KC, C])
        looped = [0]
        kvw1 = part("kvw1", [KC, C], looped, work)
        kvT = part("kvT", [KC, 128], looped, work)
        kvsum = part("kvsum", [KC, 128], looped, work)
        kvc = part("kvc", [HEADS, 2, HD], looped, work)
        kvs = part("kvs", [HEADS, 2, HD], looped, work)
        xst = part("xst", [KC, B], looped, work)
        kvn = part("kvn", [2, HEADS, HD], looped, work)
        hot = part("hot", [RING, 128], looped, work)
        mhT = part("mhT", [KC, B], looped, work)
        s_one = part("s_one", [SR, 128])
        s_lo = part("s_lo", [SR, 2, 128])
        s_hi = part("s_hi", [SR, HMAX])
        tout = part("tout", [2, C])
        bias_kv = part("bias_kv", [HEADS, 3 * HD])
        ln_g = part("ln_g", [2, HD])
        ln_b = part("ln_b", [2, HD])
        mb2 = part("mb2", [C])
        ew, pack, lo = part("ew", [COLS]), part("pack", [COLS]), part("lo", [COLS])
        key = hi = part("hi", [COLS])
        zeros = part("zeros", [264])
        brow = part("brow", [128])
        g_row = part("g_row", [CHUNKS]).bitcast(I32)
        g_lo, g_w = part("g_lo", [CHUNKS]), part("g_w", [CHUNKS])

        X = sb("X", [128, NT, C])
        acc = sb("acc", [128, NT, C])
        accf = acc[:, :, :].rearrange("p t c -> p (t c)")
        later = [0]
        b2b = part("b2b", [NE, C], later, accf)
        w1c = part("w1c", [KC, F], later, accf)
        hT = part("hT", [2, KF, 128], later, accf)
        p_lo = hT[:, :, :, :].rearrange("p a k n -> p (a k n)").rearrange("p (r a n) -> p r a n", r=PR, a=2)
        final = [0]
        yb = part("yb", [2, GT, C], final)
        zb = part("zb", [GT, C], final)
        ub = part("ub", [GT, C], final)
        ob = part("ob", [GT, C], final)
        gam, bet = part("gam", [C], final), part("bet", [C], final)

        rows = sb("rows", [128, RING, C])
        early = rows[:, :, :].rearrange("p k c -> p (k c)").bitcast(I32)
        esrc, edst, eq = (early[:, j * COLS:(j + 1) * COLS] for j in range(3))
        slot = sb("slot", [128, 192])
        slot_i = sb("slot_i", [128, HMAX], I32)
        slot_j = sb("slot_j", [128, HMAX], I32)
        small = sb("small", [128, 6, 32])
        cnt_i = sb("cnt_i", [128, 32], I32)
        bk_f = sb("bk_f", [1, HMAX])
        bk = sb("bk", [1, CHUNKS], I32)
        idx = sb("idx", [128, RING], I32)
        iota = sb("iota", [128, HMAX])
        slot_id = sb("slot_id", [128, SLOTS])
        tT = sb("tT", [128, 2, KC, 128])
        yv = sb("yv", [128, 2, C])
        p_hi = yv[:, :, :].rearrange("p a c -> p (a c)")[:, 0:PR * SLOTS].rearrange("p (r n) -> p r n", r=PR)
        odx = sb("odx", [128, RING], I32)
        pair_key = sb("pair_key", [128, 2, NT])
        pair_lo = sb("pair_lo", [128, PAIRS])
        pair_hi = sb("pair_hi", [128, PAIRS])
        pair_row = sb("pair_row", [128, 2, NT])
        s_tok = sb("s_tok", [128, SLOTS], I32)
        s_row = sb("s_row", [128, SLOTS], I32)
        s_tmp = sb("s_tmp", [128, 2, SLOTS])
        ex_w = sb("ex_w", [1, SLOTS], I32)
        ex_b1 = sb("ex_b1", [1, SLOTS], I32)
        ex_b2 = sb("ex_b2", [1, SLOTS], I32)
        lg = sb("lg", [128, 2, NE])
        mx5 = sb("mx5", [128, GT, 8])
        ix5 = sb("ix5", [128, GT, 8], U32)
        topv = sb("topv", [128, 2, NT])
        pair_w = sb("pair_w", [128, 2, NT])
        mv5 = sb("mv5", [128, GT, 2])
        st5 = sb("st5", [128, 6, GT])
        mid_rs = sb("mid_rs", [128, NT])
        mid_nb = sb("mid_nb", [128, NT])
        tri = sb("tri", [128, 128])
        ident = sb("ident", [128, 128])
        ones = sb("ones", [128, 128])
        node = sb("node", [128, NT])
        gb = sb("gb", [128, C])
        gate = sb("gate", [128, KC, NE])
        gateb = sb("gateb", [128, NE])
        bcol = sb("bcol", [128, 70])
        beff = sb("beff", [128, KC])
        kvst = sb("kvst", [128, 4, 16])
        bn6 = sb("bn6", [128, 6])
        mv = sb("mv", [128, NT, 2])
        st = sb("st", [128, 16, NT + 1])
        wmean = sb("wmean", [128, KC, 3 * HEADS])

        bank = [ctx.enter_context(nc.psum_tensor(f"bank{i}", [128, 512], F32)) for i in range(8)]

        pads, ld_edge, ld_x, ld_w, ld_b = sem("pads"), sem("ld_edge"), sem("ld_x"), sem("ld_w"), sem("ld_b")
        consts = sem("consts")
        dve_step, act_step, pool_step = sem("dve_step"), sem("act_step"), sem("pool_step")
        rank_rows, rank_sums = sem("rank_rows"), sem("rank_sums")
        hots_made, loads_made, hots_used, sorted_ = sem("hots_made"), sem("loads_made"), sem("hots_used"), sem("sorted_")
        psum_zeroed = sem("psum_zeroed")
        var_ready, sqrt_done, squares = sem("var_ready"), sem("sqrt_done"), sem("squares")
        xn_ready, ln_arg, ln_done, row_scale = sem("xn_ready"), sem("ln_arg"), sem("ln_done"), sem("row_scale")
        xn_t, xn_t_out, tab_mm, tab_out, tab_stored = (sem("xn_t"), sem("xn_t_out"), sem("tab_mm"), sem("tab_out"),
                                                       [sem("tab_stored0"), sem("tab_stored1")])
        wcen_ready, setup_t, setup_t_out = sem("wcen_ready"), sem("setup_t"), sem("setup_t_out")
        x_plus = sem("x_plus")
        group_ready, routed = sem("group_ready"), sem("routed")
        may_go = sem("may_go")
        idx_ready = sem("idx_ready")
        gathered = [sem(f"gathered{k}") for k in range(RING)]
        hot_ready, chunk_done, chunk_added = sem("hot_ready"), sem("chunk_done"), sem("chunk_added")
        kv_mm, kv_sb, kv_sq, kv_norm, kv_used = sem("kv_mm"), sem("kv_sb"), sem("kv_sq"), sem("kv_norm"), sem("kv_used")
        xst_ready = sem("xst_ready")
        kv_var, kv_std = sem("kv_var"), sem("kv_std")
        kv_sums, kv_sums_row = sem("kv_sums"), sem("kv_sums_row")
        kvT_ready, kvw1_mm, kvw1_out, weff_mm, weff_out = (sem("kvT_ready"), sem("kvw1_mm"), sem("kvw1_out"),
                                                           sem("weff_mm"), sem("weff_out"))
        mh_mm, mh_out, my_mm, my_out = sem("mh_mm"), sem("mh_out"), sem("my_mm"), sem("my_out")

        tail_ss, tail_sq, tail_tanh, tail_v = sem("tail_ss"), sem("tail_sq"), sem("tail_tanh"), sem("tail_v")
        mid_var, mid_root, mid_scale, mid_norm = sem("mid_var"), sem("mid_root"), sem("mid_scale"), sem("mid_norm")
        tok_stored, mt_mm, mt_out, mg_mm, mg_out = sem("tok_stored"), sem("mt_mm"), sem("mt_out"), sem("mg_mm"), sem("mg_out")
        acc_free, ld_gb, ld_moe, ld_b2 = sem("acc_free"), sem("ld_gb"), sem("ld_moe"), sem("ld_b2")
        exp_arg, exp_done = sem("exp_arg"), sem("exp_done")
        pairs_made, pairs_used, slots_ready = sem("pairs_made"), sem("pairs_used"), sem("slots_ready")
        tok_idx, out_idx = sem("tok_idx"), sem("out_idx")
        tok_got = [sem(f"tok_got{k}") for k in range(RING)]
        y_put = [sem(f"y_put{k}") for k in range(RING)]
        x_mm, x_out, w_copied, h_mm, h_out, y_mm, y_out = (sem("x_mm"), sem("x_out"), sem("w_copied"), sem("h_mm"),
                                                           sem("h_out"), sem("y_mm"), sem("y_out"))
        y_ld = [sem(f"y_ld{j}") for j in range(GT)]
        y_used, fz, fz_sum, fin_var, fin_root, fin_scale, fin_norm, fin_aff, fin_out = (
            sem("y_used"), sem("fz"), sem("fz_sum"), sem("fin_var"), sem("fin_root"), sem("fin_scale"), sem("fin_norm"),
            sem("fin_aff"), sem("fin_out"))
        out_put = [sem(f"out_put{j}") for j in range(GT)]

        block = ctx.enter_context(nc.Block())

        x_t = x.rearrange("(t p) c -> p t c", p=B)
        out_t = out.rearrange("(t p) c -> p t c", p=B)
        table_t = table.rearrange("(t p) c -> p t c", p=B)

        def edge_whole(a):
            return a[0:128 * FULL].rearrange("(p j) -> p j", j=FULL)

        def edge_rest(a):
            return a[128 * FULL:E].rearrange("(p j) -> p j", j=1)

        def row(v):
            return v.rearrange("(a n) -> a n", a=1)

        W_LOADS, B_LOADS = 5, 14
        @block.sync
        def _(sp):
            sp.wait_ge(pads, 3)
            for a, t in ((src, esrc), (dst, edst), (edge_weight, ew)):
                sp.dma_start(t[:, 0:FULL], edge_whole(a)).then_inc(ld_edge, 16)
                with nc.allow_non_contiguous_dma(reason="the last few edges, one a partition"):
                    sp.dma_start(t[0:E - 128 * FULL, FULL:FULL + 1], edge_rest(a)).then_inc(ld_edge, 16)
            sp.dma_start(X[0:112, :, :], x_t[0:112]).then_inc(ld_x, 16)
            sp.dma_start(X[112:B, :, :], x_t[112:B]).then_inc(ld_x, 16)
            for t, a in ((wgnn, gnn_w), (wqkv, w_qkv), (mw1, mix_w1), (mw2, mix_w2), (gate, gate_w)):
                sp.dma_start(t[:, :, :], a.rearrange("(k p) n -> p k n", p=128)).then_inc(ld_w, 16)
            for q in range(NT):
                sp.wait_ge(tab_out, q + 1)
                sp.dma_start(table_t[:, q, :], tout[0:B, q % 2, :]).then_inc(tab_stored[q % 2], 16)

            sp.wait_ge(chunk_done, RING + CHUNKS)
            sp.wait_ge(my_out, NT)
            for e in range(NE):
                half = slab[:, e * 2048:(e + 1) * 2048]
                sp.dma_start(half[:, 0:1024].rearrange("p (k n) -> p k n", k=KC),
                             w1[e].rearrange("(k p) n -> p k n", p=128)).then_inc(ld_moe, 16)
                sp.dma_start(half[:, 1024:2048].rearrange("p (k n) -> p k n", k=KF),
                             w2[e].rearrange("(k p) n -> p k n", p=128)).then_inc(ld_moe, 16)
            with sp.Fori(0, NT // GT) as i:
                sp.wait_ge(mid_norm, i * GT + GT)
                sp.dma_start(tokens.rearrange("(t p) c -> p t c", p=B)[:, ds(i * GT, GT), :], rows[0:B, 0:GT, :]).then_inc(tok_stored, 16)
            sp.wait_ge(acc_free, 1)
            sp.dma_start(b2b[:, :, :].rearrange("p e c -> p (e c)"), b2.rearrange("(a e) c -> a (e c)", a=1).to_broadcast([128, NE * C])).then_inc(ld_b2, 16)
            for k in range(RING):
                sp.wait_ge(y_put[k], 16 * SLOTS // RING)
            sp.wait_ge(y_out, SLOTS)
            for t, a in ((gam, gamma), (bet, beta)):
                sp.dma_start(t[:, :], row(a).to_broadcast([128, C])).then_inc(ld_gb, 16)
            y_t = pair_out[0:2 * N, :].rearrange("(k t p) c -> k p t c", k=2, p=B)

            def load_results(i, j):
                for k in range(2):
                    sp.wait_ge(y_used, i * GT + (j + 1))
                    sp.dma_start(yb[0:B, k, j, :], y_t[k, :, ds(i * GT + j, 1), :].rearrange("p a c -> p (a c)")).then_inc(y_ld[j], 16)

            def store_tile(i, j):
                sp.wait_ge(fin_out, i * GT + (j + 1))
                sp.dma_start(out_t[:, ds(i * GT + j, 1), :].rearrange("p a c -> p (a c)"), ob[0:B, j, :]).then_inc(out_put[j], 16)

            for j in range(GT):
                load_results(0, j)
            with sp.Fori(0, NT // GT - 1) as i:
                for j in range(GT):
                    load_results(i + 1, j)
                for j in range(GT):
                    store_tile(i, j)
            for j in range(GT):
                store_tile(NT // GT - 1, j)
            for j in range(GT):
                sp.wait_ge(out_put[j], 16 * (NT // GT))

        def attention_fold_act(act):
            act.wait_ge(kvw1_mm, 1)
            nc.scalar.activation(kvw1[:, :, :].rearrange("p k n -> p (k n)"), bank[4][:, :], ACT.Copy).then_inc(kvw1_out, 1)

        def sort_loads(act, j, n, s):
            act.wait_ge(hots_made, n)
            nc.scalar.activation(s_lo[:, s, 0, :], s_one[:, s, :], ACT.Copy, scale=pack[:, ds(j, 1)])
            nc.scalar.activation(s_lo[:, s, 1, :], s_one[:, s, :], ACT.Copy, scale=ew[:, ds(j, 1)]).then_inc(loads_made, 1)

        @block.scalar
        def _(act):
            step = Steps(act, act_step)
            act.dma_start(bias_kv[:, :, :].rearrange("p h c -> p (h c)"), row(b_qkv).to_broadcast([128, 3 * C])).then_inc(ld_b, 16)
            for t, k, a in ((ln_g, 0, kln_g), (ln_g, 1, vln_g), (ln_b, 0, kln_b), (ln_b, 1, vln_b)):
                act.dma_start(t[:, k, :], row(a).to_broadcast([128, HD])).then_inc(ld_b, 16)
            for t, a in ((mb2, mix_b2), (gb, gnn_b)):
                act.dma_start(t[:, :], row(a).to_broadcast([128, C])).then_inc(ld_b, 16)
            act.dma_start(gateb[:, :], row(gate_b).to_broadcast([128, NE])).then_inc(ld_b, 16)
            act.dma_start(brow[0:NE * KF, :], b1.rearrange("e (m p) -> (e m) p", p=128)).then_inc(ld_b, 16)
            for j in range(2):
                act.dma_start(brow[64 + j:65 + j, :].rearrange("a (h d) -> a h d", d=HD),
                              b_qkv.rearrange("(a h s d) -> a h s d", a=2, s=3, d=HD)[j:j + 1, :, 0, :]).then_inc(ld_b, 16)
            act.dma_start(brow[66:68, :], mix_b1.rearrange("(a d) -> a d", d=128)).then_inc(ld_b, 16)
            for j, a in ((68, vln_g), (69, vln_b)):
                act.dma_start(brow[j:j + 1, :].rearrange("a (h d) -> a h d", d=HD),
                              a.rearrange("(a h d) -> a h d", a=1, h=1).to_broadcast([1, 4, HD])).then_inc(ld_b, 16)

            act.wait_ge(var_ready, 1)
            nc.scalar.activation(st[0:B, 0, 0:NT], st[0:B, 1, 0:NT], ACT.Sqrt).then_inc(sqrt_done, 1)
            act.wait_ge(xn_ready, 1)
            for t in range(NT):
                ins = nc.scalar.activation(tout[0:B, t % 2, :], xn[0:B, t, :], ACT.Square, accum_out=st[0:B, 2, t:t + 1])
                step(ins)
            nc.scalar.activation(st[0:1, 13, 0:1], st[0:1, 2, 0:1], ACT.Copy).then_inc(squares, 1)
            with act.Fori(0, T_OF[0] // SR) as i:
                for s in range(SR):
                    sort_loads(act, i * SR + s, i * SR + (s + 1), s)
            for j in range(T_OF[0] // SR * SR, T_OF[0]):
                sort_loads(act, j, j + 1, j % SR)
            act.wait_ge(var_ready, 2)
            nc.scalar.activation(st[0:B, 0, 0:NT], st[0:B, 1, 0:NT], ACT.Sqrt).then_inc(sqrt_done, 1)
            act.wait_ge(ln_arg, 1)
            nc.scalar.activation(st[0:B, 0, 0:NT], st[0:B, 6, 0:NT], ACT.Ln).then_inc(ln_done, 1)
            for t in range(NT):
                act.wait_ge(xn_t, t + 1)
                nc.scalar.activation(xnT[:, :, t * B:(t + 1) * B], bank[4 + t % 2][:, 0:KC * B].rearrange("p (k n) -> p k n", k=KC),
                                     ACT.Copy).then_inc(xn_t_out, 1)
            act.wait_ge(row_scale, 1)
            act.wait_ge(squares, 1)
            for t in range(NT):
                act.wait_ge(tab_mm, t + 1)
                if t >= 2:
                    act.wait_ge(tab_stored[t % 2], 16 * (t // 2))
                nc.scalar.activation(tout[0:B, t % 2, :], bank[2 + t % 2][0:B, 0:C], ACT.Copy,
                                     scale=st[0:B, 7, t:t + 1]).then_inc(tab_out, 1)
            act.wait_ge(setup_t, 1)
            nc.scalar.activation(wqT[:, :, :].rearrange("p k n -> p (k n)"), bank[5][:, :], ACT.Copy)
            nc.scalar.activation(bcol[:, :], bank[4][:, 0:70], ACT.Copy).then_inc(setup_t_out, 1)

            def row_numbers(c, k):
                nc.scalar.activation(idx[:, k:k + 1], g_row[:, ds(c, 1)], ACT.Copy).then_inc(idx_ready, 1)

            act.wait_ge(group_ready, 1)
            act.wait_ge(routed, 1)
            for k in range(RING):
                row_numbers(k, k)
            for g, turns, turn0, nsort, mix, tile0 in SEGS:
                c0 = CHUNK0[g] + RING * turn0
                col0 = AT[g + 1] + nsort * turn0 if nsort else 0
                split = shares(nsort, RING)
                last = c0 + turns * RING == CHUNKS
                if g < 2 and turn0 == SORT_TURNS[g]:
                    act.wait_ge(group_ready, g + 2)
                    if g == 1:
                        attention_fold_act(act)

                def turn(i):
                    m = 0
                    for k in range(RING):
                        for _ in range(split[k]):
                            sort_loads(act, i * nsort + (col0 + m), i * nsort + (col0 + m + 1), m % SR)
                            m += 1
                        if mix == 1 and k == 0:
                            await_ge(act, kv_mm, i + tile0)
                            nc.scalar.activation(xst[:, :, :], xnT[:, :, ds((i + tile0) * B, B)], ACT.Copy).then_inc(xst_ready, 1)
                        if mix == 1 and k == 5:
                            act.wait_ge(kv_sb, i + (tile0 + 1))
                            await_ge(act, kv_var, i + tile0)
                            nc.scalar.activation(kvs[0:B], kvc[0:B], ACT.Square).then_inc(kv_sq, 1)
                        if mix == 1 and k == 7:
                            act.wait_ge(kv_var, i + (tile0 + 1))
                            nc.scalar.activation(kvst[0:B, 1, :], kvst[0:B, 0, :], ACT.Sqrt).then_inc(kv_std, 1)
                        if mix == 2 and k == 2:
                            act.wait_ge(mh_mm, i + (tile0 + 1))
                            await_ge(act, my_mm, i + tile0)
                            for m2 in range(KC):
                                ins = nc.scalar.activation(mhT[:, m2, :], bank[4][:, m2 * B:(m2 + 1) * B], ACT.Gelu, bias=beff[:, m2:m2 + 1])
                            ins.then_inc(mh_out, 1)
                        if not last:
                            act.wait_ge(chunk_done, i * RING + (RING + c0 + k + 1))
                            row_numbers(i * RING + (c0 + RING + k), k)

                if turns == 1:
                    turn(0)
                else:
                    with act.Fori(0, turns) as i:
                        turn(i)
            act.wait_ge(chunk_added, RING + CHUNKS)
            act.wait_ge(chunk_done, RING + CHUNKS)
            for t in range(NT + 1):
                step(nc.scalar.activation(rows[0:B, 0, :], acc[0:B, t, :] if t < NT else gb[0:B, :], ACT.Square,
                                          accum_out=st[0:B, 2, t:t + 1]))
            nc.scalar.activation(small[0:1, 5, 0:1], small[0:1, 4, 0:1], ACT.Copy).then_inc(tail_ss, 1)
            act.wait_ge(tail_v, 1)
            nc.scalar.activation(st[0:B, 0, :], st[0:B, 1, :], ACT.Sqrt).then_inc(tail_sq, 1)
            act.wait_ge(tail_v, 2)
            nc.scalar.activation(st[0:B, 7, :], st[0:B, 6, :], ACT.Tanh).then_inc(tail_tanh, 1)
            act.wait_ge(tail_v, 3)
            nc.scalar.activation(st[0:B, 0, 0:NT], st[0:B, 1, 0:NT], ACT.Sqrt).then_inc(tail_sq, 1)
            def middle_turn(i):
                act.wait_ge(mid_var, i + 1)
                nc.scalar.activation(st5[0:B, 1, :], st5[0:B, 0, :], ACT.Sqrt).then_inc(mid_root, 1)
                act.wait_ge(mid_scale, i + 1)
                await_ge(act, tok_stored, i * 16)
                await_ge(act, mt_mm, i * GT)
                for j in range(GT):
                    nc.scalar.activation(rows[0:B, j, :], X[0:B, ds(i * GT + j, 1), :].rearrange("p a c -> p (a c)"), ACT.Identity,
                                         bias=st5[0:B, 3, j:j + 1], scale=st5[0:B, 2, j:j + 1]).then_inc(mid_norm, 1)
                for j in range(GT):
                    act.wait_ge(mt_mm, i * GT + (j + 1))
                    await_ge(act, mg_mm, i * GT + max(j - 1, 0))
                    nc.scalar.activation(tT[:, j % 2, :, 0:B], bank[4 + j % 2][:, 0:KC * B].rearrange("p (k n) -> p k n", k=KC),
                                         ACT.Copy).then_inc(mt_out, 1)

            turns_of(act, 0, NT // GT, middle_turn)
            act.wait_ge(exp_arg, 1)
            nc.scalar.activation(st[0:B, 1, 0:NT], st[0:B, 0, 0:NT], ACT.Exp).then_inc(exp_done, 1)
            act.wait_ge(slots_ready, 1)

            def token_numbers(i, k):
                await_ge(act, tok_got[k], i * 16)
                nc.scalar.activation(idx[:, k:k + 1], s_tok[:, ds(i * RING + k, 1)], ACT.Copy).then_inc(tok_idx, 1)

            for k in range(RING):
                token_numbers(0, k)

            def expert_turn(i, last):
                _, offs = nc.values_load_multi_w_load_instructions(
                    ex_b1[0:1, ds(i * RING, RING)], engines=[ACT_], min_val=0, max_val=(NE - 1) * KF,
                    skip_runtime_bounds_check_because="the router clamps it")
                for k in range(RING):
                    await_ge(act, y_put[k], i * 16)
                    nc.scalar.activation(odx[:, k:k + 1], s_row[:, ds(i * RING + k, 1)], ACT.Copy).then_inc(out_idx, 1)
                    act.wait_ge(h_mm, i * RING + (k + 1))
                    if not (isinstance(i, int) and k < 2):
                        act.wait_ge(y_mm, i * RING + (k - 1))
                    for m in range(KF):
                        ins = nc.scalar.activation(hT[:, k % 2, m, :], bank[2 + k % 2][:, m * 128:(m + 1) * 128], ACT.Relu,
                                                   bias=bcol[:, ds(offs[k] + m, 1)])
                    ins.then_inc(h_out, 1)
                    if not last:
                        token_numbers(i + 1, k)

            turns_of(act, 0, SLOTS // RING, lambda i: expert_turn(i, False), lambda i: expert_turn(i, True))
            def last_turn(i):
                for j in range(GT):
                    await_ge(act, fin_norm, i * GT)
                    nc.scalar.activation(zb[0:B, j, :], X[0:B, ds(i * GT + j, 1), :].rearrange("p a c -> p (a c)"), ACT.Identity,
                                         bias=mid_nb[0:B, ds(i * GT + j, 1)], scale=mid_rs[0:B, ds(i * GT + j, 1)]).then_inc(fz, 1)
                act.wait_ge(fin_var, i + 1)
                nc.scalar.activation(st5[0:B, 1, :], st5[0:B, 0, :], ACT.Sqrt).then_inc(fin_root, 1)
                act.wait_ge(fin_scale, i + 1)
                for j in range(GT):
                    await_ge(act, fin_out, i * GT)
                    nc.scalar.activation(ub[0:B, j, :], zb[0:B, j, :], ACT.Identity,
                                         bias=st5[0:B, 3, j:j + 1], scale=st5[0:B, 2, j:j + 1]).then_inc(fin_norm, 1)

            turns_of(act, 0, NT // GT, last_turn)

        @block.gpsimd
        def _(pool):
            step = Steps(pool, pool_step)
            nc.gpsimd.memset(esrc[:, FULL:COLS], 0).then_inc(pads, 1)
            nc.gpsimd.memset(edst[:, FULL:COLS], 0).then_inc(pads, 1)
            nc.gpsimd.memset(ew[:, FULL:COLS], 0.0).then_inc(pads, 1)
            step.mark(nc.gpsimd.iota(iota[:, :], pattern=[[1, HMAX]], base=0, channel_multiplier=0, allow_small_or_imprecise_dtypes=True))
            step.mark(nc.gpsimd.iota(node[:, :], pattern=[[B, NT]], base=0, channel_multiplier=1, allow_small_or_imprecise_dtypes=True))
            step.mark(nc.gpsimd.iota(slot_id[:, :], pattern=[[128, SLOTS]], base=2 * N + 1, channel_multiplier=1,
                                     allow_small_or_imprecise_dtypes=True))
            step.mark(nc.gpsimd.memset(ones[:, :], 1.0))
            step.mark(nc.gpsimd.memset(ident[:, :], 0.0))
            step.mark(nc.gpsimd.memset(small[:, :, :], 0.0))
            step(nc.gpsimd.memset(zeros[:, :], 0.0))
            step(nc.gpsimd.affine_select(out=tri[:, :], in_=ones[:, :], compare_op=ALU.is_gt, fill=0.0, base=0,
                                         pattern=[[1, 128]], channel_multiplier=-1))
            nc.gpsimd.affine_select(out=ident[:, :], in_=ident[:, :], compare_op=ALU.not_equal, fill=1.0, base=0,
                                    pattern=[[-1, 128]], channel_multiplier=1).then_inc(consts, 1)
            step(nc.gpsimd.memset(accf[:, :], 0.0))
            pool.wait_ge(xn_ready, 1)
            pool.wait_ge(ld_b, 16 * B_LOADS)
            step(nc.gpsimd.tensor_tensor(X[0:B, :, :], X[0:B, :, :], xn[0:B, :, :], ALU.add))
            nc.gpsimd.tensor_tensor(X[0:B, :, :], X[0:B, :, :], mb2[0:B, :].unsqueeze(1).to_broadcast([B, NT, C]),
                                    ALU.add).then_inc(x_plus, 1)
            pool.wait_ge(tab_stored[0], 16 * (NT - NT // 2))
            pool.wait_ge(tab_stored[1], 16 * (NT // 2))
            for g in range(3):
                turn_base = CHUNK0[g] // RING
                with pool.Fori(0, TURNS[g]) as i:
                    for k in range(RING):
                        pool.wait_ge(idx_ready, i * RING + CHUNK0[g] + k + 1)
                        pool.wait_ge(chunk_done, i * RING + (CHUNK0[g] + k + 1))
                        pool.sem_inc(may_go, 1)
                        nc.gpsimd.indirect_dma_start(
                            out=rows[:, k, :], out_offset=None, in_=table[:, :],
                            in_offset=bass.IndirectOffsetOnAxis(ap=idx[:, k:k + 1], axis=0)).then_inc(gathered[k], 16)

            pool.wait_ge(tok_stored, 16 * (NT // GT))

            def get_tokens(i, k, turns_before, turned):
                pool.wait_ge(tok_idx, i * RING + (k + 1))
                await_ge(pool, x_mm, turns_before * RING + (k + 1 if turned else 0))
                pool.sem_inc(may_go, 1)
                nc.gpsimd.indirect_dma_start(
                    out=rows[:, k, :], out_offset=None, in_=tokens[:, :],
                    in_offset=bass.IndirectOffsetOnAxis(ap=idx[:, k:k + 1], axis=0)).then_inc(tok_got[k], 16)

            def put_results(i, k):
                pool.wait_ge(out_idx, i * RING + (k + 1))
                pool.wait_ge(y_out, i * RING + (k + 1))
                pool.sem_inc(may_go, 1)
                nc.gpsimd.indirect_dma_start(
                    out=pair_out[:, :], out_offset=bass.IndirectOffsetOnAxis(ap=odx[:, k:k + 1], axis=0),
                    in_=yv[:, k % 2, :], in_offset=None).then_inc(y_put[k], 16)

            for k in range(RING):
                get_tokens(0, k, 0, False)
            with pool.Fori(0, SLOTS // RING - 1) as i:
                for k in range(RING):
                    get_tokens(i + 1, k, i, True)
                    put_results(i, k)
            for k in range(RING):
                put_results(SLOTS // RING - 1, k)
            pool.wait_ge(ld_gb, 32)
            pstep = Steps(pool, pool_step)
            pstep.done = step.done
            with pstep.loop(NT // GT, GT) as i:
                for j in range(GT):
                    pool.wait_ge(fin_norm, i * GT + (j + 1))
                    pstep(nc.gpsimd.tensor_tensor(ub[0:B, j, :], ub[0:B, j, :], gam[0:B, :], ALU.mult))
                    nc.gpsimd.tensor_tensor(ub[0:B, j, :], ub[0:B, j, :], bet[0:B, :], ALU.add).then_inc(fin_aff, 1)

        def rsqrt_refined(step, out_, var, root, tmp):
            step(nc.vector.reciprocal(out_, root))
            step(nc.vector.tensor_tensor(tmp, out_, out_, ALU.mult))
            step(nc.vector.tensor_tensor(tmp, tmp, var, ALU.mult))
            step(nc.vector.tensor_scalar(tmp, tmp, -0.5, 1.5, ALU.mult, ALU.add))
            step(nc.vector.tensor_tensor(out_, out_, tmp, ALU.mult))

        def route(dve, step, rounds, P, T, nb, H, key_, lo_, hi_, buckets, rt_one=rt_one, rt_sum=rt_sum):
            one = rt_one[0:P, 0:nb * T]
            run = rt_sum[0:P, 0:nb * T]
            one3, run3 = one.rearrange("p (b t) -> p b t", b=nb), run.rearrange("p (b t) -> p b t", b=nb)
            ends, mine, first, off = small[0:P, 0, :], small[0:P, 1, :], small[0:P, 2, :], small[0:P, 3, :]
            step(nc.vector.tensor_tensor(one3, key_.unsqueeze(1).to_broadcast([P, nb, T]),
                                         iota[0:P, 0:nb].unsqueeze(2).to_broadcast([P, nb, T]), ALU.is_equal))
            step(nc.vector.tensor_tensor_scan(run, one, one, 0.0, ALU.add, ALU.max))
            step(nc.vector.tensor_copy(ends[:, 1:nb + 1], run3[:, :, T - 1]))
            nc.vector.tensor_tensor(mine[:, 0:nb], ends[:, 1:nb + 1], ends[:, 0:nb], ALU.subtract).then_inc(rank_rows, 1)
            dve.wait_ge(rank_sums, rounds)
            before, total = bank[6][0:P, 0:nb], bank[6][0:P, 32:32 + nb]
            step(nc.vector.tensor_scalar(slot_i[0:P, 0:nb], total, 127.0, None, ALU.add))
            step(nc.vector.tensor_scalar(cnt_i[0:P, 0:nb], slot_i[0:P, 0:nb], 7, None, ALU.logical_shift_right))
            step(nc.vector.tensor_copy(off[:, 0:nb], cnt_i[0:P, 0:nb]))
            step(nc.vector.tensor_tensor_scan(first[:, 1:nb + 1], off[:, 0:nb], off[:, 0:nb], 0.0, ALU.add, ALU.max))
            step(nc.vector.scalar_tensor_tensor(off[:, 0:nb], first[:, 0:nb], 128.0, before, ALU.mult, ALU.add))
            step(nc.vector.scalar_tensor_tensor(off[:, 0:nb], off[:, 0:nb], -1.0, ends[:, 0:nb], ALU.add, ALU.subtract))
            step(nc.vector.tensor_tensor(run3, run3, off[:, 0:nb].unsqueeze(2).to_broadcast([P, nb, T]), ALU.add))
            step(nc.vector.tensor_tensor(run, run, one, ALU.mult))
            step(nc.vector.tensor_reduce(slot[0:P, 0:T], run.rearrange("p (b t) -> p t b", b=nb), AX.X, ALU.add))
            cmp = rt_one[0:1, 0:H * nb].rearrange("p (h b) -> p h b", b=nb)
            step.mark(nc.vector.tensor_tensor(cmp, first[0:1, 1:nb + 1].unsqueeze(1).to_broadcast([1, H, nb]),
                                              iota[0:1, 0:H].unsqueeze(2).to_broadcast([1, H, nb]), ALU.is_le))
            step(nc.vector.tensor_copy(slot_i[0:P, 0:T], slot[0:P, 0:T]))
            step.mark(nc.vector.tensor_reduce(bk_f[0:1, 0:H], cmp, AX.X, ALU.add))
            step(nc.vector.tensor_scalar(slot_j[0:P, 0:T], slot_i[0:P, 0:T], 7, None, ALU.logical_shift_right))
            for bucket, scale in buckets:
                step.mark(nc.vector.tensor_scalar(bucket, bk_f[0:1, 0:H], float(nb - 1), float(scale), ALU.min, ALU.mult))
            step(nc.vector.tensor_copy(hi_, slot_j[0:P, 0:T]))
            step(nc.vector.tensor_scalar(slot_j[0:P, 0:T], slot_i[0:P, 0:T], 127, None, ALU.bitwise_and))
            step(nc.vector.tensor_copy(lo_, slot_j[0:P, 0:T]))

        def sort_column(dve, j, n, s, H):
            dve.wait_ge(hots_used, n)
            nc.vector.tensor_scalar(s_hi[:, s, 0:H], iota[:, 0:H], hi[:, ds(j, 1)], None, ALU.is_equal)
            nc.vector.tensor_scalar(s_one[:, s, :], iota[:, 0:128], lo[:, ds(j, 1)], None, ALU.is_equal).then_inc(hots_made, 1)

        def take_group(dve, step, g):
            H, c = H_OF[g], CHUNK0[g]
            dve.wait_ge(sorted_, g + 1)
            step.mark(nc.vector.tensor_copy(g_w[:, c:c + H], bank[1][:, 0:H]))
            step(nc.vector.tensor_copy(slot_i[:, 0:H], bank[0][:, 0:H]))
            step.mark(nc.vector.tensor_scalar(g_row[:, c:c + H], slot_i[:, 0:H], 7, None, ALU.logical_shift_right))
            step(nc.vector.tensor_scalar(slot_j[:, 0:H], slot_i[:, 0:H], 127, None, ALU.bitwise_and))
            step(nc.vector.tensor_copy(g_lo[:, c:c + H], slot_j[:, 0:H]))
            nc.vector.memset(slot[0:1, 191:192], 0.0).then_inc(group_ready, 1)

        def attention_fold_dve(dve, step):
            normalise_keys(dve, step, NT - 1)
            dve.wait_ge(kv_used, NT)
            gv, bv = bcol[:, 68:69], bcol[:, 69:70]
            for j in range(KC):
                step.mark(nc.vector.tensor_copy(kvsum[:, j, :], bank[6][:, 260 + j:261 + j].to_broadcast([128, 128])))
            step.mark(nc.vector.tensor_scalar(kvst[:, 2, 0:KC], bank[6][:, 256:256 + KC], gv, None, ALU.mult))
            step.wait()
            nc.vector.scalar_tensor_tensor(kvst[:, 2, 0:KC], bv.to_broadcast([128, KC]), float(N), kvst[:, 2, 0:KC],
                                           ALU.mult, ALU.add).then_inc(kv_sums, 1)
            step(nc.vector.memset(kvT[:, :, :], 0.0))
            dve.wait_ge(kv_sums_row, 1)
            full = kvs[:, :, :, :].rearrange("p h s d -> p (h s d)")[:, 0:C]
            step(nc.vector.tensor_scalar(full, bank[1][:, 0:C], bv, None, ALU.mult))
            step(nc.vector.scalar_tensor_tensor(full, bank[6][:, 0:C], gv, full, ALU.mult, ALU.add))
            f3 = full.rearrange("p (h d) -> p h d", d=HD)
            step(nc.vector.tensor_tensor(f3, f3, ln_g[:, 0, :].unsqueeze(1).to_broadcast([128, HEADS, HD]), ALU.mult))
            for j in range(KC):
                fj = f3[:, 4 * j:4 * j + 4, :]
                step(nc.vector.scalar_tensor_tensor(fj, ln_b[:, 0, :].unsqueeze(1).to_broadcast([128, 4, HD]), kvst[:, 2, j:j + 1], fj,
                                                    ALU.mult, ALU.add))
            for j in range(KC):
                for h in range(4):
                    s = slice(h * HD, (h + 1) * HD)
                    ins = nc.vector.tensor_scalar(kvT[s, j, s], full[s, j * 128 + h * HD:j * 128 + (h + 1) * HD], 1.0 / N, None, ALU.mult)
            ins.then_inc(kvT_ready, 1)
            dve.wait_ge(weff_mm, 1)
            step.mark(nc.vector.tensor_tensor(weff[:, :, :].rearrange("p k n -> p (k n)"), bank[0][:, :],
                                              mw1[:, :, :].rearrange("p k n -> p (k n)"), ALU.add))
            for m in range(KC):
                step.mark(nc.vector.tensor_tensor(beff[:, m:m + 1], bank[1][:, 256 + m:257 + m], bcol[:, 66 + m:67 + m], ALU.add))
            step.wait()
            nc.vector.memset(slot[0:1, 191:192], 0.0).then_inc(weff_out, 1)

        def normalise_keys(dve, step, tile):
            dve.wait_ge(kv_std, tile + 1)
            step(nc.vector.reciprocal(kvst[0:B, 3, :], kvst[0:B, 1, :]))
            await_ge(dve, kv_used, tile)
            nc.vector.tensor_tensor(kvn[0:B, :, :, :].rearrange("p s h d -> p h s d"), kvc[0:B],
                                    kvst[0:B, 3, :].rearrange("p (h s) -> p h s", s=2).unsqueeze(3).to_broadcast([B, HEADS, 2, HD]),
                                    ALU.mult).then_inc(kv_norm, 1)

        def attention_keys_dve(dve, step, k, i, tile0):
            if k == 1 and not (isinstance(i, int) and i + tile0 == 0):
                normalise_keys(dve, step, i + (tile0 - 1))
            if k == 4:
                dve.wait_ge(kv_mm, i + (tile0 + 1))
                await_ge(dve, kv_norm, i + tile0)
                nc.vector.tensor_tensor(kvc[0:B], bank[4][0:B, :].rearrange("p (h s d) -> p h s d", h=HEADS, s=2),
                                        bias_kv[0:B, :, HD:3 * HD].rearrange("p h (s d) -> p h s d", s=2), ALU.add).then_inc(kv_sb, 1)
            if k == 6:
                dve.wait_ge(kv_sq, i + (tile0 + 1))
                step(nc.vector.tensor_reduce(kvst[0:B, 2, :], kvs[0:B].rearrange("p h s d -> p (h s) d"), AX.X, ALU.add))
                nc.vector.tensor_scalar(kvst[0:B, 0, :], kvst[0:B, 2, :], 1.0 / HD, LN_EPS, ALU.mult, ALU.add).then_inc(kv_var, 1)

        @block.vector
        def _(dve):
            step = Steps(dve, dve_step)
            dve.wait_ge(ld_edge, 16 * 6)
            step(nc.vector.tensor_scalar(eq[:, :], esrc[:, :], 4195.0, None, ALU.mult))
            step(nc.vector.tensor_scalar(eq[:, :], eq[:, :], 19, None, ALU.logical_shift_right))
            step(nc.vector.tensor_copy(key[:, :], eq[:, :]))
            step(nc.vector.scalar_tensor_tensor(pack[:, :], key[:, :], -float(B), esrc[:, :], ALU.mult, ALU.add))
            step(nc.vector.scalar_tensor_tensor(pack[:, :], edst[:, :], 128.0, pack[:, :], ALU.mult, ALU.add))
            dve.wait_ge(consts, 1)
            nc.vector.memset(slot[0:1, 191:192], 0.0).then_inc(chunk_added, RING)
            T = T_OF[0]
            route(dve, step, 1, 128, T, NT, H_OF[0], key[:, 0:T], lo[:, 0:T], hi[:, 0:T], [(bk[:, 0:H_OF[0]], C)])
            dve.wait_ge(ld_x, 32)
            for t in range(NT):
                step(nc.vector.bn_stats(bn6[0:B, :], X[0:B, t, :]))
                step(nc.vector.bn_aggr(mv[0:B, t, :], bn6[0:B, :]))
            nc.vector.tensor_scalar(st[0:B, 1, 0:NT], mv[0:B, :, 1], LN_EPS, None, ALU.add).then_inc(var_ready, 1)
            dve.wait_ge(sqrt_done, 1)
            rsqrt_refined(step, st[0:B, 3, 0:NT], st[0:B, 1, 0:NT], st[0:B, 0, 0:NT], st[0:B, 4, 0:NT])
            for t in range(NT):
                ins = nc.vector.tensor_scalar(xn[0:B, t, :], X[0:B, t, :], mv[0:B, t, 0:1], st[0:B, 3, t:t + 1], ALU.subtract, ALU.mult)
            ins.then_inc(xn_ready, 1)
            with dve.Fori(0, T // SR) as i:
                for s in range(SR):
                    sort_column(dve, i * SR + s, i * SR + (s + 1), s, H_OF[0])
            for j in range(T // SR * SR, T):
                sort_column(dve, j, j + 1, j % SR, H_OF[0])
            def s_(k):
                return st[0:B, k, 0:NT]
            dve.wait_ge(squares, 1)
            nc.vector.tensor_scalar(s_(1), s_(2), EPS * EPS, None, ALU.max).then_inc(var_ready, 1)
            dve.wait_ge(sqrt_done, 2)
            rsqrt_refined(step, s_(3), s_(1), s_(0), s_(4))
            step(nc.vector.tensor_tensor(s_(3), s_(3), s_(1), ALU.mult))
            step(nc.vector.tensor_scalar(s_(3), s_(3), MAXNORM, None, ALU.min))
            step.mark(nc.vector.tensor_scalar(s_(4), s_(3), -1.0, 1.0, ALU.mult, ALU.add))
            step(nc.vector.tensor_scalar(s_(5), s_(3), 1.0, None, ALU.add))
            step(nc.vector.reciprocal(s_(4), s_(4)))
            nc.vector.tensor_tensor(s_(6), s_(5), s_(4), ALU.mult).then_inc(ln_arg, 1)
            step(nc.vector.tensor_tensor(s_(11), s_(3), s_(3), ALU.mult))
            step(nc.vector.tensor_scalar(s_(8), s_(11), 1 / 7, 1 / 5, ALU.mult, ALU.add))
            step(nc.vector.tensor_tensor(s_(8), s_(8), s_(11), ALU.mult))
            step(nc.vector.tensor_scalar(s_(8), s_(8), 1 / 3, None, ALU.add))
            step(nc.vector.tensor_tensor(s_(8), s_(8), s_(11), ALU.mult))
            step(nc.vector.tensor_scalar(s_(8), s_(8), 1.0, None, ALU.add))
            step(nc.vector.reciprocal(s_(9), s_(3)))
            dve.wait_ge(ln_done, 1)
            step(nc.vector.scalar_tensor_tensor(s_(9), s_(0), 0.5, s_(9), ALU.mult, ALU.mult))
            step(nc.vector.tensor_tensor(s_(8), s_(8), s_(9), ALU.subtract))
            step(nc.vector.tensor_scalar(s_(10), s_(3), 0.06, None, ALU.is_lt))
            step(nc.vector.tensor_tensor(s_(8), s_(8), s_(10), ALU.mult))
            nc.vector.tensor_tensor(s_(7), s_(8), s_(9), ALU.add).then_inc(row_scale, 1)
            take_group(dve, step, 0)
            dve.wait_ge(ld_w, 16 * W_LOADS)
            dve.wait_ge(ld_b, 16 * B_LOADS)
            for k in range(KC):
                step.mark(nc.vector.tensor_copy(weff[:, k, :].rearrange("p (h d) -> p h d", d=HD),
                                                wqkv[:, k, :].rearrange("p (h s d) -> p h s d", s=3, d=HD)[:, :, 0, :]))
                w3 = wqkv[:, k, :].rearrange("p (a d) -> p a d", d=HD)
                step(nc.vector.tensor_reduce(wmean[:, k, :], w3, AX.X, ALU.add))
                step.mark(nc.vector.scalar_tensor_tensor(
                    wcen[:, k, :].rearrange("p (a d) -> p a d", d=HD), wmean[:, k, :].unsqueeze(2).to_broadcast([128, 3 * HEADS, HD]),
                    -1.0 / HD, w3, ALU.mult, ALU.add))
            b3 = bias_kv[:, :, :].rearrange("p h (s d) -> p (h s) d", d=HD)
            step(nc.vector.tensor_reduce(wmean[:, 0, :], b3, AX.X, ALU.add))
            step(nc.vector.scalar_tensor_tensor(b3, wmean[:, 0, :].unsqueeze(2).to_broadcast([128, 3 * HEADS, HD]),
                                                -1.0 / HD, b3, ALU.mult, ALU.add))
            nc.vector.memset(slot[0:1, 191:192], 0.0).then_inc(wcen_ready, 1)
            dve.wait_ge(xn_t, NT)
            dve.wait_ge(squares, 1)
            dve.wait_ge(x_plus, 1)
            for g in (1, 2):
                a, T = AT[g], T_OF[g]
                route(dve, step, g + 1, 128, T, NT, H_OF[g], key[:, a:a + T], lo[:, a:a + T], hi[:, a:a + T], [(bk[:, CHUNK0[g]:CHUNK0[g] + H_OF[g]], C)])

            nc.vector.memset(slot[0:1, 191:192], 0.0).then_inc(routed, 1)

            def chunk_hot(c, k):
                nc.vector.tensor_scalar(hot[:, k, :], iota[:, 0:128], g_lo[:, ds(c, 1)], g_w[:, ds(c, 1)],
                                        ALU.is_equal, ALU.mult).then_inc(hot_ready, 1)

            for k in range(RING):
                chunk_hot(k, k)
            for g, turns, turn0, nsort, mix, tile0 in SEGS:
                c0 = CHUNK0[g] + RING * turn0
                last = c0 + turns * RING == CHUNKS
                if g < 2 and turn0 == SORT_TURNS[g]:
                    take_group(dve, step, g + 1)
                    if g == 1:
                        attention_fold_dve(dve, step)
                col0 = AT[g + 1] + nsort * turn0 if nsort else 0
                split = shares(nsort, RING)

                def turn(i):
                    _, offs = nc.values_load_multi_w_load_instructions(
                        bk[0:1, ds(i * RING + c0, RING)], engines=[DVE_], min_val=0, max_val=(NT - 1) * C,
                        skip_runtime_bounds_check_because="the router clamps it")
                    m = 0

                    def add_chunk(k):
                        dve.wait_ge(chunk_added, i * RING + (RING + c0 + k))
                        to = accf[:, ds(offs[k], C)]
                        nc.vector.tensor_tensor(to, to, bank[CHUNK_BANKS[k // 2]][:, k % 2 * C:(k % 2 + 1) * C],
                                                ALU.add).then_inc(chunk_added, 1)

                    for k in range(RING):
                        for _ in range(split[k]):
                            sort_column(dve, i * nsort + (col0 + m), i * nsort + (col0 + m + 1), m % SR, H_OF[g + 1])
                            m += 1
                        if mix == 1:
                            attention_keys_dve(dve, step, k, i, tile0)
                        if mix == 2 and k == 6:
                            dve.wait_ge(my_mm, i + (tile0 + 1))
                            nc.vector.tensor_tensor(X[0:B, ds(i + tile0, 1), :], X[0:B, ds(i + tile0, 1), :],
                                                    bank[0][0:B, 0:C].unsqueeze(1), ALU.add).then_inc(my_out, 1)
                        if k % 2:
                            dve.wait_ge(chunk_done, i * RING + (RING + c0 + k + 1))
                            add_chunk(k - 1)
                            if not last:
                                chunk_hot(i * RING + (c0 + RING + k - 1), k - 1)
                                chunk_hot(i * RING + (c0 + RING + k), k)
                            add_chunk(k)

                if turns == 1:
                    turn(0)
                else:
                    with step.loop(turns, 2 if mix == 1 else 0) as i:
                        turn(i)
            dve.wait_ge(chunk_added, RING + CHUNKS)
            for t in range(NT):
                step(nc.vector.tensor_tensor_reduce(out=rows[0:B, 1, :], in0=acc[0:B, t, :], in1=gb[0:B, :], scale=1.0, scalar=0.0,
                                                    op0=ALU.mult, op1=ALU.add, accum_out=st[0:B, 3, t:t + 1]))

            def a_(k):
                return st[0:B, k, :]

            def one(k):
                return st[0:B, k, NT:NT + 1]
            dve.wait_ge(tail_ss, 1)
            nc.vector.tensor_scalar(a_(1), a_(2), EPS * EPS, None, ALU.max).then_inc(tail_v, 1)
            dve.wait_ge(tail_sq, 1)
            rsqrt_refined(step, a_(4), a_(1), a_(0), a_(5))
            step(nc.vector.tensor_tensor(a_(5), a_(4), a_(1), ALU.mult))
            nc.vector.tensor_scalar(a_(6), a_(5), 15.0, None, ALU.min).then_inc(tail_v, 1)
            dve.wait_ge(tail_tanh, 1)
            step(nc.vector.tensor_scalar(a_(8), a_(7), EPS, None, ALU.max))
            step(nc.vector.reciprocal(a_(8), a_(8)))
            step(nc.vector.tensor_scalar(a_(8), a_(8), MAXNORM, 1.0, ALU.mult, ALU.min))
            step(nc.vector.tensor_tensor(a_(4), a_(4), a_(7), ALU.mult))
            step(nc.vector.tensor_tensor(a_(8), a_(8), a_(4), ALU.mult))
            step(nc.vector.tensor_tensor(a_(9), a_(8), a_(8), ALU.mult))
            step(nc.vector.tensor_tensor(a_(9), a_(9), a_(2), ALU.mult))
            step(nc.vector.tensor_tensor(s_(10), s_(8), s_(3), ALU.mult))
            step(nc.vector.tensor_scalar(s_(10), s_(10), one(8), 2.0, ALU.mult, ALU.mult))
            step(nc.vector.tensor_scalar(s_(11), s_(10), 1.0, None, ALU.add))
            step(nc.vector.scalar_tensor_tensor(s_(12), s_(11), one(9), s_(8), ALU.add, ALU.mult))
            step(nc.vector.scalar_tensor_tensor(s_(13), s_(9), one(9), s_(11), ALU.mult, ALU.add))
            step(nc.vector.tensor_scalar(s_(13), s_(13), EPS, None, ALU.add))
            step(nc.vector.reciprocal(s_(13), s_(13)))
            step(nc.vector.tensor_scalar(s_(10), s_(9), -1.0, 1.0, ALU.mult, ALU.add))
            step(nc.vector.tensor_scalar(s_(10), s_(10), one(8), None, ALU.mult))
            step(nc.vector.tensor_tensor(s_(12), s_(12), s_(13), ALU.mult))
            step(nc.vector.tensor_tensor(s_(13), s_(10), s_(13), ALU.mult))
            step(nc.vector.tensor_tensor(s_(5), s_(13), s_(3), ALU.mult))
            step(nc.vector.tensor_tensor(s_(6), s_(12), s_(2), ALU.mult))
            step(nc.vector.scalar_tensor_tensor(s_(5), s_(5), 2.0, s_(6), ALU.mult, ALU.add))
            step(nc.vector.tensor_tensor(s_(5), s_(5), s_(12), ALU.mult))
            step(nc.vector.tensor_tensor(s_(6), s_(13), s_(13), ALU.mult))
            step(nc.vector.scalar_tensor_tensor(s_(5), s_(6), one(2), s_(5), ALU.mult, ALU.add))
            nc.vector.tensor_scalar(s_(1), s_(5), EPS * EPS, None, ALU.max).then_inc(tail_v, 1)
            dve.wait_ge(tail_sq, 2)
            rsqrt_refined(step, s_(4), s_(1), s_(0), s_(5))
            step(nc.vector.tensor_scalar(s_(4), s_(4), MAXNORM, 1.0, ALU.mult, ALU.min))
            step.mark(nc.vector.tensor_tensor(s_(14), s_(12), s_(4), ALU.mult))
            step(nc.vector.tensor_tensor(s_(15), s_(13), s_(4), ALU.mult))

            def norm_scale(step, signal):
                rsqrt_refined(step, st5[0:B, 2, :], st5[0:B, 0, :], st5[0:B, 1, :], st5[0:B, 4, :])
                nc.vector.scalar_tensor_tensor(st5[0:B, 3, :], mv5[0:B, :, 0], -1.0, st5[0:B, 2, :], ALU.mult, ALU.mult).then_inc(signal, 1)

            for i in range(NT // GT):
                for j in range(GT):
                    xt = X[0:B, ds(i * GT + j, 1), :].rearrange("p a c -> p (a c)")
                    step(nc.vector.scalar_tensor_tensor(xt, acc[0:B, ds(i * GT + j, 1), :].rearrange("p a c -> p (a c)"),
                                                        st[0:B, 14, ds(i * GT + j, 1)], xt, ALU.mult, ALU.add))
                    step(nc.vector.scalar_tensor_tensor(xt, gb[0:B, :], st[0:B, 15, ds(i * GT + j, 1)], xt, ALU.mult, ALU.add))
                    step(nc.vector.bn_stats(bn6[0:B, :], xt))
                    step(nc.vector.bn_aggr(mv5[0:B, j, :], bn6[0:B, :]))
                nc.vector.tensor_scalar(st5[0:B, 0, :], mv5[0:B, :, 1], LN_EPS, None, ALU.add).then_inc(mid_var, 1)
                dve.wait_ge(mid_root, i + 1)
                norm_scale(step, mid_scale)
                step.mark(nc.vector.tensor_copy(mid_rs[0:B, ds(i * GT, GT)], st5[0:B, 2, :]))
                dve.wait_ge(mid_scale, i + 1)
                step.mark(nc.vector.tensor_copy(mid_nb[0:B, ds(i * GT, GT)], st5[0:B, 3, :]))
                for j in range(GT):
                    dve.wait_ge(mg_mm, i * GT + (j + 1))
                    nc.vector.tensor_tensor(lg[0:B, j % 2, :], bank[6 + j % 2][0:B, 0:NE], gateb[0:B, :], ALU.add).then_inc(mg_out, 1)
                    dve.wait_ge(mg_out, i * GT + (j + 1))
                    step(nc.vector.max(mx5[0:B, j, :], lg[0:B, j % 2, :]))
                    step(nc.vector.max_index(ix5[0:B, j, :], mx5[0:B, j, :], lg[0:B, j % 2, :]))
                step.mark(nc.vector.tensor_copy(topv[0:B, :, ds(i * GT, GT)], mx5[0:B, :, 0:2].rearrange("p t k -> p k t")))
                step(nc.vector.tensor_copy(pair_key[0:B, :, ds(i * GT, GT)], ix5[0:B, :, 0:2].rearrange("p t k -> p k t")))
            nc.vector.tensor_tensor(s_(0), topv[0:B, 1, :], topv[0:B, 0, :], ALU.subtract).then_inc(exp_arg, 1)
            nc.vector.memset(slot[0:1, 191:192], 0.0).then_inc(acc_free, 1)
            dve.wait_ge(tok_stored, 16 * (NT // GT))
            dve.wait_ge(mt_mm, NT)
            flat = rows[:, :, :].rearrange("p k c -> p (k c)")
            route(dve, step, 4, B, PAIRS, NE, SLOTS, pair_key[0:B, :, :].rearrange("p k t -> p (k t)"), pair_lo[0:B, :], pair_hi[0:B, :],
                  [(ex_w[0:1, :], 2048), (ex_b1[0:1, :], KF), (ex_b2[0:1, :], C)], flat[:, 0:NE * SLOTS], flat[:, 1024:2048])
            dve.wait_ge(exp_done, 1)
            step(nc.vector.tensor_scalar(s_(2), s_(1), 1.0, None, ALU.add))
            step(nc.vector.reciprocal(pair_w[0:B, 0, :], s_(2)))
            step(nc.vector.tensor_tensor(pair_w[0:B, 1, :], s_(1), pair_w[0:B, 0, :], ALU.mult))
            step.mark(nc.vector.tensor_scalar(pair_row[0:B, 0, :], node[0:B, :], 1.0, None, ALU.add))
            step(nc.vector.tensor_scalar(pair_row[0:B, 1, :], node[0:B, :], float(N + 1), None, ALU.add))

            def pair_column(j, node_, row_, s):
                nc.vector.tensor_scalar(p_lo[0:B, s, 0, :], iota[0:B, 0:128], pair_lo[0:B, ds(j, 1)], node_, ALU.is_equal, ALU.mult)
                nc.vector.tensor_scalar(p_lo[0:B, s, 1, :], iota[0:B, 0:128], pair_lo[0:B, ds(j, 1)], row_, ALU.is_equal, ALU.mult)
                nc.vector.tensor_scalar(p_hi[0:B, s, :], iota[0:B, 0:SLOTS], pair_hi[0:B, ds(j, 1)], None,
                                        ALU.is_equal).then_inc(pairs_made, 1)

            for k in range(2):
                rowk = pair_row[0:B, k, :]
                if k:
                    dve.wait_ge(pairs_used, NT)
                pair_column(k * NT, node[0:B, 0:1], rowk[:, 0:1], 0)
                with dve.Fori(0, (NT - 1) // PR) as i:
                    dve.wait_ge(pairs_used, i * PR + (k * NT + 1))
                    for s in range(PR):
                        pair_column(i * PR + (k * NT + 1 + s), node[0:B, ds(i * PR + (1 + s), 1)], rowk[:, ds(i * PR + (1 + s), 1)], s)
            dve.wait_ge(pairs_used, PAIRS)
            step.mark(nc.vector.tensor_copy(s_tok[:, :], bank[0][:, 0:SLOTS]))
            step(nc.vector.tensor_copy(s_tmp[:, 0, :], bank[1][:, 0:SLOTS]))
            step(nc.vector.tensor_scalar(s_tmp[:, 1, :], s_tmp[:, 0, :], 0.0, None, ALU.is_equal))
            step(nc.vector.tensor_tensor(s_tmp[:, 1, :], s_tmp[:, 1, :], slot_id[:, :], ALU.mult))
            step(nc.vector.scalar_tensor_tensor(s_row[:, :], s_tmp[:, 0, :], -1.0, s_tmp[:, 1, :], ALU.add, ALU.add))
            nc.vector.memset(slot[0:1, 191:192], 0.0).then_inc(slots_ready, 1)
            dve.wait_ge(ld_moe, 32 * NE)
            dve.wait_ge(ld_b2, 16)

            def expert_weights(off):
                nc.vector.tensor_copy(w1c[:, :, :].rearrange("p k n -> p (k n)"), slab[:, ds(off, 1024)]).then_inc(w_copied, 1)

            def add_output_bias(turn, k, off):
                dve.wait_ge(y_mm, turn * RING + (k + 1))
                if k >= 2:
                    dve.wait_ge(y_put[k - 2], turn * 16 + 16)
                else:
                    await_ge(dve, y_put[k + RING - 2], turn * 16)
                nc.vector.tensor_tensor(yv[:, k % 2, :], bank[4 + k % 2][:, 0:C],
                                        b2b[:, :, :].rearrange("p e c -> p (e c)")[:, ds(off, C)], ALU.add).then_inc(y_out, 1)

            def bias_offsets(start, n):
                return nc.values_load_multi_w_load_instructions(
                    ex_b2[0:1, ds(start, n)], engines=[DVE_], min_val=0, max_val=(NE - 1) * C,
                    skip_runtime_bounds_check_because="the router clamps it")[1]

            def expert_turn(i):
                _, woff = nc.values_load_multi_w_load_instructions(
                    ex_w[0:1, ds(i * RING, RING)], engines=[DVE_], min_val=0, max_val=(NE - 1) * 2048,
                    skip_runtime_bounds_check_because="the router clamps it")
                first = isinstance(i, int)
                boff = [None, None, *bias_offsets(0, RING - 2)] if first else bias_offsets(i * RING - 2, RING)
                for k in range(RING):
                    await_ge(dve, h_mm, i * RING + k)
                    expert_weights(woff[k])
                    dve.wait_ge(x_mm, i * RING + (k + 1))
                    nc.vector.tensor_copy(tT[:, k % 2, :, :].rearrange("p k n -> p (k n)"), bank[k % 2][:, 0:C]).then_inc(x_out, 1)
                    if k >= 2:
                        add_output_bias(i, k - 2, boff[k])
                    elif not first:
                        add_output_bias(i - 1, k - 2 + RING, boff[k])

            turns_of(dve, 0, SLOTS // RING, expert_turn)
            boff = bias_offsets(SLOTS - 2, 2)
            for k in range(2):
                add_output_bias(SLOTS // RING - 1, RING - 2 + k, boff[k])
            nc.vector.memset(slot[0:1, 191:192], 0.0).then_inc(y_used, GT)
            for i in range(NT // GT):
                for j in range(GT):
                    dve.wait_ge(y_ld[j], i * 32 + 32)
                    dve.wait_ge(fz, i * GT + (j + 1))
                    step(nc.vector.scalar_tensor_tensor(zb[0:B, j, :], yb[0:B, 0, j, :], pair_w[0:B, 0, ds(i * GT + j, 1)], zb[0:B, j, :],
                                                        ALU.mult, ALU.add))
                    nc.vector.scalar_tensor_tensor(zb[0:B, j, :], yb[0:B, 1, j, :], pair_w[0:B, 1, ds(i * GT + j, 1)], zb[0:B, j, :],
                                                   ALU.mult, ALU.add).then_inc(y_used, 1)
                    dve.wait_ge(y_used, i * GT + (GT + j + 1))
                    step(nc.vector.bn_stats(bn6[0:B, :], zb[0:B, j, :]))
                    step(nc.vector.bn_aggr(mv5[0:B, j, :], bn6[0:B, :]))
                nc.vector.tensor_scalar(st5[0:B, 0, :], mv5[0:B, :, 1], LN_EPS, None, ALU.add).then_inc(fin_var, 1)
                dve.wait_ge(fin_root, i + 1)
                norm_scale(step, fin_scale)
                for j in range(GT):
                    dve.wait_ge(fin_aff, i * GT + (j + 1))
                    await_ge(dve, out_put[j], i * 16)
                    nc.vector.tensor_tensor(ob[0:B, j, :], ub[0:B, j, :], X[0:B, ds(i * GT + j, 1), :].rearrange("p a c -> p (a c)"),
                                            ALU.add).then_inc(fin_out, 1)

        def rank_products(pe, rounds, P, nb):
            pe.wait_ge(rank_rows, rounds)
            mine = small[0:P, 1, 0:nb]
            nc.tensor.matmul(bank[6][0:P, 0:nb], tri[0:P, 0:P], mine, start=True, stop=True)
            nc.tensor.matmul(bank[6][0:P, 32:32 + nb], ones[0:P, 0:P], mine, start=True, stop=True).then_inc(rank_sums, 1)

        def clear_banks(which, cols):
            for b in which:
                ins = nc.tensor.matmul(bank[b][:, 0:cols], zeros[:, 0:128], zeros[:, 0:cols], start=True, stop=True)
            return ins

        def sort_product(pe, n, s, H):
            pe.wait_ge(loads_made, n)
            for b in range(2):
                ins = nc.tensor.matmul(bank[b][:, 0:H], s_lo[:, s, b, :], s_hi[:, s, 0:H], start=False, stop=True,
                                       skip_group_check=True)
            ins.then_inc(hots_used, 1)

        def attention_fold_pe(pe):
            accumulate_keys(pe, NT - 1)
            pe.wait_ge(kv_sums, 1)
            for j in range(KC):
                ins = nc.tensor.matmul(bank[1][:, j * 128:(j + 1) * 128], kvsum[:, j, :], ident[:, :], start=True, stop=True)
            ins.then_inc(kv_sums_row, 1)
            pe.wait_ge(kvT_ready, 1)
            for j in range(KC):
                ins = nc.tensor.matmul(bank[4][:, j * C:(j + 1) * C], kvT[:, j, :], mw1[:, j, :], start=True, stop=True)
            ins.then_inc(kvw1_mm, 1)
            pe.wait_ge(kvw1_out, 1)
            for m in range(KC):
                for j in range(KC):
                    nc.tensor.matmul(bank[0][:, m * C:(m + 1) * C], wqT[:, j, m * 128:(m + 1) * 128], kvw1[:, j, :],
                                     start=(j == 0), stop=(j == KC - 1))
            for m in range(KC):
                for j in range(KC):
                    ins = nc.tensor.matmul(bank[1][:, 256 + m:257 + m], kvw1[:, j, m * 128:(m + 1) * 128], bcol[:, 64 + j:65 + j],
                                           start=(j == 0), stop=(j == KC - 1))
            ins.then_inc(weff_mm, 1)
            pe.wait_ge(weff_out, 1)

        def accumulate_keys(pe, tile):
            pe.wait_ge(kv_norm, tile + 1)
            for j in range(KC):
                kj, vj = (kvn[0:B, s, 4 * j:4 * j + 4, :].rearrange("p h d -> p (h d)") for s in range(2))
                for a, side, lo_, n in ((vj, kj, j * 128, 128), (vj, ones[0:B, 0:1], 256 + j, 1), (kj, ones[0:B, 0:1], 260 + j, 1)):
                    ins = nc.tensor.matmul(bank[6][:, lo_:lo_ + n], a, side, start=False, stop=True, skip_group_check=True)
            ins.then_inc(kv_used, 1)

        @block.tensor
        def _(pe):
            pe.wait_ge(consts, 1)
            clear_banks((0, 1), HMAX).then_inc(hots_used, SR)
            nc.tensor.matmul(bank[7][0:1, 1:2], zeros[:, 0:1], zeros[:, 0:1], start=True, stop=True).then_inc(chunk_done, RING)
            rank_products(pe, 1, 128, NT)
            T = T_OF[0]
            with pe.Fori(0, T // SR) as i:
                for s in range(SR):
                    sort_product(pe, i * SR + s + 1, s, H_OF[0])
            for j in range(T // SR * SR, T):
                sort_product(pe, j + 1, j % SR, H_OF[0])
            nc.tensor.matmul(bank[7][0:1, 0:1], zeros[:, 0:1], zeros[:, 0:1], start=True, stop=True).then_inc(sorted_, 1)
            pe.wait_ge(xn_ready, 1)
            for t in range(NT):
                if t >= 2:
                    pe.wait_ge(xn_t_out, t - 1)
                for k in range(KC):
                    ins = nc.tensor.transpose(bank[4 + t % 2][:, k * B:(k + 1) * B], xn[0:B, t, k * 128:(k + 1) * 128],
                                              ident[0:B, 0:B])
                ins.then_inc(xn_t, 1)
            pe.wait_ge(ld_w, 16 * W_LOADS)
            pe.wait_ge(xn_t_out, NT)
            for t in range(NT):
                if t >= 2:
                    pe.wait_ge(tab_out, t - 1)
                for k in range(KC):
                    ins = nc.tensor.matmul(bank[2 + t % 2][0:B, 0:C], xnT[:, k, t * B:(t + 1) * B], wgnn[:, k, :],
                                           start=(k == 0), stop=(k == KC - 1))
                ins.then_inc(tab_mm, 1)
            pe.wait_ge(ld_b, 16 * B_LOADS)
            pe.wait_ge(wcen_ready, 1)
            for j in range(KC):
                for k in range(KC):
                    nc.tensor.transpose(bank[5][:, j * C + k * 128:j * C + (k + 1) * 128], weff[:, k, j * 128:(j + 1) * 128],
                                        ident[:, :])
            nc.tensor.transpose(bank[4][:, 0:70], brow[0:70, :], ident[0:70, 0:70]).then_inc(setup_t, 1)
            rank_products(pe, 2, 128, NT)
            rank_products(pe, 3, 128, NT)
            pe.wait_ge(group_ready, 1)
            clear_banks((0, 1), HMAX)
            pe.wait_ge(hots_made, T_OF[0])
            pe.wait_ge(setup_t_out, 1)
            pe.wait_ge(routed, 1)
            clear_banks((6,), 262)
            for g, turns, turn0, nsort, mix, tile0 in SEGS:
                c0 = CHUNK0[g] + RING * turn0
                if g == 1 and turn0 == 0:
                    pe.wait_ge(group_ready, g + 1)
                    clear_banks((0, 1), HMAX)
                if g == 1 and turn0 == SORT_TURNS[g]:
                    attention_fold_pe(pe)
                col0 = AT[g + 1] + nsort * turn0 if nsort else 0
                split = shares(nsort, RING)

                def turn(i):
                    m = 0
                    for k in range(RING):
                        pe.wait_ge(hot_ready, i * RING + (c0 + k + 1))
                        pe.wait_ge(gathered[k], i * 16 + (c0 // RING + 1) * 16)
                        if k % 2 == 0:
                            pe.wait_ge(chunk_added, i * RING + (c0 + k + 2))
                        nc.tensor.matmul(bank[CHUNK_BANKS[k // 2]][:, k % 2 * C:(k % 2 + 1) * C], hot[:, k, :], rows[:, k, :],
                                         start=True, stop=True).then_inc(chunk_done, 1)
                        for _ in range(split[k]):
                            if m >= LAG:
                                sort_product(pe, i * nsort + (col0 + m - LAG + 1), (m - LAG) % SR, H_OF[g + 1])
                            elif turn0:
                                sort_product(pe, i * nsort + (col0 + m - LAG + 1), (m - LAG) % SR, H_OF[g + 1])
                            m += 1
                        if mix == 1 and k == 2:
                            await_ge(pe, kv_sb, i + tile0)
                            pe.wait_ge(xst_ready, i + (tile0 + 1))
                            for kc in range(KC):
                                wkv = wcen[:, kc, :].rearrange("p (h c) -> p h c", h=HEADS)[:, :, HD:3 * HD]
                                ins = nc.tensor.matmul(bank[4][0:B, :], xst[:, kc, :],
                                                       wkv, start=(kc == 0), stop=(kc == KC - 1))
                            ins.then_inc(kv_mm, 1)
                        if mix == 1 and k == 3 and not (isinstance(i, int) and i + tile0 == 0):
                            accumulate_keys(pe, i + (tile0 - 1))
                        if mix == 2 and k == 0:
                            await_ge(pe, mh_out, i + tile0)
                            for m2 in range(KC):
                                for kc in range(KC):
                                    ins = nc.tensor.matmul(bank[4][:, m2 * B:(m2 + 1) * B], weff[:, kc, m2 * 128:(m2 + 1) * 128],
                                                           xnT[:, kc, ds((i + tile0) * B, B)], start=(kc == 0), stop=(kc == KC - 1))
                            ins.then_inc(mh_mm, 1)
                        if mix == 2 and k == 4:
                            pe.wait_ge(mh_out, i + (tile0 + 1))
                            await_ge(pe, my_out, i + tile0)
                            for kc in range(KC):
                                ins = nc.tensor.matmul(bank[0][0:B, 0:C], mhT[:, kc, :], mw2[:, kc, :],
                                                       start=(kc == 0), stop=(kc == KC - 1))
                            ins.then_inc(my_mm, 1)
                if turns == 1:
                    turn(0)
                else:
                    with pe.Fori(0, turns) as i:
                        turn(i)
                if nsort and turn0 + turns == SORT_TURNS[g]:
                    for m in range(LAG):
                        sort_product(pe, AT[g + 1] + T_OF[g + 1] - LAG + m + 1, (m - LAG) % SR, H_OF[g + 1])
                    nc.tensor.matmul(bank[1][0:1, 500:501], zeros[:, 0:1], zeros[:, 0:1], start=False, stop=True,
                                     skip_group_check=True).then_inc(sorted_, 1)
            def mid_transpose(i, j):
                pe.wait_ge(mid_norm, i * GT + (j + 1))
                await_ge(pe, mt_out, i * GT + max(j - 1, 0))
                for k in range(KC):
                    ins = nc.tensor.transpose(bank[4 + j % 2][:, k * B:(k + 1) * B], rows[0:B, j, k * 128:(k + 1) * 128], ident[0:B, 0:B])
                ins.then_inc(mt_mm, 1)

            def middle_turn(i):
                mid_transpose(i, 0)
                for j in range(GT):
                    if j + 1 < GT:
                        mid_transpose(i, j + 1)
                    pe.wait_ge(mt_out, i * GT + (j + 1))
                    await_ge(pe, mg_out, i * GT + max(j - 1, 0))
                    for k in range(KC):
                        ins = nc.tensor.matmul(bank[6 + j % 2][0:B, 0:NE], tT[:, j % 2, k, 0:B], gate[:, k, :],
                                               start=(k == 0), stop=(k == KC - 1))
                    ins.then_inc(mg_mm, 1)

            turns_of(pe, 0, NT // GT, middle_turn)
            pe.wait_ge(mg_out, NT)
            rank_products(pe, 4, B, NE)

            def pair_product(n, s, first):
                pe.wait_ge(pairs_made, n)
                for b in range(2):
                    ins = nc.tensor.matmul(bank[b][:, 0:SLOTS], p_lo[0:B, s, b, :], p_hi[0:B, s, :], start=first, stop=True,
                                           skip_group_check=True)
                ins.then_inc(pairs_used, 1)

            for k in range(2):
                pair_product(k * NT + 1, 0, k == 0)
                with pe.Fori(0, (NT - 1) // PR) as i:
                    for s in range(PR):
                        pair_product(i * PR + (k * NT + 2 + s), s, False)
            pe.wait_ge(slots_ready, 1)

            def tokens_transposed(i, k):
                pe.wait_ge(tok_got[k], i * 16 + 16)
                await_ge(pe, x_out, i * RING + max(k - 1, 0))
                for c in range(KC):
                    ins = nc.tensor.transpose(bank[k % 2][:, c * 128:(c + 1) * 128], rows[:, k, c * 128:(c + 1) * 128], ident[:, :])
                ins.then_inc(x_mm, 1)

            def second_product(turn, k, off):
                pe.wait_ge(h_out, turn * RING + (k + 1))
                if not (isinstance(turn, int) and turn == 0 and k < 2):
                    pe.wait_ge(y_out, turn * RING + (k - 1))
                for m in range(KF):
                    ins = nc.tensor.matmul(bank[4 + k % 2][:, 0:C], hT[:, k % 2, m, :], slab[:, ds(off + (1024 + m * C), C)],
                                           start=(m == 0), stop=(m == KF - 1))
                ins.then_inc(y_mm, 1)

            def weight_offsets(start, n):
                return nc.values_load_multi_w_load_instructions(
                    ex_w[0:1, ds(start, n)], engines=[PE_], min_val=0, max_val=(NE - 1) * 2048,
                    skip_runtime_bounds_check_because="the router clamps it")[1]

            def expert_turn(i, last):
                first = isinstance(i, int) and i == 0
                woff = [None, *weight_offsets(0, RING - 1)] if first else weight_offsets(i * RING - 1, RING)
                for k in range(RING):
                    pe.wait_ge(w_copied, i * RING + (k + 1))
                    pe.wait_ge(x_out, i * RING + (k + 1))
                    for m in range(KF):
                        for c in range(KC):
                            ins = nc.tensor.matmul(bank[2 + k % 2][:, m * 128:(m + 1) * 128], w1c[:, c, m * 128:(m + 1) * 128],
                                                   tT[:, k % 2, c, :], start=(c == 0), stop=(c == KC - 1))
                    ins.then_inc(h_mm, 1)
                    if k + 1 < RING:
                        tokens_transposed(i, k + 1)
                    elif not last:
                        tokens_transposed(i + 1, 0)
                    if k:
                        second_product(i, k - 1, woff[k])
                    elif not first:
                        second_product(i - 1, RING - 1, woff[k])

            tokens_transposed(0, 0)
            turns_of(pe, 0, SLOTS // RING, lambda i: expert_turn(i, False), lambda i: expert_turn(i, True))
            second_product(SLOTS // RING - 1, RING - 1, weight_offsets(SLOTS - 1, 1)[0])


_INS = ["x", "src", "dst", "edge_weight", "L0_gnn_weight_mat", "L0_gnn_bias_vec", "L0_mix_w_qkv", "L0_mix_b_qkv",
        "L0_mix_kln_g", "L0_mix_kln_b", "L0_mix_vln_g", "L0_mix_vln_b", "L0_mix_w1", "L0_mix_b1", "L0_mix_w2",
        "L0_mix_b2", "L0_ffn_gate_w", "L0_ffn_gate_b", "L0_ffn_w1", "L0_ffn_b1", "L0_ffn_w2", "L0_ffn_b2",
        "L0_ffn_gamma", "L0_ffn_beta"]


def kernel(**inputs):
    import numpy as np
    import concourse.bacc as bacc
    from concourse import mybir
    from concourse.bass_utils import run_bass_kernel_spmd

    nc = bacc.Bacc("TRN2", target_bir_lowering=False, num_devices=1)
    arrays, args = {}, []
    for name in _INS:
        a = np.ascontiguousarray(inputs[name])
        arrays[f"in_{name}"] = a
        args.append(nc.dram_tensor(f"in_{name}", a.shape, mybir.dt.from_np(a.dtype), kind="ExternalInput").ap())
    out = nc.dram_tensor("out", arrays["in_x"].shape, mybir.dt.float32, kind="ExternalOutput").ap()
    graph_transformer_layer(nc, *args, out)
    r = run_bass_kernel_spmd(nc, [arrays], core_ids=[0])
    return r.results[0]["out"]
```

```python
from contextlib import ExitStack, contextmanager


class Steps:

    def __init__(self, engine, semaphore):
        self.engine, self.semaphore, self.done, self.turn = engine, semaphore, 0, None

    def mark(self, instruction):
        instruction.then_inc(self.semaphore, 1)
        self.done += 1

    def wait(self):
        self.engine.wait_ge(self.semaphore, self.done if self.turn is None else self.turn + self.done)

    def wait_for(self, step):
        self.engine.wait_ge(self.semaphore, step)

    def __call__(self, instruction):
        self.mark(instruction)
        self.wait()

    @contextmanager
    def loop(self, turns, marks):
        start = self.done
        with self.engine.Fori(0, turns) as i:
            self.turn = i * marks
            yield i
            assert self.done - start == marks, self.done - start
        self.turn, self.done = None, start + turns * marks


def await_ge(engine, semaphore, value):
    if not isinstance(value, int) or value > 0:
        engine.wait_ge(semaphore, value)


def turns_of(engine, first, count, body, last=None):
    if first == 0:
        body(0)
        first = 1
    end = count - (last is not None)
    if end > first:
        with engine.Fori(first, end) as i:
            body(i)
    if last is not None:
        last(count - 1)


def shares(n, parts):
    return [(n * (k + 1)) // parts - (n * k) // parts for k in range(parts)]


def graph_transformer_layer(nc, x, src, dst, edge_weight, gnn_w, gnn_b, w_qkv, b_qkv, kln_g, kln_b, vln_g, vln_b,
                            mix_w1, mix_b1, mix_w2, mix_b2, gate_w, gate_b, w1, b1, w2, b2, gamma, beta, out):
    import concourse.bass as bass
    from concourse import mybir

    F32, I32, U32 = mybir.dt.float32, mybir.dt.int32, mybir.dt.uint32
    ALU, ACT, AX = mybir.AluOpType, mybir.ActivationFunctionType, mybir.AxisListType
    PE_, DVE_, ACT_ = mybir.EngineType.PE, mybir.EngineType.DVE, mybir.EngineType.Activation
    ds = bass.ds

    N, C = x.shape
    E = src.shape[0]
    NE, _, F = w1.shape
    B, NT = 125, N // 125
    KC, KF = C // 128, F // 128
    HEADS, HD = 8, 32
    assert N == B * NT and NT * 4195 < 2 ** 24
    COLS = -(-E // 128)
    FULL = E // 128
    EPS, LN_EPS, MAXNORM = 1e-15, 1e-5, 1.0 - 1e-5

    RING = 8
    T_OF = [119, 136, 136]
    assert sum(T_OF) == COLS
    AT = [0, T_OF[0], T_OF[0] + T_OF[1]]
    H_OF = [-(-(t + NT - 1) // RING) * RING for t in T_OF]
    TURNS = [h // RING for h in H_OF]
    HMAX = max(H_OF)
    CHUNK0 = [0, H_OF[0], H_OF[0] + H_OF[1]]
    CHUNKS = sum(H_OF)
    SORT_TURNS = [17, 17]
    SORT = [T_OF[1] // SORT_TURNS[0], T_OF[2] // SORT_TURNS[1]]
    assert SORT[0] * SORT_TURNS[0] == T_OF[1] and SORT[1] * SORT_TURNS[1] == T_OF[2]
    SEGS = [(0, 1, 0, SORT[0], 0, 0, 0),
            (0, SORT_TURNS[0] - 1, 1, SORT[0], 0, 0, 0),
            (0, TURNS[0] - SORT_TURNS[0], SORT_TURNS[0], 0, 0, 0, 0),
            (1, 1, 0, SORT[1], 0, 0, 0),
            (1, 9, 1, SORT[1], 0, 0, 0),
            (1, 1, 10, SORT[1], 1, 1, 0),
            (1, 6, 11, SORT[1], 1, 1, 1),
            (1, 3, 17, 0, 1, 2, 7),
            (2, 6, 0, 0, 1, 2, 13),
            (2, 1, 6, 0, 2, 2, 0),
            (2, 11, 7, 0, 2, 2, 2),
            (2, 1, 18, 0, 2, 1, 24),
            (2, 1, 19, 0, 0, 0, 0)]
    for attention_pass in (1, 2):
        assert sum(turns * tiles for _, turns, _, _, m, tiles, _ in SEGS if m == attention_pass) == NT
    assert [sum(s[1] for s in SEGS if s[0] == g) for g in range(3)] == TURNS
    PLACES = {1: dict(columns=0, project=2, out=4, square=5, variance=0, root=1, norm=2, sums=3,
                      hidden=0, gelu=2, second=4, add=6),
              2: dict(columns=0, project=1, out=3, square=3, variance=0, root=1, norm=2, sums=3,
                      hidden=0, gelu=1, second=2, add=3)}
    BEHIND = ("variance", "root", "norm", "sums")

    def attention_steps(tiles, k, i, tile0):
        for h in range(tiles):
            for name, place in PLACES[tiles].items():
                if h * (RING // tiles) + place == k:
                    tile = i * tiles + (tile0 + h - (name in BEHIND))
                    if not (isinstance(tile, int) and tile < 0):
                        yield name, tile

    CHUNK_BANKS = [2, 3, 5, 7]
    GT = 5
    assert NT % GT == 0
    SR = 8
    LAG = 4
    assert all(n % SR == 0 for n in SORT)

    PAIRS = 2 * NT
    SLOTS = (2 * N + NE * 127) // 128
    assert SLOTS % RING == 0 and SLOTS == 64
    PR = 8
    YROWS = 2 * N + 128 * SLOTS

    table = nc.dram_tensor("table", (N, C), F32).ap()
    tokens = nc.dram_tensor("tokens", (N, C), F32).ap()
    pair_out = nc.dram_tensor("pair_out", (YROWS, C), F32).ap()

    ctx = ExitStack()
    with ctx:
        def sb(name, shape, dt=F32):
            return ctx.enter_context(nc.sbuf_tensor(name, shape, dt))

        def sem(name):
            return ctx.enter_context(nc.semaphore(name))

        slab = sb("slab", [128, NE * 2048])
        used = [0]

        def part(of, shape, count=used, base=slab):
            n = 1
            for d in shape:
                n *= d
            a = base[:, count[0]:count[0] + n]
            count[0] += n
            assert count[0] <= base.shape[1]
            names = "abc"[:len(shape)]
            return a if len(shape) == 1 else a.rearrange(
                f"p ({' '.join(names)}) -> p {' '.join(names)}", **dict(zip(names[:-1], shape)))

        xnT = part("xnT", [KC, N])
        work = part("work", [2 * HMAX * NT])
        rt_one, rt_sum = work[:, 0:HMAX * NT], work[:, HMAX * NT:2 * HMAX * NT]
        wqkv = part("wqkv", [KC, 3 * C])
        wcen = part("wcen", [KC, 3 * C])
        wgnn = part("wgnn", [KC, C])
        mw1 = part("mw1", [KC, C])
        mw2 = part("mw2", [KC, C])
        weff = part("weff", [KC, C])
        wqT = part("wqT", [KC, C])
        looped = [0]
        kvw1 = part("kvw1", [KC, C], looped, work)
        kvT = part("kvT", [KC, 128], looped, work)
        kvsum = part("kvsum", [KC, 128], looped, work)
        kvc = part("kvc", [HEADS, 2, HD], looped, work)
        kvs = part("kvs", [HEADS, 2, HD], looped, work)
        xst = part("xst", [KC, B], looped, work)
        kvn = part("kvn", [2, HEADS, HD], looped, work)
        hot = part("hot", [RING, 128], looped, work)
        mhT = part("mhT", [KC, B], looped, work)
        s_one = part("s_one", [SR, 128])
        s_hi = part("s_hi", [SR, HMAX])
        s_load = part("s_load", [SR, 2 * HMAX])
        bias_kv = part("bias_kv", [HEADS, 3 * HD])
        ln_g = part("ln_g", [2, HD])
        ln_b = part("ln_b", [2, HD])
        mb2 = part("mb2", [C])
        ew, pack, lo = part("ew", [COLS]), part("pack", [COLS]), part("lo", [COLS])
        key = hi = part("hi", [COLS])
        zeros = part("zeros", [256])
        brow = part("brow", [128])
        g_row = part("g_row", [CHUNKS]).bitcast(I32)
        g_lo, g_w = part("g_lo", [CHUNKS]), part("g_w", [CHUNKS])

        X = sb("X", [128, NT, C])
        acc = sb("acc", [128, NT, C])
        xn = tout = acc
        accf = acc[:, :, :].rearrange("p t c -> p (t c)")
        later = [0]
        b2b = part("b2b", [NE, C], later, accf)
        w1c = part("w1c", [KC, F], later, accf)
        hT = part("hT", [2, KF, 128], later, accf)
        p_one = hT[:, :, :, :].rearrange("p a k n -> p (a k) n")
        assert 2 * KF == PR and KC * F == PR * 2 * SLOTS
        p_load = w1c[:, :, :].rearrange("p k n -> p (k n)").rearrange("p (r n) -> p r n", r=PR)
        final = [0]
        yb = part("yb", [2, NT, C], final)
        zb = part("zb", [NT, C], final)
        ub = part("ub", [NT, C], final)
        gam, bet = w1c[:, 0, 0:C], w1c[:, 1, 0:C]

        rows = sb("rows", [128, RING, C])
        p_hi = rows[:, 0:PR * SLOTS // C, :].rearrange("p k c -> p (k c)").rearrange("p (r n) -> p r n", r=PR)
        early = rows[:, :, :].rearrange("p k c -> p (k c)").bitcast(I32)
        esrc, edst, eq = (early[:, j * COLS:(j + 1) * COLS] for j in range(3))
        slot = sb("slot", [128, 192])
        marker = sb("marker", [1, 1])
        slot_i = sb("slot_i", [128, HMAX], I32)
        slot_j = sb("slot_j", [128, HMAX], I32)
        small = sb("small", [128, 6, 32])
        cnt_i = sb("cnt_i", [128, 32], I32)
        bk = sb("bk", [1, CHUNKS], I32)
        idx = sb("idx", [128, RING], I32)
        iota = sb("iota", [128, HMAX])
        slot_id = sb("slot_id", [128, SLOTS])
        tT = sb("tT", [128, 2, KC, 128])
        yv = sb("yv", [128, 2, C])
        bias_ring = [yv[0:B, 0, :], yv[0:B, 1, :], *(tT[0:B, j, :, :].rearrange("p k n -> p (k n)") for j in range(2))]
        odx = sb("odx", [128, RING], I32)
        pair_key = sb("pair_key", [128, 2, NT])
        pair_lo = sb("pair_lo", [128, PAIRS])
        pair_hi = sb("pair_hi", [128, PAIRS])
        pair_row = sb("pair_row", [128, 2, NT])
        s_tok = sb("s_tok", [128, SLOTS], I32)
        s_row = sb("s_row", [128, SLOTS], I32)
        s_tmp = sb("s_tmp", [128, 2, SLOTS])
        ex_w = sb("ex_w", [1, SLOTS], I32)
        ex_b1 = sb("ex_b1", [1, SLOTS], I32)
        ex_b2 = sb("ex_b2", [1, SLOTS], I32)
        lg = sb("lg", [128, GT, NE])
        mx = sb("mx", [128, NT, 8])
        ix = sb("ix", [128, NT, 8], U32)
        topv = sb("topv", [128, 2, NT])
        pair_w = sb("pair_w", [128, 2, NT])
        mid_rs = sb("mid_rs", [128, NT])
        mid_nb = sb("mid_nb", [128, NT])
        tri = sb("tri", [128, 128])
        ident = sb("ident", [128, 128])
        ones = sb("ones", [128, 128])
        node2 = sb("node2", [128, 2, NT])
        gb = sb("gb", [128, C])
        gate = sb("gate", [128, KC, NE])
        gateb = sb("gateb", [128, NE])
        bcol = sb("bcol", [128, 70])
        beff = sb("beff", [128, KC])
        kvst = sb("kvst", [128, 4, 16])
        bn6 = sb("bn6", [128, NT, 6])
        chunk_id = sb("chunk_id", [128, 2])
        unused = sb("unused", [1, 1])
        bucket = sb("bucket", [128, 2])
        mv = sb("mv", [128, NT, 2])
        st = sb("st", [128, 16, NT + 1])
        wmean = sb("wmean", [128, KC, 3 * HEADS])

        bank = [ctx.enter_context(nc.psum_tensor(f"bank{i}", [128, 512], F32)) for i in range(8)]

        pads, ld_edge, ld_x, ld_w, ld_b = sem("pads"), sem("ld_edge"), sem("ld_x"), sem("ld_w"), sem("ld_b")
        consts = sem("consts")
        dve_step, pool_step = sem("dve_step"), sem("pool_step")
        rank_rows, rank_sums = sem("rank_rows"), sem("rank_sums")
        hots_made, loads_made, hots_used, sorted_ = sem("hots_made"), sem("loads_made"), sem("hots_used"), sem("sorted_")
        var_ready, sqrt_done, squares = sem("var_ready"), sem("sqrt_done"), sem("squares")
        xn_ready, ln_arg, ln_done, row_scale = sem("xn_ready"), sem("ln_arg"), sem("ln_done"), sem("row_scale")
        xn_t, xn_t_out, tab_mm, tab_out, tab_stored = (sem("xn_t"), sem("xn_t_out"), sem("tab_mm"), sem("tab_out"),
                                                       sem("tab_stored"))
        wcen_ready, setup_t, setup_t_out = sem("wcen_ready"), sem("setup_t"), sem("setup_t_out")
        x_plus, acc_zero = sem("x_plus"), sem("acc_zero")
        group_ready, routed = sem("group_ready"), sem("routed")
        may_go = sem("may_go")
        idx_ready = sem("idx_ready")
        gathered = [sem(f"gathered{k}") for k in range(RING)]
        hot_ready, chunk_done, chunk_added = sem("hot_ready"), sem("chunk_done"), sem("chunk_added")
        kv_mm, kv_sb, kv_sq, kv_norm, kv_used = sem("kv_mm"), sem("kv_sb"), sem("kv_sq"), sem("kv_norm"), sem("kv_used")
        xst_ready = sem("xst_ready")
        kv_var, kv_std = sem("kv_var"), sem("kv_std")
        kv_sums, kv_sums_row = sem("kv_sums"), sem("kv_sums_row")
        kvT_ready, kvw1_mm, kvw1_out, weff_mm, weff_out = (sem("kvT_ready"), sem("kvw1_mm"), sem("kvw1_out"),
                                                           sem("weff_mm"), sem("weff_out"))
        mh_mm, mh_out, my_mm, my_out = sem("mh_mm"), sem("mh_out"), sem("my_mm"), sem("my_out")

        tail_dot = sem("tail_dot")
        tail_ss, tail_sq, tail_tanh, tail_v = sem("tail_ss"), sem("tail_sq"), sem("tail_tanh"), sem("tail_v")
        mid_var, mid_root, mid_scale, mid_norm = sem("mid_var"), sem("mid_root"), sem("mid_scale"), sem("mid_norm")
        tok_stored, mt_mm, mt_out, mg_mm, mg_out = sem("tok_stored"), sem("mt_mm"), sem("mt_out"), sem("mg_mm"), sem("mg_out")
        gb_added, ld_gb, ld_moe, ld_b2 = sem("gb_added"), sem("ld_gb"), sem("ld_moe"), sem("ld_b2")
        factors, gb_scaled = sem("factors"), sem("gb_scaled")
        exp_arg, exp_done = sem("exp_arg"), sem("exp_done")
        rows_known, pair_loads = sem("rows_known"), sem("pair_loads")
        pairs_made, pairs_used, slots_ready = sem("pairs_made"), sem("pairs_used"), sem("slots_ready")
        tok_idx, out_idx = sem("tok_idx"), sem("out_idx")
        tok_got = [sem(f"tok_got{k}") for k in range(RING)]
        y_put = [sem(f"y_put{k}") for k in range(RING)]
        x_mm, x_out, w_copied, h_mm, h_out, y_mm, y_out = (sem("x_mm"), sem("x_out"), sem("w_copied"), sem("h_mm"),
                                                           sem("h_out"), sem("y_mm"), sem("y_out"))
        y_ld = [sem(f"y_ld{j}") for j in range(GT)]
        tokens_again, fin_var, fin_root, fin_scale, fin_norm, fin_aff, fin_out = (
            sem("tokens_again"), sem("fin_var"), sem("fin_root"), sem("fin_scale"), sem("fin_norm"), sem("fin_aff"),
            sem("fin_out"))
        out_put, beta_added = sem("out_put"), sem("beta_added")

        block = ctx.enter_context(nc.Block())

        x_t = x.rearrange("(t p) c -> p t c", p=B)
        out_t = out.rearrange("(t p) c -> p t c", p=B)
        table_t = table.rearrange("(t p) c -> p t c", p=B)

        y_t = pair_out[0:2 * N, :].rearrange("(k t p) c -> k p t c", k=2, p=B)

        def edge_whole(a):
            return a[0:128 * FULL].rearrange("(p j) -> p j", j=FULL)

        def edge_rest(a):
            return a[128 * FULL:E].rearrange("(p j) -> p j", j=1)

        def row(v):
            return v.rearrange("(a n) -> a n", a=1)

        W_LOADS, B_LOADS = 5, 14
        @block.sync
        def _(sp):
            sp.wait_ge(pads, 3)
            for a, t in ((src, esrc), (dst, edst), (edge_weight, ew)):
                sp.dma_start(t[:, 0:FULL], edge_whole(a)).then_inc(ld_edge, 16)
                with nc.allow_non_contiguous_dma(reason="the last few edges, one a partition"):
                    sp.dma_start(t[0:E - 128 * FULL, FULL:FULL + 1], edge_rest(a)).then_inc(ld_edge, 16)
            sp.dma_start(X[0:112, :, :], x_t[0:112]).then_inc(ld_x, 16)
            sp.dma_start(X[112:B, :, :], x_t[112:B]).then_inc(ld_x, 16)
            for t, a in ((wgnn, gnn_w), (wqkv, w_qkv), (mw1, mix_w1), (mw2, mix_w2), (gate, gate_w)):
                sp.dma_start(t[:, :, :], a.rearrange("(k p) n -> p k n", p=128)).then_inc(ld_w, 16)
            for q in range(NT // GT):
                t = slice(q * GT, (q + 1) * GT)
                sp.wait_ge(tab_out, (q + 1) * GT)
                sp.dma_start(table_t[:, t, :], tout[0:B, t, :]).then_inc(tab_stored, 16)

            sp.wait_ge(chunk_done, RING + CHUNKS)
            sp.wait_ge(my_out, NT)
            for e in range(NE):
                half = slab[:, e * 2048:(e + 1) * 2048]
                sp.dma_start(half[:, 0:1024].rearrange("p (k n) -> p k n", k=KC),
                             w1[e].rearrange("(k p) n -> p k n", p=128)).then_inc(ld_moe, 16)
                sp.dma_start(half[:, 1024:2048].rearrange("p (k n) -> p k n", k=KF),
                             w2[e].rearrange("(k p) n -> p k n", p=128)).then_inc(ld_moe, 16)
            for q in range(NT // GT):
                t = slice(q * GT, (q + 1) * GT)
                sp.wait_ge(mid_norm, (q + 1) * GT)
                sp.dma_start(tokens.rearrange("(t p) c -> p t c", p=B)[:, t, :], acc[0:B, t, :]).then_inc(tok_stored, 16)
            sp.wait_ge(tok_stored, 16 * (NT // GT))
            sp.wait_ge(mt_mm, NT)
            sp.dma_start(b2b[:, :, :].rearrange("p e c -> p (e c)"), b2.rearrange("(a e) c -> a (e c)", a=1).to_broadcast([128, NE * C])).then_inc(ld_b2, 16)
            sp.wait_ge(h_mm, SLOTS)
            for t, a in ((gam, gamma), (bet, beta)):
                sp.dma_start(t, row(a).to_broadcast([128, C])).then_inc(ld_gb, 16)
            for k in range(RING):
                sp.wait_ge(y_put[k], 16 * SLOTS // RING)
            sp.wait_ge(y_out, SLOTS)
            for q in range(NT // GT):
                t = slice(q * GT, (q + 1) * GT)
                sp.dma_start(yb[0:B, 0, t, :], y_t[0, :, t, :]).then_inc(y_ld[q], 16)
            for q in range(NT // GT):
                t = slice(q * GT, (q + 1) * GT)
                sp.wait_ge(fin_out, (q + 1) * GT)
                sp.dma_start(out_t[:, t, :], ub[0:B, t, :]).then_inc(out_put, 16)
            sp.wait_ge(out_put, 16 * (NT // GT))

        def attention_fold_act(act):
            act.wait_ge(kv_var, NT)
            nc.scalar.activation(kvst[0:B, 1, :], kvst[0:B, 0, :], ACT.Sqrt).then_inc(kv_std, 1)
            act.wait_ge(kvw1_mm, 1)
            nc.scalar.activation(kvw1[:, :, :].rearrange("p k n -> p (k n)"), bank[4][:, :], ACT.Copy).then_inc(kvw1_out, 1)

        def hold_table(function):
            nc.scalar.activation(unused[:, :], ones[0:1, 0:1], function)

        def on_vector(s):
            return s % 4 == 3

        def sort_loads(act, j, n, s, H, edges_made=False):
            act.wait_ge(hots_made, n)
            if not edges_made:
                nc.scalar.activation(s_load[:, s, 0:H], s_hi[:, s, 0:H], ACT.Copy, scale=pack[:, ds(j, 1)])
            nc.scalar.activation(s_load[:, s, H:2 * H], s_hi[:, s, 0:H], ACT.Copy, scale=ew[:, ds(j, 1)]).then_inc(loads_made, 1)

        @block.scalar
        def _(act):
            act.dma_start(bias_kv[:, :, :].rearrange("p h c -> p (h c)"), row(b_qkv).to_broadcast([128, 3 * C])).then_inc(ld_b, 16)
            for t, k, a in ((ln_g, 0, kln_g), (ln_g, 1, vln_g), (ln_b, 0, kln_b), (ln_b, 1, vln_b)):
                act.dma_start(t[:, k, :], row(a).to_broadcast([128, HD])).then_inc(ld_b, 16)
            for t, a in ((mb2, mix_b2), (gb, gnn_b)):
                act.dma_start(t[:, :], row(a).to_broadcast([128, C])).then_inc(ld_b, 16)
            act.dma_start(gateb[:, :], row(gate_b).to_broadcast([128, NE])).then_inc(ld_b, 16)
            act.dma_start(brow[0:NE * KF, :], b1.rearrange("e (m p) -> (e m) p", p=128)).then_inc(ld_b, 16)
            for j in range(2):
                act.dma_start(brow[64 + j:65 + j, :].rearrange("a (h d) -> a h d", d=HD),
                              b_qkv.rearrange("(a h s d) -> a h s d", a=2, s=3, d=HD)[j:j + 1, :, 0, :]).then_inc(ld_b, 16)
            act.dma_start(brow[66:68, :], mix_b1.rearrange("(a d) -> a d", d=128)).then_inc(ld_b, 16)
            for j, a in ((68, vln_g), (69, vln_b)):
                act.dma_start(brow[j:j + 1, :].rearrange("a (h d) -> a h d", d=HD),
                              a.rearrange("(a h d) -> a h d", a=1, h=1).to_broadcast([1, 4, HD])).then_inc(ld_b, 16)

            act.wait_ge(consts, 1)
            hold_table(ACT.Copy)
            with act.Fori(0, T_OF[0] // SR) as i:
                for s in range(SR):
                    sort_loads(act, i * SR + s, i * SR + (s + 1), s, H_OF[0], on_vector(s))
            for j in range(T_OF[0] // SR * SR, T_OF[0]):
                sort_loads(act, j, j + 1, j % SR, H_OF[0], on_vector(j % SR))
            act.wait_ge(var_ready, 1)
            nc.scalar.activation(st[0:B, 0, 0:NT], st[0:B, 1, 0:NT], ACT.Sqrt).then_inc(sqrt_done, 1)
            act.wait_ge(xn_ready, 1)
            for t in range(NT):
                if t >= RING:
                    act.wait_ge(squares, t - RING + 1)
                nc.scalar.activation(rows[0:B, t % RING, :], xn[0:B, t, :], ACT.Square,
                                     accum_out=st[0:B, 2, t:t + 1]).then_inc(squares, 1)
                act.wait_ge(xn_t, t + 1)
                nc.scalar.activation(xnT[:, :, t * B:(t + 1) * B], bank[4 + t % 2][:, 0:KC * B].rearrange("p (k n) -> p k n", k=KC),
                                     ACT.Copy).then_inc(xn_t_out, 1)
            act.wait_ge(var_ready, 2)
            nc.scalar.activation(st[0:B, 0, 0:NT], st[0:B, 1, 0:NT], ACT.Sqrt).then_inc(sqrt_done, 1)
            act.wait_ge(ln_arg, 1)
            nc.scalar.activation(st[0:B, 0, 0:NT], st[0:B, 6, 0:NT], ACT.Ln).then_inc(ln_done, 1)
            act.wait_ge(row_scale, 1)
            for t in range(NT):
                act.wait_ge(tab_mm, t + 1)
                if t % GT == 0:
                    act.wait_ge(x_plus, t // GT + 1)
                nc.scalar.activation(tout[0:B, t, :], bank[2 + t % 2][0:B, 0:C], ACT.Copy,
                                     scale=st[0:B, 7, t:t + 1]).then_inc(tab_out, 1)
            act.wait_ge(setup_t, 1)
            nc.scalar.activation(wqT[:, :, :].rearrange("p k n -> p (k n)"), bank[5][:, :], ACT.Copy)
            nc.scalar.activation(bcol[:, :], bank[4][:, 0:70], ACT.Copy).then_inc(setup_t_out, 1)

            def row_numbers(c, k):
                nc.scalar.activation(idx[:, k:k + 1], g_row[:, ds(c, 1)], ACT.Copy).then_inc(idx_ready, 1)

            act.wait_ge(tab_stored, 16 * NT // GT)
            nc.scalar.activation(acc[:, :, :], zeros[:, 0:C].unsqueeze(1).to_broadcast([128, NT, C]), ACT.Copy).then_inc(acc_zero, 1)
            act.wait_ge(group_ready, 1)
            for k in range(RING):
                row_numbers(k, k)
            act.wait_ge(routed, 1)
            for g, turns, turn0, nsort, mix, tiles, tile0 in SEGS:
                c0 = CHUNK0[g] + RING * turn0
                col0 = AT[g + 1] + nsort * turn0 if nsort else 0
                split = shares(nsort, RING)
                last = c0 + turns * RING == CHUNKS
                if mix == 2 and tile0 == 0:
                    attention_fold_act(act)
                if mix == 1 and tile0 == 0:
                    hold_table(ACT.Sqrt)
                if g < 2 and turn0 == SORT_TURNS[g]:
                    act.wait_ge(group_ready, g + 2)

                def turn(i):
                    m = 0
                    for k in range(RING):
                        for _ in range(split[k]):
                            sort_loads(act, i * nsort + (col0 + m), i * nsort + (col0 + m + 1), m % SR, H_OF[g + 1])
                            m += 1
                        for name, tile in attention_steps(tiles, k, i, tile0):
                            if mix == 1 and name == "columns":
                                await_ge(act, kv_mm, tile)
                                nc.scalar.activation(xst[:, :, :], xnT[:, :, ds(tile * B, B)], ACT.Copy).then_inc(xst_ready, 1)
                            if mix == 1 and name == "square":
                                act.wait_ge(kv_sb, tile + 1)
                                nc.scalar.activation(kvs[0:B], kvc[0:B], ACT.Square).then_inc(kv_sq, 1)
                            if mix == 1 and name == "root":
                                act.wait_ge(kv_var, tile + 1)
                                nc.scalar.activation(kvst[0:B, 1, :], kvst[0:B, 0, :], ACT.Sqrt).then_inc(kv_std, 1)
                            if mix == 2 and name == "gelu":
                                act.wait_ge(mh_mm, tile + 1)
                                await_ge(act, my_mm, tile)
                                for m2 in range(KC):
                                    ins = nc.scalar.activation(mhT[:, m2, :], bank[4][:, m2 * B:(m2 + 1) * B], ACT.Gelu, bias=beff[:, m2:m2 + 1])
                                ins.then_inc(mh_out, 1)
                        if not last:
                            act.wait_ge(chunk_done, i * RING + (RING + c0 + k + 1))
                            row_numbers(i * RING + (c0 + RING + k), k)

                if turns == 1:
                    turn(0)
                else:
                    with act.Fori(0, turns) as i:
                        turn(i)
            act.wait_ge(chunk_added, RING + CHUNKS)
            act.wait_ge(chunk_done, RING + CHUNKS)
            for t in range(NT + 1):
                if t >= 4:
                    act.wait_ge(tail_ss, t - 3)
                nc.scalar.activation(rows[0:B, t % 4, :], acc[0:B, t, :] if t < NT else gb[0:B, :], ACT.Square,
                                     accum_out=st[0:B, 2, t:t + 1]).then_inc(tail_ss, 1)
            act.wait_ge(tail_v, 1)
            nc.scalar.activation(st[0:B, 0, :], st[0:B, 1, :], ACT.Sqrt).then_inc(tail_sq, 1)
            act.wait_ge(tail_v, 2)
            nc.scalar.activation(st[0:B, 7, :], st[0:B, 6, :], ACT.Tanh).then_inc(tail_tanh, 1)
            act.wait_ge(tail_v, 3)
            nc.scalar.activation(st[0:B, 0, 0:NT], st[0:B, 1, 0:NT], ACT.Sqrt).then_inc(tail_sq, 1)
            def token_columns(t):
                act.wait_ge(mt_mm, t + 1)
                if t >= RING:
                    act.wait_ge(mg_mm, (t - RING) // GT + 1)
                nc.scalar.activation(rows[:, t % RING, 0:KC * B], bank[t % 4][:, 0:KC * B], ACT.Copy).then_inc(mt_out, 1)

            act.wait_ge(factors, 1)

            def scaled_bias(q):
                for t in range(q * GT, (q + 1) * GT):
                    if t >= 4:
                        act.wait_ge(gb_added, t - 3)
                    nc.scalar.activation(bias_ring[t % 4], gb[0:B, :], ACT.Copy, scale=st[0:B, 15, t:t + 1]).then_inc(gb_scaled, 1)

            for q in range(2):
                scaled_bias(q)
            for q in range(NT // GT + 1):
                if q < NT // GT:
                    g = slice(q * GT, (q + 1) * GT)
                    act.wait_ge(mid_var, q + 1)
                    nc.scalar.activation(st[0:B, 0, g], st[0:B, 1, g], ACT.Sqrt).then_inc(mid_root, 1)
                if q + 2 < NT // GT:
                    scaled_bias(q + 2)
                for t in range((q - 1) * GT, q * GT) if q else ():
                    act.wait_ge(mid_scale, q)
                    nc.scalar.activation(acc[0:B, t, :], X[0:B, t, :], ACT.Identity,
                                         bias=mid_nb[0:B, t:t + 1], scale=mid_rs[0:B, t:t + 1]).then_inc(mid_norm, 1)
                    if t:
                        token_columns(t - 1)
            token_columns(NT - 1)
            act.wait_ge(exp_arg, 1)
            nc.scalar.activation(st[0:B, 1, 0:NT], st[0:B, 0, 0:NT], ACT.Exp).then_inc(exp_done, 1)
            act.wait_ge(rows_known, 1)
            node_rows = [node2[0:B, :, :].rearrange("p k t -> p (k t)"), pair_row[0:B, :, :].rearrange("p k t -> p (k t)")]

            def pair_loads_of(j, n, s):
                act.wait_ge(pairs_made, n)
                for a in range(s % 2, 2):
                    ins = nc.scalar.activation(p_load[0:B, s, a * SLOTS:(a + 1) * SLOTS], p_hi[0:B, s, :], ACT.Copy,
                                               scale=node_rows[a][:, ds(j, 1)])
                ins.then_inc(pair_loads, 1)

            with act.Fori(0, PAIRS // PR) as i:
                for s in range(PR):
                    pair_loads_of(i * PR + s, i * PR + (s + 1), s)
            for j in range(PAIRS // PR * PR, PAIRS):
                pair_loads_of(j, j + 1, j % PR)
            act.wait_ge(slots_ready, 1)

            def token_numbers(i, k):
                await_ge(act, tok_got[k], i * 16)
                nc.scalar.activation(idx[:, k:k + 1], s_tok[:, ds(i * RING + k, 1)], ACT.Copy).then_inc(tok_idx, 1)

            for k in range(RING):
                token_numbers(0, k)

            def expert_turn(i, last):
                _, offs = nc.values_load_multi_w_load_instructions(
                    ex_b1[0:1, ds(i * RING, RING)], engines=[ACT_], min_val=0, max_val=(NE - 1) * KF,
                    skip_runtime_bounds_check_because="the router clamps it")
                for k in range(RING):
                    await_ge(act, y_put[k], i * 16)
                    nc.scalar.activation(odx[:, k:k + 1], s_row[:, ds(i * RING + k, 1)], ACT.Copy).then_inc(out_idx, 1)
                    act.wait_ge(h_mm, i * RING + (k + 1))
                    if not (isinstance(i, int) and k < 2):
                        act.wait_ge(y_mm, i * RING + (k - 1))
                    for m in range(KF):
                        ins = nc.scalar.activation(hT[:, k % 2, m, :], bank[2 + k % 2][:, m * 128:(m + 1) * 128], ACT.Relu,
                                                   bias=bcol[:, ds(offs[k] + m, 1)])
                    ins.then_inc(h_out, 1)
                    if not last:
                        token_numbers(i + 1, k)

            turns_of(act, 0, SLOTS // RING, lambda i: expert_turn(i, False), lambda i: expert_turn(i, True))
            act.wait_ge(y_out, SLOTS)

            def token_again(t):
                nc.scalar.activation(zb[0:B, t, :], X[0:B, t, :], ACT.Identity,
                                     bias=mid_nb[0:B, t:t + 1], scale=mid_rs[0:B, t:t + 1]).then_inc(tokens_again, 1)

            for t in range(2 * GT):
                token_again(t)
            for k in range(RING):
                act.wait_ge(y_put[k], 16 * SLOTS // RING)
            for q in range(NT // GT):
                t = slice(q * GT, (q + 1) * GT)
                act.dma_start(yb[0:B, 1, t, :], y_t[1, :, t, :]).then_inc(y_ld[q], 16)
            for t in range(2 * GT, NT):
                token_again(t)
            for q in range(NT // GT + 1):
                if q < NT // GT:
                    g = slice(q * GT, (q + 1) * GT)
                    act.wait_ge(fin_var, q + 1)
                    nc.scalar.activation(st[0:B, 0, g], st[0:B, 1, g], ACT.Sqrt).then_inc(fin_root, 1)
                for t in range((q - 1) * GT, q * GT) if q else ():
                    act.wait_ge(fin_scale, q)
                    nc.scalar.activation(ub[0:B, t, :], zb[0:B, t, :], ACT.Identity,
                                         bias=mid_nb[0:B, t:t + 1], scale=mid_rs[0:B, t:t + 1]).then_inc(fin_norm, 1)

        @block.gpsimd
        def _(pool):
            step = Steps(pool, pool_step)
            nc.gpsimd.memset(esrc[:, FULL:COLS], 0).then_inc(pads, 1)
            nc.gpsimd.memset(edst[:, FULL:COLS], 0).then_inc(pads, 1)
            nc.gpsimd.memset(ew[:, FULL:COLS], 0.0).then_inc(pads, 1)
            step.mark(nc.gpsimd.iota(iota[:, :], pattern=[[1, HMAX]], base=0, channel_multiplier=0, allow_small_or_imprecise_dtypes=True))
            step.mark(nc.gpsimd.iota(node2[:, :, :], pattern=[[0, 2], [B, NT]], base=0, channel_multiplier=1, allow_small_or_imprecise_dtypes=True))
            step.mark(nc.gpsimd.iota(slot_id[:, :], pattern=[[128, SLOTS]], base=2 * N + 1, channel_multiplier=1,
                                     allow_small_or_imprecise_dtypes=True))
            step.mark(nc.gpsimd.iota(chunk_id[:, :], pattern=[[128, 2]], base=0, channel_multiplier=1, allow_small_or_imprecise_dtypes=True))
            step.mark(nc.gpsimd.memset(ones[:, :], 1.0))
            step.mark(nc.gpsimd.memset(ident[:, :], 0.0))
            step.mark(nc.gpsimd.memset(small[:, :, :], 0.0))
            step(nc.gpsimd.memset(zeros[:, :], 0.0))
            step(nc.gpsimd.affine_select(out=tri[:, :], in_=ones[:, :], compare_op=ALU.is_gt, fill=0.0, base=0,
                                         pattern=[[1, 128]], channel_multiplier=-1))
            nc.gpsimd.affine_select(out=ident[:, :], in_=ident[:, :], compare_op=ALU.not_equal, fill=1.0, base=0,
                                    pattern=[[-1, 128]], channel_multiplier=1).then_inc(consts, 1)
            pool.wait_ge(xn_ready, 1)
            pool.wait_ge(ld_b, 16 * B_LOADS)
            for q in range(NT // GT):
                t = slice(q * GT, (q + 1) * GT)
                step(nc.gpsimd.tensor_tensor(X[0:B, t, :], X[0:B, t, :], xn[0:B, t, :], ALU.add))
                nc.gpsimd.tensor_tensor(X[0:B, t, :], X[0:B, t, :], mb2[0:B, :].unsqueeze(1).to_broadcast([B, GT, C]),
                                        ALU.add).then_inc(x_plus, 1)
            pool.wait_ge(tab_stored, 16 * NT // GT)
            for g in range(3):
                with pool.Fori(0, TURNS[g]) as i:
                    for k in range(RING):
                        pool.wait_ge(idx_ready, i * RING + CHUNK0[g] + k + 1)
                        pool.wait_ge(chunk_done, i * RING + (CHUNK0[g] + k + 1))
                        pool.sem_inc(may_go, 1)
                        nc.gpsimd.indirect_dma_start(
                            out=rows[:, k, :], out_offset=None, in_=table[:, :],
                            in_offset=bass.IndirectOffsetOnAxis(ap=idx[:, k:k + 1], axis=0)).then_inc(gathered[k], 16)

            for t in range(NT):
                pool.wait_ge(gb_scaled, t + 1)
                nc.gpsimd.tensor_tensor(X[0:B, t, :], bias_ring[t % 4], X[0:B, t, :], ALU.add).then_inc(gb_added, 1)
            pool.wait_ge(tok_stored, 16 * (NT // GT))

            def get_tokens(i, k, turns_before, turned):
                pool.wait_ge(tok_idx, i * RING + (k + 1))
                await_ge(pool, x_mm, turns_before * RING + (k + 1 if turned else 0))
                pool.sem_inc(may_go, 1)
                nc.gpsimd.indirect_dma_start(
                    out=rows[:, k, :], out_offset=None, in_=tokens[:, :],
                    in_offset=bass.IndirectOffsetOnAxis(ap=idx[:, k:k + 1], axis=0)).then_inc(tok_got[k], 16)

            def put_results(i, k):
                pool.wait_ge(out_idx, i * RING + (k + 1))
                pool.wait_ge(y_out, i * RING + (k + 1))
                pool.sem_inc(may_go, 1)
                nc.gpsimd.indirect_dma_start(
                    out=pair_out[:, :], out_offset=bass.IndirectOffsetOnAxis(ap=odx[:, k:k + 1], axis=0),
                    in_=yv[:, k % 2, :], in_offset=None).then_inc(y_put[k], 16)

            for k in range(RING):
                get_tokens(0, k, 0, False)
            with pool.Fori(0, SLOTS // RING - 1) as i:
                for k in range(RING):
                    get_tokens(i + 1, k, i, True)
                    put_results(i, k)
            for k in range(RING):
                put_results(SLOTS // RING - 1, k)
            pool.wait_ge(ld_gb, 32)
            for t in range(NT):
                pool.wait_ge(tokens_again, t + 1)
                nc.gpsimd.tensor_tensor(X[0:B, t, :], X[0:B, t, :], bet[0:B, :], ALU.add).then_inc(beta_added, 1)
            for t in range(NT):
                pool.wait_ge(fin_norm, t + 1)
                nc.gpsimd.tensor_tensor(ub[0:B, t, :], ub[0:B, t, :], gam[0:B, :], ALU.mult).then_inc(fin_aff, 1)

        def rsqrt_refined(step, out_, var, root, tmp):
            step(nc.vector.reciprocal(out_, root))
            step(nc.vector.tensor_tensor(tmp, out_, out_, ALU.mult))
            step(nc.vector.tensor_tensor(tmp, tmp, var, ALU.mult))
            step(nc.vector.tensor_scalar(tmp, tmp, -0.5, 1.5, ALU.mult, ALU.add))
            step(nc.vector.tensor_tensor(out_, out_, tmp, ALU.mult))

        def route(dve, step, rounds, P, T, nb, H, key_, lo_, hi_, buckets, memory, meanwhile=None):
            one, run = (m[0:P, 0:nb * T] for m in memory)
            one3, run3 = one.rearrange("p (b t) -> p b t", b=nb), run.rearrange("p (b t) -> p b t", b=nb)
            ends, mine, first, off = small[0:P, 0, :], small[0:P, 1, :], small[0:P, 2, :], small[0:P, 3, :]
            step(nc.vector.tensor_tensor(one3, key_.unsqueeze(1).to_broadcast([P, nb, T]),
                                         iota[0:P, 0:nb].unsqueeze(2).to_broadcast([P, nb, T]), ALU.is_equal))
            step(nc.vector.tensor_tensor_scan(run, one, one, 0.0, ALU.add, ALU.max))
            step(nc.vector.tensor_copy(ends[:, 1:nb + 1], run3[:, :, T - 1]))
            nc.vector.tensor_tensor(mine[:, 0:nb], ends[:, 1:nb + 1], ends[:, 0:nb], ALU.subtract).then_inc(rank_rows, 1)
            if meanwhile:
                meanwhile()
            dve.wait_ge(rank_sums, 2 * rounds - 1)
            before, total = bank[6][0:P, 0:nb], bank[6][0:P, 32:32 + nb]
            step(nc.vector.tensor_scalar(slot_i[0:P, 0:nb], total, 127.0, None, ALU.add))
            step(nc.vector.tensor_scalar(cnt_i[0:P, 0:nb], slot_i[0:P, 0:nb], 7, None, ALU.logical_shift_right))
            step(nc.vector.tensor_copy(off[:, 0:nb], cnt_i[0:P, 0:nb]))
            step(nc.vector.tensor_tensor_scan(first[:, 1:nb + 1], off[:, 0:nb], off[:, 0:nb], 0.0, ALU.add, ALU.max))
            step(nc.vector.scalar_tensor_tensor(off[:, 0:nb], first[:, 0:nb], 128.0, before, ALU.mult, ALU.add))
            step(nc.vector.scalar_tensor_tensor(off[:, 0:nb], off[:, 0:nb], -1.0, ends[:, 0:nb], ALU.add, ALU.subtract))
            step(nc.vector.tensor_tensor(run3, run3, off[:, 0:nb].unsqueeze(2).to_broadcast([P, nb, T]), ALU.add))
            step(nc.vector.tensor_tensor(run, run, one, ALU.mult))
            step(nc.vector.tensor_reduce(slot[0:P, 0:T], run.rearrange("p (b t) -> p t b", b=nb), AX.X, ALU.add))
            W = -(-H // 128)
            step(nc.vector.tensor_tensor(one[:, 0:W * nb].rearrange("p (h b) -> p h b", b=nb),
                                         first[:, 1:nb + 1].unsqueeze(1).to_broadcast([P, W, nb]),
                                         chunk_id[0:P, 0:W].unsqueeze(2).to_broadcast([P, W, nb]), ALU.is_le))
            nc.vector.tensor_reduce(bucket[0:P, 0:W], one[:, 0:W * nb].rearrange("p (h b) -> p h b", b=nb),
                                    AX.X, ALU.add).then_inc(rank_rows, 1)
            step(nc.vector.tensor_copy(slot_i[0:P, 0:T], slot[0:P, 0:T]))
            step(nc.vector.tensor_scalar(slot_j[0:P, 0:T], slot_i[0:P, 0:T], 7, None, ALU.logical_shift_right))
            dve.wait_ge(rank_sums, 2 * rounds)
            for offsets, scale in buckets:
                step.mark(nc.vector.tensor_scalar(offsets, bank[6][0:1, 128:128 + H], float(nb - 1), float(scale), ALU.min, ALU.mult))
            step(nc.vector.tensor_copy(hi_, slot_j[0:P, 0:T]))
            step(nc.vector.tensor_scalar(slot_j[0:P, 0:T], slot_i[0:P, 0:T], 127, None, ALU.bitwise_and))
            step(nc.vector.tensor_copy(lo_, slot_j[0:P, 0:T]))

        def sort_column(dve, j, n, s, H, make_edges=False):
            dve.wait_ge(hots_used, n)
            nc.vector.tensor_scalar(s_hi[:, s, 0:H], iota[:, 0:H], hi[:, ds(j, 1)], None, ALU.is_equal)
            if make_edges:
                nc.vector.tensor_scalar(s_load[:, s, 0:H], iota[:, 0:H], hi[:, ds(j, 1)], pack[:, ds(j, 1)], ALU.is_equal, ALU.mult)
            nc.vector.tensor_scalar(s_one[:, s, :], iota[:, 0:128], lo[:, ds(j, 1)], None, ALU.is_equal).then_inc(hots_made, 1)

        def take_group(dve, step, g):
            H, c = H_OF[g], CHUNK0[g]
            dve.wait_ge(sorted_, g + 1)
            step.mark(nc.vector.tensor_copy(g_w[:, c:c + H], bank[0][:, H:2 * H]))
            step(nc.vector.tensor_copy(slot_i[:, 0:H], bank[0][:, 0:H]))
            step.mark(nc.vector.tensor_scalar(g_row[:, c:c + H], slot_i[:, 0:H], 7, None, ALU.logical_shift_right))
            step(nc.vector.tensor_scalar(slot_j[:, 0:H], slot_i[:, 0:H], 127, None, ALU.bitwise_and))
            step(nc.vector.tensor_copy(g_lo[:, c:c + H], slot_j[:, 0:H]))
            nc.vector.memset(marker[:, :], 0.0).then_inc(group_ready, 1)

        def key_weights_centred(dve, step):
            dve.wait_ge(ld_w, 16 * W_LOADS)
            dve.wait_ge(ld_b, 16 * B_LOADS)
            for k in range(KC):
                step.mark(nc.vector.tensor_copy(weff[:, k, :].rearrange("p (h d) -> p h d", d=HD),
                                                wqkv[:, k, :].rearrange("p (h s d) -> p h s d", s=3, d=HD)[:, :, 0, :]))
                w3 = wqkv[:, k, :].rearrange("p (a d) -> p a d", d=HD)
                step(nc.vector.tensor_reduce(wmean[:, k, :], w3, AX.X, ALU.add))
                step.mark(nc.vector.scalar_tensor_tensor(
                    wcen[:, k, :].rearrange("p (a d) -> p a d", d=HD), wmean[:, k, :].unsqueeze(2).to_broadcast([128, 3 * HEADS, HD]),
                    -1.0 / HD, w3, ALU.mult, ALU.add))
            b3 = bias_kv[:, :, :].rearrange("p h (s d) -> p (h s) d", d=HD)
            step(nc.vector.tensor_reduce(wmean[:, 0, :], b3, AX.X, ALU.add))
            step(nc.vector.scalar_tensor_tensor(b3, wmean[:, 0, :].unsqueeze(2).to_broadcast([128, 3 * HEADS, HD]),
                                                -1.0 / HD, b3, ALU.mult, ALU.add))
            nc.vector.memset(marker[:, :], 0.0).then_inc(wcen_ready, 1)

        def attention_fold_dve(dve, step):
            attention_keys_dve(dve, step, "variance", NT - 1)
            attention_keys_dve(dve, step, "norm", NT - 1)
            dve.wait_ge(kv_used, NT)
            gv, bv = bcol[:, 68:69], bcol[:, 69:70]
            for j in range(KC):
                step.mark(nc.vector.tensor_copy(kvsum[:, j, :], bank[6][:, 260 + j:261 + j].to_broadcast([128, 128])))
            step.mark(nc.vector.tensor_scalar(kvst[:, 2, 0:KC], bank[6][:, 256:256 + KC], gv, None, ALU.mult))
            step.wait()
            nc.vector.scalar_tensor_tensor(kvst[:, 2, 0:KC], bv.to_broadcast([128, KC]), float(N), kvst[:, 2, 0:KC],
                                           ALU.mult, ALU.add).then_inc(kv_sums, 1)
            step(nc.vector.memset(kvT[:, :, :], 0.0))
            dve.wait_ge(kv_sums_row, 1)
            full = kvs[:, :, :, :].rearrange("p h s d -> p (h s d)")[:, 0:C]
            step(nc.vector.tensor_scalar(full, bank[1][:, 0:C], bv, None, ALU.mult))
            step(nc.vector.scalar_tensor_tensor(full, bank[6][:, 0:C], gv, full, ALU.mult, ALU.add))
            f3 = full.rearrange("p (h d) -> p h d", d=HD)
            step(nc.vector.tensor_tensor(f3, f3, ln_g[:, 0, :].unsqueeze(1).to_broadcast([128, HEADS, HD]), ALU.mult))
            for j in range(KC):
                fj = f3[:, 4 * j:4 * j + 4, :]
                step(nc.vector.scalar_tensor_tensor(fj, ln_b[:, 0, :].unsqueeze(1).to_broadcast([128, 4, HD]), kvst[:, 2, j:j + 1], fj,
                                                    ALU.mult, ALU.add))
            for j in range(KC):
                for h in range(4):
                    s = slice(h * HD, (h + 1) * HD)
                    ins = nc.vector.tensor_scalar(kvT[s, j, s], full[s, j * 128 + h * HD:j * 128 + (h + 1) * HD], 1.0 / N, None, ALU.mult)
            ins.then_inc(kvT_ready, 1)
            dve.wait_ge(weff_mm, 1)
            step.mark(nc.vector.tensor_tensor(weff[:, :, :].rearrange("p k n -> p (k n)"), bank[0][:, :],
                                              mw1[:, :, :].rearrange("p k n -> p (k n)"), ALU.add))
            for m in range(KC):
                step.mark(nc.vector.tensor_tensor(beff[:, m:m + 1], bank[1][:, 256 + m:257 + m], bcol[:, 66 + m:67 + m], ALU.add))
            step.wait()
            nc.vector.memset(marker[:, :], 0.0).then_inc(weff_out, 1)

        def normalise_keys(dve, step, tile):
            dve.wait_ge(kv_std, tile + 1)
            step(nc.vector.reciprocal(kvst[0:B, 3, :], kvst[0:B, 1, :]))
            await_ge(dve, kv_used, tile)
            nc.vector.tensor_tensor(kvn[0:B, :, :, :].rearrange("p s h d -> p h s d"), kvc[0:B],
                                    kvst[0:B, 3, :].rearrange("p (h s) -> p h s", s=2).unsqueeze(3).to_broadcast([B, HEADS, 2, HD]),
                                    ALU.mult).then_inc(kv_norm, 1)

        def attention_keys_dve(dve, step, name, tile):
            if name == "norm":
                normalise_keys(dve, step, tile)
            if name == "out":
                dve.wait_ge(kv_mm, tile + 1)
                await_ge(dve, kv_norm, tile)
                nc.vector.tensor_tensor(kvc[0:B], bank[4][0:B, :].rearrange("p (h s d) -> p h s d", h=HEADS, s=2),
                                        bias_kv[0:B, :, HD:3 * HD].rearrange("p h (s d) -> p h s d", s=2), ALU.add).then_inc(kv_sb, 1)
            if name == "variance":
                dve.wait_ge(kv_sq, tile + 1)
                step(nc.vector.tensor_reduce(kvst[0:B, 2, :], kvs[0:B].rearrange("p h s d -> p (h s) d"), AX.X, ALU.add))
                nc.vector.tensor_scalar(kvst[0:B, 0, :], kvst[0:B, 2, :], 1.0 / HD, LN_EPS, ALU.mult, ALU.add).then_inc(kv_var, 1)

        @block.vector
        def _(dve):
            step = Steps(dve, dve_step)
            dve.wait_ge(ld_edge, 16 * 6)
            step(nc.vector.tensor_scalar(eq[:, :], esrc[:, :], 4195.0, None, ALU.mult))
            step(nc.vector.tensor_scalar(eq[:, :], eq[:, :], 19, None, ALU.logical_shift_right))
            step(nc.vector.tensor_copy(key[:, :], eq[:, :]))
            step(nc.vector.scalar_tensor_tensor(pack[:, :], key[:, :], -float(B), esrc[:, :], ALU.mult, ALU.add))
            step(nc.vector.scalar_tensor_tensor(pack[:, :], edst[:, :], 128.0, pack[:, :], ALU.mult, ALU.add))
            dve.wait_ge(consts, 1)
            nc.vector.memset(marker[:, :], 0.0).then_inc(chunk_added, RING)
            T = T_OF[0]
            route(dve, step, 1, 128, T, NT, H_OF[0], key[:, 0:T], lo[:, 0:T], hi[:, 0:T], [(bk[:, 0:H_OF[0]], C)],
                  (rt_one, rt_sum))
            dve.wait_ge(ld_x, 32)
            with step.loop(NT // 2, 2) as i:
                for s in range(SR):
                    sort_column(dve, i * SR + s, i * SR + (s + 1), s, H_OF[0], on_vector(s))
                    if s % (SR // 2) == 0:
                        t = i * 2 + s // (SR // 2)
                        step.mark(nc.vector.bn_stats(bn6[0:B, ds(t, 1), :].rearrange("p a s -> p (a s)"),
                                                     X[0:B, ds(t, 1), :].rearrange("p a c -> p (a c)")))
            step.mark(nc.vector.bn_stats(bn6[0:B, NT - 1, :], X[0:B, NT - 1, :]))
            with dve.Fori(NT // 2, T // SR) as i:
                for s in range(SR):
                    sort_column(dve, i * SR + s, i * SR + (s + 1), s, H_OF[0], on_vector(s))
            for j in range(T // SR * SR, T):
                sort_column(dve, j, j + 1, j % SR, H_OF[0], on_vector(j % SR))
            step.wait()
            for t in range(NT):
                step.mark(nc.vector.bn_aggr(mv[0:B, t, :], bn6[0:B, t, :]))
            step.wait()
            nc.vector.tensor_scalar(st[0:B, 1, 0:NT], mv[0:B, :, 1], LN_EPS, None, ALU.add).then_inc(var_ready, 1)
            dve.wait_ge(sqrt_done, 1)
            rsqrt_refined(step, st[0:B, 3, 0:NT], st[0:B, 1, 0:NT], st[0:B, 0, 0:NT], st[0:B, 4, 0:NT])
            for t in range(NT):
                ins = nc.vector.tensor_scalar(xn[0:B, t, :], X[0:B, t, :], mv[0:B, t, 0:1], st[0:B, 3, t:t + 1], ALU.subtract, ALU.mult)
            ins.then_inc(xn_ready, 1)
            take_group(dve, step, 0)
            key_weights_centred(dve, step)

            def s_(k):
                return st[0:B, k, 0:NT]

            def log_map():
                dve.wait_ge(squares, NT)
                nc.vector.tensor_scalar(s_(1), s_(2), EPS * EPS, None, ALU.max).then_inc(var_ready, 1)
                dve.wait_ge(sqrt_done, 2)
                rsqrt_refined(step, s_(3), s_(1), s_(0), s_(4))
                step(nc.vector.tensor_tensor(s_(3), s_(3), s_(1), ALU.mult))
                step(nc.vector.tensor_scalar(s_(3), s_(3), MAXNORM, None, ALU.min))
                step.mark(nc.vector.tensor_scalar(s_(4), s_(3), -1.0, 1.0, ALU.mult, ALU.add))
                step(nc.vector.tensor_scalar(s_(5), s_(3), 1.0, None, ALU.add))
                step(nc.vector.reciprocal(s_(4), s_(4)))
                nc.vector.tensor_tensor(s_(6), s_(5), s_(4), ALU.mult).then_inc(ln_arg, 1)
                step(nc.vector.tensor_tensor(s_(11), s_(3), s_(3), ALU.mult))
                step(nc.vector.tensor_scalar(s_(8), s_(11), 1 / 7, 1 / 5, ALU.mult, ALU.add))
                step(nc.vector.tensor_tensor(s_(8), s_(8), s_(11), ALU.mult))
                step(nc.vector.tensor_scalar(s_(8), s_(8), 1 / 3, None, ALU.add))
                step(nc.vector.tensor_tensor(s_(8), s_(8), s_(11), ALU.mult))
                step(nc.vector.tensor_scalar(s_(8), s_(8), 1.0, None, ALU.add))
                step(nc.vector.reciprocal(s_(9), s_(3)))
                dve.wait_ge(ln_done, 1)
                step(nc.vector.scalar_tensor_tensor(s_(9), s_(0), 0.5, s_(9), ALU.mult, ALU.mult))
                step(nc.vector.tensor_tensor(s_(8), s_(8), s_(9), ALU.subtract))
                step(nc.vector.tensor_scalar(s_(10), s_(3), 0.06, None, ALU.is_lt))
                step(nc.vector.tensor_tensor(s_(8), s_(8), s_(10), ALU.mult))
                nc.vector.tensor_tensor(s_(7), s_(8), s_(9), ALU.add).then_inc(row_scale, 1)

            for g in (1, 2):
                a, T = AT[g], T_OF[g]
                route(dve, step, g + 1, 128, T, NT, H_OF[g], key[:, a:a + T], lo[:, a:a + T], hi[:, a:a + T],
                      [(bk[:, CHUNK0[g]:CHUNK0[g] + H_OF[g]], C)], (rt_one, rt_sum), meanwhile=log_map if g == 1 else None)

            nc.vector.memset(marker[:, :], 0.0).then_inc(routed, 1)

            def chunk_hot(c, k):
                nc.vector.tensor_scalar(hot[:, k, :], iota[:, 0:128], g_lo[:, ds(c, 1)], g_w[:, ds(c, 1)],
                                        ALU.is_equal, ALU.mult).then_inc(hot_ready, 1)

            def block_offsets(start, n):
                return nc.values_load_multi_w_load_instructions(
                    bk[0:1, ds(start, n)], engines=[DVE_], min_val=0, max_val=(NT - 1) * C,
                    skip_runtime_bounds_check_because="the router clamps it")[1]

            def add_chunk(c, k, off):
                dve.wait_ge(chunk_added, c + RING)
                to = accf[:, ds(off, C)]
                nc.vector.tensor_tensor(to, to, bank[CHUNK_BANKS[k // 2]][:, k % 2 * C:(k % 2 + 1) * C],
                                        ALU.add).then_inc(chunk_added, 1)

            for k in range(RING):
                chunk_hot(k, k)
            dve.wait_ge(acc_zero, 1)
            for g, turns, turn0, nsort, mix, tiles, tile0 in SEGS:
                c0 = CHUNK0[g] + RING * turn0
                last = c0 + turns * RING == CHUNKS
                if g < 2 and turn0 == SORT_TURNS[g]:
                    take_group(dve, step, g + 1)
                if mix == 2 and tile0 == 0:
                    attention_fold_dve(dve, step)
                col0 = AT[g + 1] + nsort * turn0 if nsort else 0
                split = shares(nsort, RING)

                def turn(i):
                    first = c0 == 0
                    offs = block_offsets(c0, RING - 2) if first else block_offsets(i * RING + (c0 - 2), RING)
                    offs = [None, None, *offs] if first else offs
                    m = 0
                    for k in range(RING):
                        for _ in range(split[k]):
                            sort_column(dve, i * nsort + (col0 + m), i * nsort + (col0 + m + 1), m % SR, H_OF[g + 1])
                            m += 1
                        for name, tile in attention_steps(tiles, k, i, tile0):
                            if mix == 1:
                                attention_keys_dve(dve, step, name, tile)
                            elif name == "add":
                                dve.wait_ge(my_mm, tile + 1)
                                nc.vector.tensor_tensor(X[0:B, ds(tile, 1), :], X[0:B, ds(tile, 1), :],
                                                        bank[0][0:B, 0:C].unsqueeze(1), ALU.add).then_inc(my_out, 1)
                        if k % 2:
                            c, k2 = i * RING + (c0 - 2), (k - 2) % RING
                            if not (first and k == 1):
                                dve.wait_ge(chunk_done, c + (RING + k + 1))
                                add_chunk(c + (k - 1), k2 - 1, offs[k - 1])
                                if not (last and k > 1):
                                    chunk_hot(c + (RING + k - 1), k2 - 1)
                                    chunk_hot(c + (RING + k), k2)
                                add_chunk(c + k, k2, offs[k])

                if turns == 1:
                    turn(0)
                else:
                    with step.loop(turns, 2 * tiles if mix == 1 else 0) as i:
                        turn(i)
            dve.wait_ge(chunk_done, RING + CHUNKS)
            for k, off in enumerate(block_offsets(CHUNKS - 2, 2)):
                add_chunk(CHUNKS - 2 + k, RING - 2 + k, off)
            dve.wait_ge(chunk_added, RING + CHUNKS)
            for t in range(NT):
                if t >= 4:
                    dve.wait_ge(tail_dot, t - 3)
                nc.vector.tensor_tensor_reduce(out=rows[0:B, 4 + t % 4, :], in0=acc[0:B, t, :], in1=gb[0:B, :], scale=1.0, scalar=0.0,
                                               op0=ALU.mult, op1=ALU.add, accum_out=st[0:B, 3, t:t + 1]).then_inc(tail_dot, 1)
            dve.wait_ge(tail_dot, NT)

            def a_(k):
                return st[0:B, k, :]

            def one(k):
                return st[0:B, k, NT:NT + 1]
            dve.wait_ge(tail_ss, NT + 1)
            nc.vector.tensor_scalar(a_(1), a_(2), EPS * EPS, None, ALU.max).then_inc(tail_v, 1)
            dve.wait_ge(tail_sq, 1)
            rsqrt_refined(step, a_(4), a_(1), a_(0), a_(5))
            step(nc.vector.tensor_tensor(a_(5), a_(4), a_(1), ALU.mult))
            nc.vector.tensor_scalar(a_(6), a_(5), 15.0, None, ALU.min).then_inc(tail_v, 1)
            dve.wait_ge(tail_tanh, 1)
            step(nc.vector.tensor_scalar(a_(8), a_(7), EPS, None, ALU.max))
            step(nc.vector.reciprocal(a_(8), a_(8)))
            step(nc.vector.tensor_scalar(a_(8), a_(8), MAXNORM, 1.0, ALU.mult, ALU.min))
            step(nc.vector.tensor_tensor(a_(4), a_(4), a_(7), ALU.mult))
            step(nc.vector.tensor_tensor(a_(8), a_(8), a_(4), ALU.mult))
            step(nc.vector.tensor_tensor(a_(9), a_(8), a_(8), ALU.mult))
            step(nc.vector.tensor_tensor(a_(9), a_(9), a_(2), ALU.mult))
            step(nc.vector.tensor_tensor(s_(10), s_(8), s_(3), ALU.mult))
            step(nc.vector.tensor_scalar(s_(10), s_(10), one(8), 2.0, ALU.mult, ALU.mult))
            step(nc.vector.tensor_scalar(s_(11), s_(10), 1.0, None, ALU.add))
            step(nc.vector.scalar_tensor_tensor(s_(12), s_(11), one(9), s_(8), ALU.add, ALU.mult))
            step(nc.vector.scalar_tensor_tensor(s_(13), s_(9), one(9), s_(11), ALU.mult, ALU.add))
            step(nc.vector.tensor_scalar(s_(13), s_(13), EPS, None, ALU.add))
            step(nc.vector.reciprocal(s_(13), s_(13)))
            step(nc.vector.tensor_scalar(s_(10), s_(9), -1.0, 1.0, ALU.mult, ALU.add))
            step(nc.vector.tensor_scalar(s_(10), s_(10), one(8), None, ALU.mult))
            step(nc.vector.tensor_tensor(s_(12), s_(12), s_(13), ALU.mult))
            step(nc.vector.tensor_tensor(s_(13), s_(10), s_(13), ALU.mult))
            step(nc.vector.tensor_tensor(s_(5), s_(13), s_(3), ALU.mult))
            step(nc.vector.tensor_tensor(s_(6), s_(12), s_(2), ALU.mult))
            step(nc.vector.scalar_tensor_tensor(s_(5), s_(5), 2.0, s_(6), ALU.mult, ALU.add))
            step(nc.vector.tensor_tensor(s_(5), s_(5), s_(12), ALU.mult))
            step(nc.vector.tensor_tensor(s_(6), s_(13), s_(13), ALU.mult))
            step(nc.vector.scalar_tensor_tensor(s_(5), s_(6), one(2), s_(5), ALU.mult, ALU.add))
            nc.vector.tensor_scalar(s_(1), s_(5), EPS * EPS, None, ALU.max).then_inc(tail_v, 1)
            dve.wait_ge(tail_sq, 2)
            rsqrt_refined(step, s_(4), s_(1), s_(0), s_(5))
            step(nc.vector.tensor_scalar(s_(4), s_(4), MAXNORM, 1.0, ALU.mult, ALU.min))
            step.mark(nc.vector.tensor_tensor(s_(14), s_(12), s_(4), ALU.mult))
            step(nc.vector.tensor_tensor(s_(15), s_(13), s_(4), ALU.mult))
            nc.vector.memset(marker[:, :], 0.0).then_inc(factors, 1)

            def variances(tiles, sums, signal, source):
                marks = []
                for t in tiles:
                    sums(t)
                    marks.append(step.done)
                    if len(marks) > 1:
                        step.wait_for(marks[-2])
                        step.mark(nc.vector.bn_stats(bn6[0:B, t - 1, :], source(t - 1)))
                step.wait()
                step(nc.vector.bn_stats(bn6[0:B, tiles[-1], :], source(tiles[-1])))
                for t in tiles:
                    step.mark(nc.vector.bn_aggr(mv[0:B, t, :], bn6[0:B, t, :]))
                step.wait()
                g = slice(tiles[0], tiles[-1] + 1)
                nc.vector.tensor_scalar(st[0:B, 1, g], mv[0:B, g, 1], LN_EPS, None, ALU.add).then_inc(signal, 1)

            def norm_scale(tiles, signal):
                g = slice(tiles[0], tiles[-1] + 1)
                rsqrt_refined(step, mid_rs[0:B, g], st[0:B, 1, g], st[0:B, 0, g], st[0:B, 4, g])
                nc.vector.scalar_tensor_tensor(mid_nb[0:B, g], mv[0:B, g, 0], -1.0, mid_rs[0:B, g], ALU.mult, ALU.mult).then_inc(signal, 1)

            def middle_value(t):
                dve.wait_ge(gb_added, t + 1)
                step.mark(nc.vector.scalar_tensor_tensor(X[0:B, t, :], acc[0:B, t, :], st[0:B, 14, t:t + 1], X[0:B, t, :],
                                                         ALU.mult, ALU.add))

            def best_two(q):
                tiles = range(q * GT, (q + 1) * GT)
                dve.wait_ge(mg_mm, q + 1)
                nc.vector.tensor_tensor(lg[0:B, :, :], bank[6 + q % 2][0:B, 0:GT * NE].rearrange("p (t e) -> p t e", t=GT),
                                        gateb[0:B, :].unsqueeze(1).to_broadcast([B, GT, NE]), ALU.add).then_inc(mg_out, 1)
                dve.wait_ge(mg_out, q + 1)
                for t in tiles:
                    step.mark(nc.vector.max(mx[0:B, t, :], lg[0:B, t % GT, :]))
                step.wait()
                for t in tiles:
                    step.mark(nc.vector.max_index(ix[0:B, t, :], mx[0:B, t, :], lg[0:B, t % GT, :]))
                step.wait()

            turns = NT // GT
            for q in range(turns + 3):
                if q < turns:
                    variances(range(q * GT, (q + 1) * GT), middle_value, mid_var, lambda t: X[0:B, t, :])
                if 1 <= q <= turns:
                    dve.wait_ge(mid_root, q)
                    norm_scale(range((q - 1) * GT, q * GT), mid_scale)
                if q >= 3:
                    best_two(q - 3)
            step.mark(nc.vector.tensor_copy(topv[0:B, :, :], mx[0:B, :, 0:2].rearrange("p t k -> p k t")))
            step(nc.vector.tensor_copy(pair_key[0:B, :, :], ix[0:B, :, 0:2].rearrange("p t k -> p k t")))
            nc.vector.tensor_tensor(s_(0), topv[0:B, 1, :], topv[0:B, 0, :], ALU.subtract).then_inc(exp_arg, 1)
            flat = rows[:, :, :].rearrange("p k c -> p (k c)")
            route(dve, step, 4, B, PAIRS, NE, SLOTS, pair_key[0:B, :, :].rearrange("p k t -> p (k t)"), pair_lo[0:B, :], pair_hi[0:B, :],
                  [(ex_w[0:1, :], 2048), (ex_b1[0:1, :], KF), (ex_b2[0:1, :], C)], (flat[:, 0:1024], flat[:, 1024:2048]))
            dve.wait_ge(exp_done, 1)
            step(nc.vector.tensor_scalar(s_(2), s_(1), 1.0, None, ALU.add))
            step(nc.vector.reciprocal(pair_w[0:B, 0, :], s_(2)))
            step(nc.vector.tensor_tensor(pair_w[0:B, 1, :], s_(1), pair_w[0:B, 0, :], ALU.mult))
            step.mark(nc.vector.tensor_scalar(pair_row[0:B, 0, :], node2[0:B, 0, :], 1.0, None, ALU.add))
            step(nc.vector.tensor_scalar(pair_row[0:B, 1, :], node2[0:B, 0, :], float(N + 1), None, ALU.add))

            nc.vector.memset(marker[:, :], 0.0).then_inc(rows_known, 1)

            dve.wait_ge(tok_stored, 16 * (NT // GT))
            dve.wait_ge(mt_mm, NT)

            def pair_column(j, s):
                nc.vector.tensor_scalar(p_hi[0:B, s, :], iota[0:B, 0:SLOTS], pair_hi[0:B, ds(j, 1)], None, ALU.is_equal)
                if s % 2:
                    nc.vector.tensor_scalar(p_load[0:B, s, 0:SLOTS], iota[0:B, 0:SLOTS], pair_hi[0:B, ds(j, 1)],
                                            node2[0:B, :, :].rearrange("p k t -> p (k t)")[:, ds(j, 1)], ALU.is_equal, ALU.mult)
                nc.vector.tensor_scalar(p_one[0:B, s, :], iota[0:B, 0:128], pair_lo[0:B, ds(j, 1)], None,
                                        ALU.is_equal).then_inc(pairs_made, 1)

            def pair_turn(i):
                for s in range(PR):
                    if not isinstance(i, int):
                        dve.wait_ge(pairs_used, i * PR + (s + 1 - PR))
                    pair_column(i * PR + s, s)

            turns_of(dve, 0, PAIRS // PR, pair_turn)
            for j in range(PAIRS // PR * PR, PAIRS):
                dve.wait_ge(pairs_used, j + 1 - PR)
                pair_column(j, j % PR)
            dve.wait_ge(pairs_used, PAIRS)
            step.mark(nc.vector.tensor_copy(s_tok[:, :], bank[0][:, 0:SLOTS]))
            step(nc.vector.tensor_copy(s_tmp[:, 0, :], bank[0][:, SLOTS:2 * SLOTS]))
            step(nc.vector.tensor_scalar(s_tmp[:, 1, :], s_tmp[:, 0, :], 0.0, None, ALU.is_equal))
            step(nc.vector.tensor_tensor(s_tmp[:, 1, :], s_tmp[:, 1, :], slot_id[:, :], ALU.mult))
            step(nc.vector.scalar_tensor_tensor(s_row[:, :], s_tmp[:, 0, :], -1.0, s_tmp[:, 1, :], ALU.add, ALU.add))
            nc.vector.memset(marker[:, :], 0.0).then_inc(slots_ready, 1)
            dve.wait_ge(ld_moe, 32 * NE)
            dve.wait_ge(ld_b2, 16)

            def expert_weights(off):
                nc.vector.tensor_copy(w1c[:, :, :].rearrange("p k n -> p (k n)"), slab[:, ds(off, 1024)]).then_inc(w_copied, 1)

            def add_output_bias(turn, k, off):
                dve.wait_ge(y_mm, turn * RING + (k + 1))
                if k >= 2:
                    dve.wait_ge(y_put[k - 2], turn * 16 + 16)
                else:
                    await_ge(dve, y_put[k + RING - 2], turn * 16)
                nc.vector.tensor_tensor(yv[:, k % 2, :], bank[4 + k % 2][:, 0:C],
                                        b2b[:, :, :].rearrange("p e c -> p (e c)")[:, ds(off, C)], ALU.add).then_inc(y_out, 1)

            def bias_offsets(start, n):
                return nc.values_load_multi_w_load_instructions(
                    ex_b2[0:1, ds(start, n)], engines=[DVE_], min_val=0, max_val=(NE - 1) * C,
                    skip_runtime_bounds_check_because="the router clamps it")[1]

            def expert_turn(i):
                _, woff = nc.values_load_multi_w_load_instructions(
                    ex_w[0:1, ds(i * RING, RING)], engines=[DVE_], min_val=0, max_val=(NE - 1) * 2048,
                    skip_runtime_bounds_check_because="the router clamps it")
                first = isinstance(i, int)
                boff = [None, None, *bias_offsets(0, RING - 2)] if first else bias_offsets(i * RING - 2, RING)
                for k in range(RING):
                    await_ge(dve, h_mm, i * RING + k)
                    expert_weights(woff[k])
                    dve.wait_ge(x_mm, i * RING + (k + 1))
                    nc.vector.tensor_copy(tT[:, k % 2, :, :].rearrange("p k n -> p (k n)"), bank[k % 2][:, 0:C]).then_inc(x_out, 1)
                    if k >= 2:
                        add_output_bias(i, k - 2, boff[k])
                    elif not first:
                        add_output_bias(i - 1, k - 2 + RING, boff[k])

            turns_of(dve, 0, SLOTS // RING, expert_turn)
            boff = bias_offsets(SLOTS - 2, 2)
            for k in range(2):
                add_output_bias(SLOTS // RING - 1, RING - 2 + k, boff[k])
            first_marks = {}

            def first_experts(tiles):
                dve.wait_ge(y_ld[tiles[0] // GT], 32)
                for t in tiles:
                    dve.wait_ge(tokens_again, t + 1)
                    step.mark(nc.vector.scalar_tensor_tensor(zb[0:B, t, :], yb[0:B, 0, t, :], pair_w[0:B, 0, t:t + 1], zb[0:B, t, :],
                                                             ALU.mult, ALU.add))
                    first_marks[t] = step.done

            def with_experts(t):
                step.wait_for(first_marks[t])
                step.mark(nc.vector.scalar_tensor_tensor(zb[0:B, t, :], yb[0:B, 1, t, :], pair_w[0:B, 1, t:t + 1], zb[0:B, t, :],
                                                         ALU.mult, ALU.add))

            for q in range(turns + 2):
                if q < turns:
                    first_experts(range(q * GT, (q + 1) * GT))
                    variances(range(q * GT, (q + 1) * GT), with_experts, fin_var, lambda t: zb[0:B, t, :])
                if 1 <= q <= turns:
                    dve.wait_ge(fin_root, q)
                    norm_scale(range((q - 1) * GT, q * GT), fin_scale)
                for t in range((q - 2) * GT, (q - 1) * GT) if q >= 2 else ():
                    dve.wait_ge(fin_aff, t + 1)
                    dve.wait_ge(beta_added, t + 1)
                    nc.vector.tensor_tensor(ub[0:B, t, :], ub[0:B, t, :], X[0:B, t, :], ALU.add).then_inc(fin_out, 1)

        def bucket_row(pe, rounds, P, H):
            pe.wait_ge(rank_rows, 2 * rounds)
            for j in range(-(-H // 128)):
                n = min(P, H - j * 128)
                ins = nc.tensor.matmul(bank[6][0:1, 128 * (j + 1):128 * (j + 1) + n], bucket[0:P, j:j + 1], ident[0:P, 0:n], start=True, stop=True)
            ins.then_inc(rank_sums, 1)

        def rank_products(pe, rounds, P, nb):
            pe.wait_ge(rank_rows, 2 * rounds - 1)
            mine = small[0:P, 1, 0:nb]
            nc.tensor.matmul(bank[6][0:P, 0:nb], tri[0:P, 0:P], mine, start=True, stop=True)
            nc.tensor.matmul(bank[6][0:P, 32:32 + nb], ones[0:P, 0:P], mine, start=True, stop=True).then_inc(rank_sums, 1)

        def clear_banks(which, cols):
            for b in which:
                for c in range(0, cols, 256):
                    n = min(256, cols - c)
                    ins = nc.tensor.matmul(bank[b][:, c:c + n], zeros[:, 0:128], zeros[:, 0:n], start=True, stop=True)
            return ins

        def sort_product(pe, n, s, H):
            pe.wait_ge(loads_made, n)
            nc.tensor.matmul(bank[0][:, 0:2 * H], s_one[:, s, :], s_load[:, s, 0:2 * H], start=False, stop=True,
                             skip_group_check=True).then_inc(hots_used, 1)

        def attention_fold_pe(pe):
            accumulate_keys(pe, NT - 1)
            pe.wait_ge(kv_sums, 1)
            for j in range(KC):
                ins = nc.tensor.matmul(bank[1][:, j * 128:(j + 1) * 128], kvsum[:, j, :], ident[:, :], start=True, stop=True)
            ins.then_inc(kv_sums_row, 1)
            pe.wait_ge(kvT_ready, 1)
            for j in range(KC):
                ins = nc.tensor.matmul(bank[4][:, j * C:(j + 1) * C], kvT[:, j, :], mw1[:, j, :], start=True, stop=True)
            ins.then_inc(kvw1_mm, 1)
            pe.wait_ge(kvw1_out, 1)
            for m in range(KC):
                for j in range(KC):
                    nc.tensor.matmul(bank[0][:, m * C:(m + 1) * C], wqT[:, j, m * 128:(m + 1) * 128], kvw1[:, j, :],
                                     start=(j == 0), stop=(j == KC - 1))
            for m in range(KC):
                for j in range(KC):
                    ins = nc.tensor.matmul(bank[1][:, 256 + m:257 + m], kvw1[:, j, m * 128:(m + 1) * 128], bcol[:, 64 + j:65 + j],
                                           start=(j == 0), stop=(j == KC - 1))
            ins.then_inc(weff_mm, 1)
            pe.wait_ge(weff_out, 1)

        def accumulate_keys(pe, tile):
            pe.wait_ge(kv_norm, tile + 1)
            for j in range(KC):
                kj, vj = (kvn[0:B, s, 4 * j:4 * j + 4, :].rearrange("p h d -> p (h d)") for s in range(2))
                for a, side, lo_, n in ((vj, kj, j * 128, 128), (vj, ones[0:B, 0:1], 256 + j, 1), (kj, ones[0:B, 0:1], 260 + j, 1)):
                    ins = nc.tensor.matmul(bank[6][:, lo_:lo_ + n], a, side, start=False, stop=True, skip_group_check=True)
            ins.then_inc(kv_used, 1)

        @block.tensor
        def _(pe):
            pe.wait_ge(consts, 1)
            clear_banks((0,), 2 * HMAX).then_inc(hots_used, SR)
            nc.tensor.matmul(bank[7][0:1, 1:2], zeros[:, 0:1], zeros[:, 0:1], start=True, stop=True).then_inc(chunk_done, RING)
            rank_products(pe, 1, 128, NT)
            bucket_row(pe, 1, 128, H_OF[0])
            T = T_OF[0]
            with pe.Fori(0, T // SR) as i:
                for s in range(SR):
                    sort_product(pe, i * SR + s + 1, s, H_OF[0])
            for j in range(T // SR * SR, T):
                sort_product(pe, j + 1, j % SR, H_OF[0])
            nc.tensor.matmul(bank[7][0:1, 0:1], zeros[:, 0:1], zeros[:, 0:1], start=True, stop=True).then_inc(sorted_, 1)
            pe.wait_ge(xn_ready, 1)
            for t in range(NT):
                if t >= 2:
                    pe.wait_ge(xn_t_out, t - 1)
                for k in range(KC):
                    ins = nc.tensor.transpose(bank[4 + t % 2][:, k * B:(k + 1) * B], xn[0:B, t, k * 128:(k + 1) * 128],
                                              ident[0:B, 0:B])
                ins.then_inc(xn_t, 1)
            rank_products(pe, 2, 128, NT)
            pe.wait_ge(ld_w, 16 * W_LOADS)
            pe.wait_ge(xn_t_out, NT)
            for t in range(NT):
                if t >= 2:
                    pe.wait_ge(tab_out, t - 1)
                for k in range(KC):
                    ins = nc.tensor.matmul(bank[2 + t % 2][0:B, 0:C], xnT[:, k, t * B:(t + 1) * B], wgnn[:, k, :],
                                           start=(k == 0), stop=(k == KC - 1))
                ins.then_inc(tab_mm, 1)
                if t == 3 * NT // 4:
                    bucket_row(pe, 2, 128, H_OF[1])
            pe.wait_ge(ld_b, 16 * B_LOADS)
            pe.wait_ge(wcen_ready, 1)
            for j in range(KC):
                for k in range(KC):
                    nc.tensor.transpose(bank[5][:, j * C + k * 128:j * C + (k + 1) * 128], weff[:, k, j * 128:(j + 1) * 128],
                                        ident[:, :])
            nc.tensor.transpose(bank[4][:, 0:70], brow[0:70, :], ident[0:70, 0:70]).then_inc(setup_t, 1)
            rank_products(pe, 3, 128, NT)
            bucket_row(pe, 3, 128, H_OF[2])
            pe.wait_ge(group_ready, 1)
            clear_banks((0,), 2 * HMAX)
            pe.wait_ge(hots_made, T_OF[0])
            pe.wait_ge(setup_t_out, 1)
            pe.wait_ge(routed, 1)
            clear_banks((6,), 262)
            for g, turns, turn0, nsort, mix, tiles, tile0 in SEGS:
                c0 = CHUNK0[g] + RING * turn0
                if g == 1 and turn0 == 0:
                    pe.wait_ge(group_ready, g + 1)
                    clear_banks((0,), 2 * HMAX)
                if mix == 2 and tile0 == 0:
                    attention_fold_pe(pe)
                col0 = AT[g + 1] + nsort * turn0 if nsort else 0
                split = shares(nsort, RING)

                def turn(i):
                    m = 0
                    for k in range(RING):
                        pe.wait_ge(hot_ready, i * RING + (c0 + k + 1))
                        pe.wait_ge(gathered[k], i * 16 + (c0 // RING + 1) * 16)
                        if k % 2 == 0:
                            pe.wait_ge(chunk_added, i * RING + (c0 + k + 2))
                        nc.tensor.matmul(bank[CHUNK_BANKS[k // 2]][:, k % 2 * C:(k % 2 + 1) * C], hot[:, k, :], rows[:, k, :],
                                         start=True, stop=True).then_inc(chunk_done, 1)
                        for _ in range(split[k]):
                            if m >= LAG or turn0:
                                sort_product(pe, i * nsort + (col0 + m - LAG + 1), (m - LAG) % SR, H_OF[g + 1])
                            m += 1
                        for name, tile in attention_steps(tiles, k, i, tile0):
                            if mix == 1 and name == "project":
                                await_ge(pe, kv_sb, tile)
                                pe.wait_ge(xst_ready, tile + 1)
                                for kc in range(KC):
                                    wkv = wcen[:, kc, :].rearrange("p (h c) -> p h c", h=HEADS)[:, :, HD:3 * HD]
                                    ins = nc.tensor.matmul(bank[4][0:B, :], xst[:, kc, :],
                                                           wkv, start=(kc == 0), stop=(kc == KC - 1))
                                ins.then_inc(kv_mm, 1)
                            if mix == 1 and name == "sums":
                                accumulate_keys(pe, tile)
                            if mix == 2 and name == "hidden":
                                await_ge(pe, mh_out, tile)
                                for m2 in range(KC):
                                    for kc in range(KC):
                                        ins = nc.tensor.matmul(bank[4][:, m2 * B:(m2 + 1) * B], weff[:, kc, m2 * 128:(m2 + 1) * 128],
                                                               xnT[:, kc, ds(tile * B, B)], start=(kc == 0), stop=(kc == KC - 1))
                                ins.then_inc(mh_mm, 1)
                            if mix == 2 and name == "second":
                                pe.wait_ge(mh_out, tile + 1)
                                await_ge(pe, my_out, tile)
                                for kc in range(KC):
                                    ins = nc.tensor.matmul(bank[0][0:B, 0:C], mhT[:, kc, :], mw2[:, kc, :],
                                                           start=(kc == 0), stop=(kc == KC - 1))
                                ins.then_inc(my_mm, 1)
                if turns == 1:
                    turn(0)
                else:
                    with pe.Fori(0, turns) as i:
                        turn(i)
                if nsort and turn0 + turns == SORT_TURNS[g]:
                    for m in range(LAG):
                        sort_product(pe, AT[g + 1] + T_OF[g + 1] - LAG + m + 1, (m - LAG) % SR, H_OF[g + 1])
                    nc.tensor.matmul(bank[1][0:1, 0:1], zeros[:, 0:1], zeros[:, 0:1], start=True, stop=True).then_inc(sorted_, 1)
            def mid_transpose(t):
                pe.wait_ge(mid_norm, t + 1)
                if t >= 4:
                    pe.wait_ge(mt_out, t - 3)
                for k in range(KC):
                    ins = nc.tensor.transpose(bank[t % 4][:, k * B:(k + 1) * B], acc[0:B, t, k * 128:(k + 1) * 128], ident[0:B, 0:B])
                ins.then_inc(mt_mm, 1)

            def logits(t):
                q = t // GT
                pe.wait_ge(mt_out, t + 1)
                if t % GT == 0 and q >= 2:
                    pe.wait_ge(mg_out, q - 1)
                for k in range(KC):
                    ins = nc.tensor.matmul(bank[6 + q % 2][0:B, t % GT * NE:(t % GT + 1) * NE], rows[:, t % RING, k * B:(k + 1) * B],
                                           gate[:, k, :], start=(k == 0), stop=(k == KC - 1))
                if t % GT == GT - 1:
                    ins.then_inc(mg_mm, 1)

            for t in range(NT + 2):
                if t < NT:
                    mid_transpose(t)
                if t >= 2:
                    logits(t - 2)
            pe.wait_ge(mg_out, NT // GT)
            rank_products(pe, 4, B, NE)
            bucket_row(pe, 4, B, SLOTS)

            def pair_product(n, s, first=False):
                pe.wait_ge(pair_loads, n)
                nc.tensor.matmul(bank[0][:, 0:2 * SLOTS], p_one[0:B, s, :], p_load[0:B, s, :], start=first, stop=True,
                                 skip_group_check=True).then_inc(pairs_used, 1)

            pair_product(1, 0, True)
            for s in range(1, PR):
                pair_product(s + 1, s)
            with pe.Fori(1, PAIRS // PR) as i:
                for s in range(PR):
                    pair_product(i * PR + (s + 1), s)
            for j in range(PAIRS // PR * PR, PAIRS):
                pair_product(j + 1, j % PR)
            pe.wait_ge(slots_ready, 1)

            def tokens_transposed(i, k):
                pe.wait_ge(tok_got[k], i * 16 + 16)
                await_ge(pe, x_out, i * RING + max(k - 1, 0))
                for c in range(KC):
                    ins = nc.tensor.transpose(bank[k % 2][:, c * 128:(c + 1) * 128], rows[:, k, c * 128:(c + 1) * 128], ident[:, :])
                ins.then_inc(x_mm, 1)

            def second_product(turn, k, off):
                pe.wait_ge(h_out, turn * RING + (k + 1))
                if not (isinstance(turn, int) and turn == 0 and k < 2):
                    pe.wait_ge(y_out, turn * RING + (k - 1))
                for m in range(KF):
                    ins = nc.tensor.matmul(bank[4 + k % 2][:, 0:C], hT[:, k % 2, m, :], slab[:, ds(off + (1024 + m * C), C)],
                                           start=(m == 0), stop=(m == KF - 1))
                ins.then_inc(y_mm, 1)

            def weight_offsets(start, n):
                return nc.values_load_multi_w_load_instructions(
                    ex_w[0:1, ds(start, n)], engines=[PE_], min_val=0, max_val=(NE - 1) * 2048,
                    skip_runtime_bounds_check_because="the router clamps it")[1]

            def expert_turn(i, last):
                first = isinstance(i, int) and i == 0
                woff = [None, *weight_offsets(0, RING - 1)] if first else weight_offsets(i * RING - 1, RING)
                for k in range(RING):
                    pe.wait_ge(w_copied, i * RING + (k + 1))
                    pe.wait_ge(x_out, i * RING + (k + 1))
                    for m in range(KF):
                        for c in range(KC):
                            ins = nc.tensor.matmul(bank[2 + k % 2][:, m * 128:(m + 1) * 128], w1c[:, c, m * 128:(m + 1) * 128],
                                                   tT[:, k % 2, c, :], start=(c == 0), stop=(c == KC - 1))
                    ins.then_inc(h_mm, 1)
                    if k + 1 < RING:
                        tokens_transposed(i, k + 1)
                    elif not last:
                        tokens_transposed(i + 1, 0)
                    if k:
                        second_product(i, k - 1, woff[k])
                    elif not first:
                        second_product(i - 1, RING - 1, woff[k])

            tokens_transposed(0, 0)
            turns_of(pe, 0, SLOTS // RING, lambda i: expert_turn(i, False), lambda i: expert_turn(i, True))
            second_product(SLOTS // RING - 1, RING - 1, weight_offsets(SLOTS - 1, 1)[0])


_INS = ["x", "src", "dst", "edge_weight", "L0_gnn_weight_mat", "L0_gnn_bias_vec", "L0_mix_w_qkv", "L0_mix_b_qkv",
        "L0_mix_kln_g", "L0_mix_kln_b", "L0_mix_vln_g", "L0_mix_vln_b", "L0_mix_w1", "L0_mix_b1", "L0_mix_w2",
        "L0_mix_b2", "L0_ffn_gate_w", "L0_ffn_gate_b", "L0_ffn_w1", "L0_ffn_b1", "L0_ffn_w2", "L0_ffn_b2",
        "L0_ffn_gamma", "L0_ffn_beta"]


def kernel(**inputs):
    import numpy as np
    import concourse.bacc as bacc
    from concourse import mybir
    from concourse.bass_utils import run_bass_kernel_spmd

    nc = bacc.Bacc("TRN2", target_bir_lowering=False, num_devices=1)
    arrays, args = {}, []
    for name in _INS:
        a = np.ascontiguousarray(inputs[name])
        arrays[f"in_{name}"] = a
        args.append(nc.dram_tensor(f"in_{name}", a.shape, mybir.dt.from_np(a.dtype), kind="ExternalInput").ap())
    out = nc.dram_tensor("out", arrays["in_x"].shape, mybir.dt.float32, kind="ExternalOutput").ap()
    graph_transformer_layer(nc, *args, out)
    r = run_bass_kernel_spmd(nc, [arrays], core_ids=[0])
    return r.results[0]["out"]
```
